# Optimizing a Trainium2 kernel written in Bass

```python
import numpy as np
import jax
import jax.numpy as jnp

def _softmax(x, axis=-1):
    return jax.nn.softmax(x, axis=axis)

def _gelu(x):
    return jax.nn.gelu(x, approximate=True)

def _silu(x):
    return jax.nn.silu(x)

def _sigmoid(x):
    return jax.nn.sigmoid(x)

def _layernorm(x, axis=-1, eps=1e-05):
    m = jnp.mean(x, axis=axis, keepdims=True)
    v = jnp.var(x, axis=axis, keepdims=True)
    return (x - m) / jnp.sqrt(v + eps)

def _scatter_add(tgt, idx, src, axis=0):
    return tgt.at[idx].add(src)

def _segment_sum(src, seg, n):
    return jax.ops.segment_sum(src, seg, n)
kernel_name = 'mk_flamingo_gated_d4_seqx_r8_dea2da'

def setup_inputs(seed: int=0):
    np.random.seed(seed)
    _w = jnp.asarray

    def _rec_inputs():
        import jax
        import jax.numpy as jnp
        _rk = jax.random.key(seed)
        x = -0.0002928 + 1 * jax.random.normal(jax.random.fold_in(_rk, 1), (4, 512, 128), jnp.float32)
        _lenS = 512 - jax.random.randint(jax.random.fold_in(_rk, 7), (4,), 0, max(1, 512 // 4) + 1, jnp.int32)
        _lenS2 = 32 - jax.random.randint(jax.random.fold_in(_rk, 8), (4,), 0, max(1, 32 // 4) + 1, jnp.int32)
        _ctx_512P = jax.random.normal(jax.random.fold_in(_rk, 11), (4, 16, 64), jnp.float32)
        _ctx_512c = jax.random.dirichlet(jax.random.fold_in(_rk, 511), 0.3 * jnp.ones((16,), jnp.float32), (4, 32))
        _ctx_512t = jnp.einsum('bsk,bkd->bsd', _ctx_512c, _ctx_512P)
        _ctx_512t = _ctx_512t * jax.lax.rsqrt(jnp.mean(jnp.square(_ctx_512t)) + 1e-12) * 0.953939
        ctx_512 = 0.00222621 + 0.99962 * (_ctx_512t + 0.3 * jax.random.normal(jax.random.fold_in(_rk, 611), (4, 32, 64), jnp.float32))
        _g = jax.random.normal(jax.random.fold_in(_rk, 9001), (2, 4), jnp.float32)
        _g = jnp.sign(_g) * jnp.maximum(jnp.abs(_g), 1.0) + (_g == 0) * 1.0
        g_xattn = _g[0]
        g_ffn = _g[1]
        return (x, ctx_512, g_xattn, g_ffn)
    x, ctx_512, g_xattn, g_ffn = _rec_inputs()

    def _L0_xattn_setup():
        import jax, jax.numpy as jnp
        import numpy as np
        H, D, C1, C2, S, M, B, W = (16, 32, 128, 64, 256, 64, 2, 4)

        def _ln(x, g, b):
            m = jnp.mean(x, -1, keepdims=True)
            v = jnp.var(x, -1, keepdims=True)
            return (x - m) * jax.lax.rsqrt(v + 1e-05) * g + b

        def _mha(x, y, wq, wk, wv, li1_w, li1_b, lnx_g, lnx_b, lny_g, lny_b, ln3_g, ln3_b, li2_w, li2_b, li3_w, li3_b, causal):
            xn = _ln(x, lnx_g, lnx_b)
            yn = _ln(y, lny_g, lny_b)
            q = jnp.einsum('bsc,hcd->bhsd', xn, wq)
            k = jnp.einsum('btc,hcd->bhtd', yn, wk)
            v = jnp.einsum('btc,hcd->bhtd', yn, wv)
            a = jax.nn.softmax(jnp.einsum('bhsd,bhtd->bhst', q, k) * D ** (-0.5), axis=-1)
            if causal:
                s, t = (a.shape[-2], a.shape[-1])
                mask = (jnp.arange(t)[None, :] > jnp.arange(s)[:, None]).astype(a.dtype)
                a = a * mask
            o = jnp.einsum('bhst,bhtd->bhsd', a, v)
            o = o.transpose(0, 2, 1, 3).reshape(x.shape[0], x.shape[1], H * D)
            x_out = x + o @ li1_w + li1_b
            h = jax.nn.gelu(_ln(x_out, ln3_g, ln3_b) @ li2_w + li2_b, approximate=False)
            return x_out + h @ li3_w + li3_b
        key = jax.random.key(seed)
        ks = iter(jax.random.split(key, 64))

        def w(shape, scale=0.02):
            return jax.random.normal(next(ks), shape, jnp.float32) * scale
        inp = {'xx': jax.random.normal(next(ks), (B, S, C1), jnp.float32), 'ee': jax.random.normal(next(ks), (B, M, C2), jnp.float32), 'ln1_g': jnp.ones(C1, jnp.float32), 'ln1_b': jnp.zeros(C1, jnp.float32), 'ln2_g': jnp.ones(C1, jnp.float32), 'ln2_b': jnp.zeros(C1, jnp.float32)}
        for pfx, cy in (('a1', C1), ('a2', C2)):
            inp[pfx + '_wq'] = w((H, C1, D))
            inp[pfx + '_wk'] = w((H, cy, D))
            inp[pfx + '_wv'] = w((H, cy, D))
            inp[pfx + '_li1_w'] = w((H * D, C1))
            inp[pfx + '_li1_b'] = jnp.zeros(C1, jnp.float32)
            inp[pfx + '_lnx_g'] = jnp.ones(C1, jnp.float32)
            inp[pfx + '_lnx_b'] = jnp.zeros(C1, jnp.float32)
            inp[pfx + '_lny_g'] = jnp.ones(cy, jnp.float32)
            inp[pfx + '_lny_b'] = jnp.zeros(cy, jnp.float32)
            inp[pfx + '_ln3_g'] = jnp.ones(C1, jnp.float32)
            inp[pfx + '_ln3_b'] = jnp.zeros(C1, jnp.float32)
            inp[pfx + '_li2_w'] = w((C1, C1 * W))
            inp[pfx + '_li2_b'] = jnp.zeros(C1 * W, jnp.float32)
            inp[pfx + '_li3_w'] = w((C1 * W, C1))
            inp[pfx + '_li3_b'] = jnp.zeros(C1, jnp.float32)
        inp['training'] = 0
        return inp
    _L0_xattn_all = _L0_xattn_setup()
    _L0_xattn_in = {k: v for k, v in _L0_xattn_all.items() if k in ('ln1_g', 'ln1_b', 'ln2_g', 'ln2_b', 'a1_wq', 'a1_wk', 'a1_wv', 'a1_li1_w', 'a1_li1_b', 'a1_lnx_g', 'a1_lnx_b', 'a1_lny_g', 'a1_lny_b', 'a1_ln3_g', 'a1_ln3_b', 'a1_li2_w', 'a1_li2_b', 'a1_li3_w', 'a1_li3_b', 'a2_wq', 'a2_wk', 'a2_wv', 'a2_li1_w', 'a2_li1_b', 'a2_lnx_g', 'a2_lnx_b', 'a2_lny_g', 'a2_lny_b', 'a2_ln3_g', 'a2_ln3_b', 'a2_li2_w', 'a2_li2_b', 'a2_li3_w', 'a2_li3_b')}
    del _L0_xattn_all

    def _L0_ffn_setup():
        import jax, jax.numpy as jnp
        import numpy as np
        B, S, D_MODEL, D_HIDDEN = (4, 256, 128, 512)

        def act_quant(x):
            scale = 127.0 / jnp.clip(jnp.max(jnp.abs(x), axis=-1, keepdims=True), 1e-05)
            return jnp.clip(jnp.round(x * scale), -128, 127) / scale

        def weight_quant(w):
            scale = 1.0 / jnp.clip(jnp.mean(jnp.abs(w)), 1e-05)
            return jnp.clip(jnp.round(w * scale), -1, 1) / scale

        def bit_linear(x, w):
            xq = x + jax.lax.stop_gradient(act_quant(x) - x)
            wq = w + jax.lax.stop_gradient(weight_quant(w) - w)
            return jnp.einsum('bsd,hd->bsh', xq, wq)

        def depthwise_conv1d(x_bcl, w, b):
            y = jax.lax.conv_general_dilated(x_bcl, w, window_strides=(1,), padding=[(1, 1)], dimension_numbers=('NCH', 'OIH', 'NCH'), feature_group_count=x_bcl.shape[1])
            return y + b[None, :, None]
        key = jax.random.key(seed)
        ks = jax.random.split(key, 5)
        lim1 = 1.0 / np.sqrt(D_MODEL)
        lim2 = 1.0 / np.sqrt(D_HIDDEN)
        limc = 1.0 / np.sqrt(3.0)
        return {'x': jax.random.normal(ks[0], (B, S, D_MODEL), dtype=jnp.float32), 'w1': jax.random.uniform(ks[1], (D_HIDDEN, D_MODEL), jnp.float32, -lim1, lim1), 'conv_w': jax.random.uniform(ks[2], (D_HIDDEN, 1, 3), jnp.float32, -limc, limc), 'conv_b': jax.random.uniform(ks[3], (D_HIDDEN,), jnp.float32, -limc, limc), 'w2': jax.random.uniform(ks[4], (D_MODEL, D_HIDDEN), jnp.float32, -lim2, lim2)}
    _L0_ffn_all = _L0_ffn_setup()
    _L0_ffn_in = {k: v for k, v in _L0_ffn_all.items() if k in ('w1', 'conv_w', 'conv_b', 'w2')}
    del _L0_ffn_all

    def _L1_xattn_setup():
        import jax, jax.numpy as jnp
        import numpy as np
        DIM = 128
        LATENT_DIM = 64
        NUM_HEADS = 16
        HEAD_DIM = DIM // NUM_HEADS
        SCALE = HEAD_DIM ** (-0.5)
        key = jax.random.key(seed)
        k1, k2, k3, k4, k5 = jax.random.split(key, 5)
        B, xN, zN = (2, 256, 256)
        x = jax.random.normal(k1, (B, xN, DIM), dtype=jnp.float32)
        z = jax.random.normal(k2, (B, zN, LATENT_DIM), dtype=jnp.float32)
        Wq = jax.random.normal(k3, (DIM, DIM), dtype=jnp.float32) * DIM ** (-0.5)
        Wkv = jax.random.normal(k4, (2 * DIM, LATENT_DIM), dtype=jnp.float32) * LATENT_DIM ** (-0.5)
        Wo = jax.random.normal(k5, (DIM, DIM), dtype=jnp.float32) * DIM ** (-0.5)
        return {'x': x, 'z': z, 'Wq': Wq, 'Wkv': Wkv, 'Wo': Wo}
    _L1_xattn_all = _L1_xattn_setup()
    _L1_xattn_in = {k: v for k, v in _L1_xattn_all.items() if k in ('Wq', 'Wkv', 'Wo')}
    del _L1_xattn_all

    def _L1_ffn_setup():
        import jax, jax.numpy as jnp
        import numpy as np
        TOP_K = 2
        key = jax.random.key(seed)
        ks = jax.random.split(key, 5)
        B, T, D, F, E = (4, 256, 128, 512, 8)
        s = 0.02
        return {'x': jax.random.normal(ks[0], (B, T, D), jnp.float32), 'gate_w': jax.random.normal(ks[1], (D, E), jnp.float32) * s, 'w1': jax.random.normal(ks[2], (E, D, F), jnp.float32) * s, 'w3': jax.random.normal(ks[3], (E, D, F), jnp.float32) * s, 'w2': jax.random.normal(ks[4], (E, F, D), jnp.float32) * s}
    _L1_ffn_all = _L1_ffn_setup()
    _L1_ffn_in = {k: v for k, v in _L1_ffn_all.items() if k in ('gate_w', 'w1', 'w3', 'w2')}
    del _L1_ffn_all

    def _L2_xattn_setup():
        import jax, jax.numpy as jnp
        import numpy as np
        NUM_HEADS = 16
        HEAD_DIM = 64
        Q_DIM = 128
        KV_DIM = 64
        INNER = NUM_HEADS * HEAD_DIM
        key = jax.random.key(seed)
        ks = jax.random.split(key, 7)
        B, N, M = (32, 128, 256)
        q = jax.random.normal(ks[0], (B, N, Q_DIM), dtype=jnp.float32)
        kv = jax.random.normal(ks[1], (B, M, KV_DIM), dtype=jnp.float32)
        Wq = jax.random.normal(ks[2], (Q_DIM, INNER), dtype=jnp.float32) / np.sqrt(Q_DIM)
        Wk = jax.random.normal(ks[3], (KV_DIM, INNER), dtype=jnp.float32) / np.sqrt(KV_DIM)
        Wv = jax.random.normal(ks[4], (KV_DIM, INNER), dtype=jnp.float32) / np.sqrt(KV_DIM)
        Wo = jax.random.normal(ks[5], (INNER, Q_DIM), dtype=jnp.float32) / np.sqrt(INNER)
        bo = jax.random.normal(ks[6], (Q_DIM,), dtype=jnp.float32) * 0.01
        return {'q': q, 'kv': kv, 'Wq': Wq, 'Wk': Wk, 'Wv': Wv, 'Wo': Wo, 'bo': bo}
    _L2_xattn_all = _L2_xattn_setup()
    _L2_xattn_in = {k: v for k, v in _L2_xattn_all.items() if k in ('Wq', 'Wk', 'Wv', 'Wo', 'bo')}
    del _L2_xattn_all

    def _L2_ffn_setup():
        import jax, jax.numpy as jnp
        import numpy as np
        DIM = 128

        def _reference_tuple_inner(x, W_r, W_k, W_v, mu_r, mu_k):
            B, T, C = x.shape
            x_prev = jnp.concatenate([jnp.zeros((B, 1, C), x.dtype), x[:, :-1, :]], axis=1)
            xr = mu_r * x + (1.0 - mu_r) * x_prev
            xk = mu_k * x + (1.0 - mu_k) * x_prev
            r = jax.nn.sigmoid(jnp.einsum('btc,dc->btd', xr, W_r))
            k = jnp.einsum('btc,dc->btd', xk, W_k)
            k_act = jnp.square(jax.nn.relu(k))
            out = r * jnp.einsum('btc,dc->btd', k_act, W_v)
            new_state = x[:, -1, :]
            return (out, new_state)
        key = jax.random.key(seed)
        ks = jax.random.split(key, 6)
        B, T, C = (8, 256, DIM)
        x = jax.random.normal(ks[0], (B, T, C), dtype=jnp.float32)
        s = 1.0 / np.sqrt(C)
        W_r = jax.random.uniform(ks[1], (C, C), jnp.float32, -s, s)
        W_k = jax.random.uniform(ks[2], (C, C), jnp.float32, -s, s)
        W_v = jax.random.uniform(ks[3], (C, C), jnp.float32, -s, s)
        mu_r = jax.random.uniform(ks[4], (C,), jnp.float32)
        mu_k = jax.random.uniform(ks[5], (C,), jnp.float32)
        return {'x': x, 'W_r': W_r, 'W_k': W_k, 'W_v': W_v, 'mu_r': mu_r, 'mu_k': mu_k}
    _L2_ffn_all = _L2_ffn_setup()
    _L2_ffn_in = {k: v for k, v in _L2_ffn_all.items() if k in ('W_r', 'W_k', 'W_v', 'mu_r', 'mu_k')}
    del _L2_ffn_all

    def _L3_xattn_setup():
        import jax, jax.numpy as jnp
        import numpy as np
        HEADS = 16
        D_MODEL = 128
        IMG_MODEL = 64
        D_K = D_MODEL // HEADS
        key = jax.random.key(seed)
        ks = jax.random.split(key, 12)
        B, LQ, LKV = (8, 256, 128)
        s_dm = 1.0 / np.sqrt(D_MODEL)
        s_im = 1.0 / np.sqrt(IMG_MODEL)
        return {'q': jax.random.normal(ks[0], (B, LQ, D_MODEL), jnp.float32), 'k': jax.random.normal(ks[1], (B, LKV, IMG_MODEL), jnp.float32), 'v': jax.random.normal(ks[2], (B, LKV, IMG_MODEL), jnp.float32), 'Wq': jax.random.normal(ks[3], (D_MODEL, D_MODEL), jnp.float32) * s_dm, 'bq': jnp.zeros((D_MODEL,), jnp.float32), 'Wk': jax.random.normal(ks[4], (IMG_MODEL, D_MODEL), jnp.float32) * s_im, 'bk': jnp.zeros((D_MODEL,), jnp.float32), 'Wv': jax.random.normal(ks[5], (IMG_MODEL, D_MODEL), jnp.float32) * s_im, 'bv': jnp.zeros((D_MODEL,), jnp.float32), 'Wo': jax.random.normal(ks[6], (D_MODEL, D_MODEL), jnp.float32) * s_dm, 'bo': jnp.zeros((D_MODEL,), jnp.float32)}
    _L3_xattn_all = _L3_xattn_setup()
    _L3_xattn_in = {k: v for k, v in _L3_xattn_all.items() if k in ('Wq', 'bq', 'Wk', 'bk', 'Wv', 'bv', 'Wo', 'bo')}
    del _L3_xattn_all

    def _L3_ffn_setup():
        import math
        import jax, jax.numpy as jnp
        import numpy as np
        H = 128
        F = 512
        E = 8
        TOP_K = 2
        CAP_FACTOR = 1.25
        MIN_CAP = 4
        SHARED_SCALE = 0.1

        def _top2_gating(logits, capacity):
            N, nE = logits.shape
            gates = jax.nn.softmax(logits, axis=-1)
            idx1 = jnp.argmax(gates, axis=-1)
            mask1 = jax.nn.one_hot(idx1, nE, dtype=gates.dtype)
            idx2 = jnp.argmax(gates * (1.0 - mask1), axis=-1)
            mask2 = jax.nn.one_hot(idx2, nE, dtype=gates.dtype)
            pos1 = jnp.cumsum(mask1, axis=0) - mask1
            mask1 = mask1 * (pos1 < capacity)
            pos2 = jnp.cumsum(mask2, axis=0) - mask2 + jnp.sum(mask1, axis=0, keepdims=True)
            mask2 = mask2 * (pos2 < capacity)
            g1 = jnp.sum(gates * mask1, axis=-1)
            g2 = jnp.sum(gates * mask2, axis=-1)
            denom = jnp.maximum(g1 + g2, jnp.finfo(gates.dtype).eps)
            g1, g2 = (g1 / denom, g2 / denom)
            loc1 = jnp.sum(pos1 * mask1, axis=-1).astype(jnp.int32)
            loc2 = jnp.sum(pos2 * mask2, axis=-1).astype(jnp.int32)
            oh1 = jax.nn.one_hot(loc1, capacity, dtype=gates.dtype)
            oh2 = jax.nn.one_hot(loc2, capacity, dtype=gates.dtype)
            combine = (g1[:, None] * mask1)[:, :, None] * oh1[:, None, :] + (g2[:, None] * mask2)[:, :, None] * oh2[:, None, :]
            dispatch = (combine > 0).astype(gates.dtype)
            return (combine, dispatch)
        key = jax.random.key(seed)
        ks = jax.random.split(key, 10)
        s_h = 1.0 / math.sqrt(H)
        s_f = 1.0 / math.sqrt(F)
        return {'hidden_states': jax.random.normal(ks[0], (2, 256, H), jnp.float32), 'router_w': jax.random.uniform(ks[1], (H, E), jnp.float32, -s_h, s_h), 'w1': jax.random.uniform(ks[2], (E, H, F), jnp.float32, -s_h, s_h), 'b1': jax.random.uniform(ks[3], (E, F), jnp.float32, -s_h, s_h), 'w2': jax.random.uniform(ks[4], (E, F, H), jnp.float32, -s_f, s_f), 'b2': jax.random.uniform(ks[5], (E, H), jnp.float32, -s_f, s_f), 'sw1': jax.random.uniform(ks[6], (H, F), jnp.float32, -s_h, s_h), 'sb1': jax.random.uniform(ks[7], (F,), jnp.float32, -s_h, s_h), 'sw2': jax.random.uniform(ks[8], (F, H), jnp.float32, -s_f, s_f), 'sb2': jax.random.uniform(ks[9], (H,), jnp.float32, -s_f, s_f)}
    _L3_ffn_all = _L3_ffn_setup()
    _L3_ffn_in = {k: v for k, v in _L3_ffn_all.items() if k in ('router_w', 'w1', 'b1', 'w2', 'b2', 'sw1', 'sb1', 'sw2', 'sb2')}
    del _L3_ffn_all
    return {'x': x, 'ctx_512': ctx_512, 'g_xattn': g_xattn, 'g_ffn': g_ffn, 'L0_xattn_ln1_g': _L0_xattn_in['ln1_g'], 'L0_xattn_ln1_b': _L0_xattn_in['ln1_b'], 'L0_xattn_ln2_g': _L0_xattn_in['ln2_g'], 'L0_xattn_ln2_b': _L0_xattn_in['ln2_b'], 'L0_xattn_a1_wq': _L0_xattn_in['a1_wq'], 'L0_xattn_a1_wk': _L0_xattn_in['a1_wk'], 'L0_xattn_a1_wv': _L0_xattn_in['a1_wv'], 'L0_xattn_a1_li1_w': _L0_xattn_in['a1_li1_w'], 'L0_xattn_a1_li1_b': _L0_xattn_in['a1_li1_b'], 'L0_xattn_a1_lnx_g': _L0_xattn_in['a1_lnx_g'], 'L0_xattn_a1_lnx_b': _L0_xattn_in['a1_lnx_b'], 'L0_xattn_a1_lny_g': _L0_xattn_in['a1_lny_g'], 'L0_xattn_a1_lny_b': _L0_xattn_in['a1_lny_b'], 'L0_xattn_a1_ln3_g': _L0_xattn_in['a1_ln3_g'], 'L0_xattn_a1_ln3_b': _L0_xattn_in['a1_ln3_b'], 'L0_xattn_a1_li2_w': _L0_xattn_in['a1_li2_w'], 'L0_xattn_a1_li2_b': _L0_xattn_in['a1_li2_b'], 'L0_xattn_a1_li3_w': _L0_xattn_in['a1_li3_w'], 'L0_xattn_a1_li3_b': _L0_xattn_in['a1_li3_b'], 'L0_xattn_a2_wq': _L0_xattn_in['a2_wq'], 'L0_xattn_a2_wk': _L0_xattn_in['a2_wk'], 'L0_xattn_a2_wv': _L0_xattn_in['a2_wv'], 'L0_xattn_a2_li1_w': _L0_xattn_in['a2_li1_w'], 'L0_xattn_a2_li1_b': _L0_xattn_in['a2_li1_b'], 'L0_xattn_a2_lnx_g': _L0_xattn_in['a2_lnx_g'], 'L0_xattn_a2_lnx_b': _L0_xattn_in['a2_lnx_b'], 'L0_xattn_a2_lny_g': _L0_xattn_in['a2_lny_g'], 'L0_xattn_a2_lny_b': _L0_xattn_in['a2_lny_b'], 'L0_xattn_a2_ln3_g': _L0_xattn_in['a2_ln3_g'], 'L0_xattn_a2_ln3_b': _L0_xattn_in['a2_ln3_b'], 'L0_xattn_a2_li2_w': _L0_xattn_in['a2_li2_w'], 'L0_xattn_a2_li2_b': _L0_xattn_in['a2_li2_b'], 'L0_xattn_a2_li3_w': _L0_xattn_in['a2_li3_w'], 'L0_xattn_a2_li3_b': _L0_xattn_in['a2_li3_b'], 'L0_ffn_w1': _L0_ffn_in['w1'], 'L0_ffn_conv_w': _L0_ffn_in['conv_w'], 'L0_ffn_conv_b': _L0_ffn_in['conv_b'], 'L0_ffn_w2': _L0_ffn_in['w2'], 'L1_xattn_Wq': _L1_xattn_in['Wq'], 'L1_xattn_Wkv': _L1_xattn_in['Wkv'], 'L1_xattn_Wo': _L1_xattn_in['Wo'], 'L1_ffn_gate_w': _L1_ffn_in['gate_w'], 'L1_ffn_w1': _L1_ffn_in['w1'], 'L1_ffn_w3': _L1_ffn_in['w3'], 'L1_ffn_w2': _L1_ffn_in['w2'], 'L2_xattn_Wq': _L2_xattn_in['Wq'], 'L2_xattn_Wk': _L2_xattn_in['Wk'], 'L2_xattn_Wv': _L2_xattn_in['Wv'], 'L2_xattn_Wo': _L2_xattn_in['Wo'], 'L2_xattn_bo': _L2_xattn_in['bo'], 'L2_ffn_W_r': _L2_ffn_in['W_r'], 'L2_ffn_W_k': _L2_ffn_in['W_k'], 'L2_ffn_W_v': _L2_ffn_in['W_v'], 'L2_ffn_mu_r': _L2_ffn_in['mu_r'], 'L2_ffn_mu_k': _L2_ffn_in['mu_k'], 'L3_xattn_Wq': _L3_xattn_in['Wq'], 'L3_xattn_bq': _L3_xattn_in['bq'], 'L3_xattn_Wk': _L3_xattn_in['Wk'], 'L3_xattn_bk': _L3_xattn_in['bk'], 'L3_xattn_Wv': _L3_xattn_in['Wv'], 'L3_xattn_bv': _L3_xattn_in['bv'], 'L3_xattn_Wo': _L3_xattn_in['Wo'], 'L3_xattn_bo': _L3_xattn_in['bo'], 'L3_ffn_router_w': _L3_ffn_in['router_w'], 'L3_ffn_w1': _L3_ffn_in['w1'], 'L3_ffn_b1': _L3_ffn_in['b1'], 'L3_ffn_w2': _L3_ffn_in['w2'], 'L3_ffn_b2': _L3_ffn_in['b2'], 'L3_ffn_sw1': _L3_ffn_in['sw1'], 'L3_ffn_sb1': _L3_ffn_in['sb1'], 'L3_ffn_sw2': _L3_ffn_in['sw2'], 'L3_ffn_sb2': _L3_ffn_in['sb2']}

def reference(x, ctx_512, g_xattn, g_ffn, L0_xattn_ln1_g, L0_xattn_ln1_b, L0_xattn_ln2_g, L0_xattn_ln2_b, L0_xattn_a1_wq, L0_xattn_a1_wk, L0_xattn_a1_wv, L0_xattn_a1_li1_w, L0_xattn_a1_li1_b, L0_xattn_a1_lnx_g, L0_xattn_a1_lnx_b, L0_xattn_a1_lny_g, L0_xattn_a1_lny_b, L0_xattn_a1_ln3_g, L0_xattn_a1_ln3_b, L0_xattn_a1_li2_w, L0_xattn_a1_li2_b, L0_xattn_a1_li3_w, L0_xattn_a1_li3_b, L0_xattn_a2_wq, L0_xattn_a2_wk, L0_xattn_a2_wv, L0_xattn_a2_li1_w, L0_xattn_a2_li1_b, L0_xattn_a2_lnx_g, L0_xattn_a2_lnx_b, L0_xattn_a2_lny_g, L0_xattn_a2_lny_b, L0_xattn_a2_ln3_g, L0_xattn_a2_ln3_b, L0_xattn_a2_li2_w, L0_xattn_a2_li2_b, L0_xattn_a2_li3_w, L0_xattn_a2_li3_b, L0_ffn_w1, L0_ffn_conv_w, L0_ffn_conv_b, L0_ffn_w2, L1_xattn_Wq, L1_xattn_Wkv, L1_xattn_Wo, L1_ffn_gate_w, L1_ffn_w1, L1_ffn_w3, L1_ffn_w2, L2_xattn_Wq, L2_xattn_Wk, L2_xattn_Wv, L2_xattn_Wo, L2_xattn_bo, L2_ffn_W_r, L2_ffn_W_k, L2_ffn_W_v, L2_ffn_mu_r, L2_ffn_mu_k, L3_xattn_Wq, L3_xattn_bq, L3_xattn_Wk, L3_xattn_bk, L3_xattn_Wv, L3_xattn_bv, L3_xattn_Wo, L3_xattn_bo, L3_ffn_router_w, L3_ffn_w1, L3_ffn_b1, L3_ffn_w2, L3_ffn_b2, L3_ffn_sw1, L3_ffn_sb1, L3_ffn_sw2, L3_ffn_sb2):
    import jax
    import jax.numpy as jnp

    def _L0_xattn_ref(xx, ee, ln1_g, ln1_b, ln2_g, ln2_b, a1_wq, a1_wk, a1_wv, a1_li1_w, a1_li1_b, a1_lnx_g, a1_lnx_b, a1_lny_g, a1_lny_b, a1_ln3_g, a1_ln3_b, a1_li2_w, a1_li2_b, a1_li3_w, a1_li3_b, a2_wq, a2_wk, a2_wv, a2_li1_w, a2_li1_b, a2_lnx_g, a2_lnx_b, a2_lny_g, a2_lny_b, a2_ln3_g, a2_ln3_b, a2_li2_w, a2_li2_b, a2_li3_w, a2_li3_b, training):
        import jax, jax.numpy as jnp
        import numpy as np
        H, D, C1, C2, S, M, B, W = (16, 32, 128, 64, 256, 64, 2, 4)

        def _ln(x, g, b):
            m = jnp.mean(x, -1, keepdims=True)
            v = jnp.var(x, -1, keepdims=True)
            return (x - m) * jax.lax.rsqrt(v + 1e-05) * g + b

        def _mha(x, y, wq, wk, wv, li1_w, li1_b, lnx_g, lnx_b, lny_g, lny_b, ln3_g, ln3_b, li2_w, li2_b, li3_w, li3_b, causal):
            xn = _ln(x, lnx_g, lnx_b)
            yn = _ln(y, lny_g, lny_b)
            q = jnp.einsum('bsc,hcd->bhsd', xn, wq)
            k = jnp.einsum('btc,hcd->bhtd', yn, wk)
            v = jnp.einsum('btc,hcd->bhtd', yn, wv)
            a = jax.nn.softmax(jnp.einsum('bhsd,bhtd->bhst', q, k) * D ** (-0.5), axis=-1)
            if causal:
                s, t = (a.shape[-2], a.shape[-1])
                mask = (jnp.arange(t)[None, :] > jnp.arange(s)[:, None]).astype(a.dtype)
                a = a * mask
            o = jnp.einsum('bhst,bhtd->bhsd', a, v)
            o = o.transpose(0, 2, 1, 3).reshape(x.shape[0], x.shape[1], H * D)
            x_out = x + o @ li1_w + li1_b
            h = jax.nn.gelu(_ln(x_out, ln3_g, ln3_b) @ li2_w + li2_b, approximate=False)
            return x_out + h @ li3_w + li3_b
        x = _ln(xx, ln1_g, ln1_b)
        x = x + _mha(x, x, a1_wq, a1_wk, a1_wv, a1_li1_w, a1_li1_b, a1_lnx_g, a1_lnx_b, a1_lny_g, a1_lny_b, a1_ln3_g, a1_ln3_b, a1_li2_w, a1_li2_b, a1_li3_w, a1_li3_b, causal=True)
        x = _ln(x, ln2_g, ln2_b)
        return x + _mha(x, ee, a2_wq, a2_wk, a2_wv, a2_li1_w, a2_li1_b, a2_lnx_g, a2_lnx_b, a2_lny_g, a2_lny_b, a2_ln3_g, a2_ln3_b, a2_li2_w, a2_li2_b, a2_li3_w, a2_li3_b, causal=False)

    def _L0_ffn_ref(x, w1, conv_w, conv_b, w2):
        import jax, jax.numpy as jnp
        import numpy as np
        B, S, D_MODEL, D_HIDDEN = (4, 256, 128, 512)

        def act_quant(x):
            scale = 127.0 / jnp.clip(jnp.max(jnp.abs(x), axis=-1, keepdims=True), 1e-05)
            return jnp.clip(jnp.round(x * scale), -128, 127) / scale

        def weight_quant(w):
            scale = 1.0 / jnp.clip(jnp.mean(jnp.abs(w)), 1e-05)
            return jnp.clip(jnp.round(w * scale), -1, 1) / scale

        def bit_linear(x, w):
            xq = x + jax.lax.stop_gradient(act_quant(x) - x)
            wq = w + jax.lax.stop_gradient(weight_quant(w) - w)
            return jnp.einsum('bsd,hd->bsh', xq, wq)

        def depthwise_conv1d(x_bcl, w, b):
            y = jax.lax.conv_general_dilated(x_bcl, w, window_strides=(1,), padding=[(1, 1)], dimension_numbers=('NCH', 'OIH', 'NCH'), feature_group_count=x_bcl.shape[1])
            return y + b[None, :, None]
        h = bit_linear(x, w1)
        h = depthwise_conv1d(h.transpose(0, 2, 1), conv_w, conv_b)
        h = h.transpose(0, 2, 1)
        h = jax.nn.silu(h)
        return bit_linear(h, w2)

    def _L1_xattn_ref(x, z, Wq, Wkv, Wo):
        import jax, jax.numpy as jnp
        import numpy as np
        DIM = 128
        LATENT_DIM = 64
        NUM_HEADS = 16
        HEAD_DIM = DIM // NUM_HEADS
        SCALE = HEAD_DIM ** (-0.5)
        B, xN, _ = x.shape
        _, zN, _ = z.shape
        Q = (x @ Wq.T).reshape(B, xN, NUM_HEADS, HEAD_DIM)
        KV = (z @ Wkv.T).reshape(B, zN, 2, NUM_HEADS, HEAD_DIM)
        K = KV[:, :, 0]
        V = KV[:, :, 1]
        attn = jnp.einsum('bqhd,bkhd->bhqk', Q, K) * SCALE
        attn = jax.nn.softmax(attn, axis=-1)
        O = jnp.einsum('bhqk,bkhd->bqhd', attn, V).reshape(B, xN, DIM)
        return O @ Wo.T

    def _L1_ffn_ref(x, gate_w, w1, w3, w2):
        import jax, jax.numpy as jnp
        import numpy as np
        TOP_K = 2
        logits = jnp.einsum('btd,de->bte', x, gate_w)
        probs = jax.nn.softmax(logits, axis=-1)
        expert_weights, expert_indices = jax.lax.top_k(probs, TOP_K)
        expert_weights = expert_weights / expert_weights.sum(-1, keepdims=True)
        E = w1.shape[0]
        out = jnp.zeros_like(x)
        for i in range(E):
            wi = jnp.where(expert_indices == i, expert_weights, 0.0).sum(-1)
            h = jax.nn.silu(jnp.einsum('btd,df->btf', x, w1[i])) * jnp.einsum('btd,df->btf', x, w3[i])
            out = out + jnp.einsum('btf,fd->btd', h, w2[i]) * wi[..., None]
        return out

    def _L2_xattn_ref(q, kv, Wq, Wk, Wv, Wo, bo):
        import jax, jax.numpy as jnp
        import numpy as np
        NUM_HEADS = 16
        HEAD_DIM = 64
        Q_DIM = 128
        KV_DIM = 64
        INNER = NUM_HEADS * HEAD_DIM
        B, N, _ = q.shape
        M = kv.shape[1]
        scale = HEAD_DIM ** (-0.5)
        qh = (q @ Wq).reshape(B, N, NUM_HEADS, HEAD_DIM).transpose(0, 2, 1, 3)
        kh = (kv @ Wk).reshape(B, M, NUM_HEADS, HEAD_DIM).transpose(0, 2, 1, 3)
        vh = (kv @ Wv).reshape(B, M, NUM_HEADS, HEAD_DIM).transpose(0, 2, 1, 3)
        scores = jnp.einsum('bhnd,bhmd->bhnm', qh, kh) * scale
        attn = jax.nn.softmax(scores, axis=-1)
        out = jnp.einsum('bhnm,bhmd->bhnd', attn, vh)
        out = out.transpose(0, 2, 1, 3).reshape(B, N, INNER)
        return out @ Wo + bo

    def _L2_ffn_ref(x, W_r, W_k, W_v, mu_r, mu_k):
        import jax, jax.numpy as jnp
        import numpy as np
        DIM = 128

        def _reference_tuple_inner(x, W_r, W_k, W_v, mu_r, mu_k):
            B, T, C = x.shape
            x_prev = jnp.concatenate([jnp.zeros((B, 1, C), x.dtype), x[:, :-1, :]], axis=1)
            xr = mu_r * x + (1.0 - mu_r) * x_prev
            xk = mu_k * x + (1.0 - mu_k) * x_prev
            r = jax.nn.sigmoid(jnp.einsum('btc,dc->btd', xr, W_r))
            k = jnp.einsum('btc,dc->btd', xk, W_k)
            k_act = jnp.square(jax.nn.relu(k))
            out = r * jnp.einsum('btc,dc->btd', k_act, W_v)
            new_state = x[:, -1, :]
            return (out, new_state)
        return _reference_tuple_inner(x, W_r, W_k, W_v, mu_r, mu_k)[0]

    def _L3_xattn_ref(q, k, v, Wq, bq, Wk, bk, Wv, bv, Wo, bo):
        import jax, jax.numpy as jnp
        import numpy as np
        HEADS = 16
        D_MODEL = 128
        IMG_MODEL = 64
        D_K = D_MODEL // HEADS
        B, LQ, _ = q.shape
        LKV = k.shape[1]
        qh = (q @ Wq + bq).reshape(B, LQ, HEADS, D_K).transpose(0, 2, 1, 3)
        kh = (k @ Wk + bk).reshape(B, LKV, HEADS, D_K).transpose(0, 2, 1, 3)
        vh = (v @ Wv + bv).reshape(B, LKV, HEADS, D_K).transpose(0, 2, 1, 3)
        scale = 1.0 / np.sqrt(D_K)
        scores = jnp.einsum('bhqd,bhkd->bhqk', qh, kh) * scale
        attn = jax.nn.softmax(scores, axis=-1)
        out = jnp.einsum('bhqk,bhkd->bhqd', attn, vh)
        concat = out.transpose(0, 2, 1, 3).reshape(B, LQ, D_MODEL)
        return concat @ Wo + bo

    def _L3_ffn_ref(hidden_states, router_w, w1, b1, w2, b2, sw1, sb1, sw2, sb2):
        import math
        import jax, jax.numpy as jnp
        import numpy as np
        H = 128
        F = 512
        E = 8
        TOP_K = 2
        CAP_FACTOR = 1.25
        MIN_CAP = 4
        SHARED_SCALE = 0.1

        def _top2_gating(logits, capacity):
            N, nE = logits.shape
            gates = jax.nn.softmax(logits, axis=-1)
            idx1 = jnp.argmax(gates, axis=-1)
            mask1 = jax.nn.one_hot(idx1, nE, dtype=gates.dtype)
            idx2 = jnp.argmax(gates * (1.0 - mask1), axis=-1)
            mask2 = jax.nn.one_hot(idx2, nE, dtype=gates.dtype)
            pos1 = jnp.cumsum(mask1, axis=0) - mask1
            mask1 = mask1 * (pos1 < capacity)
            pos2 = jnp.cumsum(mask2, axis=0) - mask2 + jnp.sum(mask1, axis=0, keepdims=True)
            mask2 = mask2 * (pos2 < capacity)
            g1 = jnp.sum(gates * mask1, axis=-1)
            g2 = jnp.sum(gates * mask2, axis=-1)
            denom = jnp.maximum(g1 + g2, jnp.finfo(gates.dtype).eps)
            g1, g2 = (g1 / denom, g2 / denom)
            loc1 = jnp.sum(pos1 * mask1, axis=-1).astype(jnp.int32)
            loc2 = jnp.sum(pos2 * mask2, axis=-1).astype(jnp.int32)
            oh1 = jax.nn.one_hot(loc1, capacity, dtype=gates.dtype)
            oh2 = jax.nn.one_hot(loc2, capacity, dtype=gates.dtype)
            combine = (g1[:, None] * mask1)[:, :, None] * oh1[:, None, :] + (g2[:, None] * mask2)[:, :, None] * oh2[:, None, :]
            dispatch = (combine > 0).astype(gates.dtype)
            return (combine, dispatch)
        B, S, h = hidden_states.shape
        x = hidden_states.reshape(-1, h)
        N = x.shape[0]
        capacity = min(max(MIN_CAP, math.ceil(TOP_K * CAP_FACTOR * N / E)), N)
        logits = x @ router_w
        combine, dispatch = _top2_gating(logits, capacity)
        expert_in = jnp.einsum('nec,nh->ech', dispatch, x)
        hmid = jax.nn.silu(jnp.einsum('ech,ehf->ecf', expert_in, w1) + b1[:, None, :])
        expert_out = jnp.einsum('ecf,efh->ech', hmid, w2) + b2[:, None, :]
        y = jnp.einsum('nec,ech->nh', combine, expert_out)
        shared = jax.nn.silu(x @ sw1 + sb1) @ sw2 + sb2
        out = y + SHARED_SCALE * shared
        return out.reshape(B, S, h)
    x = x + jnp.tanh(g_xattn[0]) * _L0_xattn_ref(_layernorm(x, axis=-1), ctx_512, L0_xattn_ln1_g, L0_xattn_ln1_b, L0_xattn_ln2_g, L0_xattn_ln2_b, L0_xattn_a1_wq, L0_xattn_a1_wk, L0_xattn_a1_wv, L0_xattn_a1_li1_w, L0_xattn_a1_li1_b, L0_xattn_a1_lnx_g, L0_xattn_a1_lnx_b, L0_xattn_a1_lny_g, L0_xattn_a1_lny_b, L0_xattn_a1_ln3_g, L0_xattn_a1_ln3_b, L0_xattn_a1_li2_w, L0_xattn_a1_li2_b, L0_xattn_a1_li3_w, L0_xattn_a1_li3_b, L0_xattn_a2_wq, L0_xattn_a2_wk, L0_xattn_a2_wv, L0_xattn_a2_li1_w, L0_xattn_a2_li1_b, L0_xattn_a2_lnx_g, L0_xattn_a2_lnx_b, L0_xattn_a2_lny_g, L0_xattn_a2_lny_b, L0_xattn_a2_ln3_g, L0_xattn_a2_ln3_b, L0_xattn_a2_li2_w, L0_xattn_a2_li2_b, L0_xattn_a2_li3_w, L0_xattn_a2_li3_b, 0)
    x = x + jnp.tanh(g_ffn[0]) * _L0_ffn_ref(_layernorm(x, axis=-1), L0_ffn_w1, L0_ffn_conv_w, L0_ffn_conv_b, L0_ffn_w2)
    x = x + jnp.tanh(g_xattn[1]) * _L1_xattn_ref(_layernorm(x, axis=-1), ctx_512, L1_xattn_Wq, L1_xattn_Wkv, L1_xattn_Wo)
    x = x + jnp.tanh(g_ffn[1]) * _L1_ffn_ref(_layernorm(x, axis=-1), L1_ffn_gate_w, L1_ffn_w1, L1_ffn_w3, L1_ffn_w2)
    x = x + jnp.tanh(g_xattn[2]) * _L2_xattn_ref(_layernorm(x, axis=-1), ctx_512, L2_xattn_Wq, L2_xattn_Wk, L2_xattn_Wv, L2_xattn_Wo, L2_xattn_bo)
    x = x + jnp.tanh(g_ffn[2]) * _L2_ffn_ref(_layernorm(x, axis=-1), L2_ffn_W_r, L2_ffn_W_k, L2_ffn_W_v, L2_ffn_mu_r, L2_ffn_mu_k)
    x = x + jnp.tanh(g_xattn[3]) * _L3_xattn_ref(_layernorm(x, axis=-1), ctx_512, ctx_512, L3_xattn_Wq, L3_xattn_bq, L3_xattn_Wk, L3_xattn_bk, L3_xattn_Wv, L3_xattn_bv, L3_xattn_Wo, L3_xattn_bo)
    x = x + jnp.tanh(g_ffn[3]) * _L3_ffn_ref(_layernorm(x, axis=-1), L3_ffn_router_w, L3_ffn_w1, L3_ffn_b1, L3_ffn_w2, L3_ffn_b2, L3_ffn_sw1, L3_ffn_sb1, L3_ffn_sw2, L3_ffn_sb2)
    return x

_drawn_inputs = setup_inputs


def setup_inputs(seed=0):
    import zlib

    import numpy as np

    out = dict(_drawn_inputs(seed))
    spreads = {'L0_xattn_ln1_g': (1.0, 0.2),
     'L0_xattn_ln1_b': (0.0, 0.1),
     'L0_xattn_ln2_g': (1.0, 0.2),
     'L0_xattn_ln2_b': (0.0, 0.1),
     'L0_xattn_a1_li1_b': (0.0, 0.274),
     'L0_xattn_a1_lnx_g': (1.0, 0.6),
     'L0_xattn_a1_lnx_b': (0.0, 0.8),
     'L0_xattn_a1_lny_g': (1.0, 0.6),
     'L0_xattn_a1_lny_b': (0.0, 0.8),
     'L0_xattn_a1_ln3_g': (1.0, 0.6),
     'L0_xattn_a1_ln3_b': (0.0, 0.8),
     'L0_xattn_a1_li2_b': (0.0, 0.8),
     'L0_xattn_a1_li3_b': (0.0, 0.275),
     'L0_xattn_a2_li1_b': (0.0, 0.276),
     'L0_xattn_a2_lnx_g': (1.0, 0.6),
     'L0_xattn_a2_lnx_b': (0.0, 0.8),
     'L0_xattn_a2_lny_g': (1.0, 0.6),
     'L0_xattn_a2_lny_b': (0.0, 0.8),
     'L0_xattn_a2_ln3_g': (1.0, 0.6),
     'L0_xattn_a2_ln3_b': (0.0, 0.8),
     'L0_xattn_a2_li2_b': (0.0, 0.8),
     'L0_xattn_a2_li3_b': (0.0, 0.29),
     'L3_xattn_bq': (0.0, 2.0),
     'L3_xattn_bk': (0.0, 2.0),
     'L3_xattn_bv': (0.0, 0.82),
     'L3_xattn_bo': (0.0, 0.274)}
    factors = {'g_ffn': 8.0,
     'L0_xattn_a1_wq': 8.0,
     'L0_xattn_a1_wk': 8.0,
     'L0_xattn_a1_wv': 8.0,
     'L0_xattn_a1_li1_w': 8.0,
     'L0_xattn_a1_li2_w': 3.609,
     'L0_xattn_a1_li3_w': 3.212,
     'L0_xattn_a2_wq': 8.0,
     'L0_xattn_a2_wk': 8.0,
     'L0_xattn_a2_wv': 3.881,
     'L0_xattn_a2_li1_w': 4.076,
     'L0_xattn_a2_li2_w': 3.384,
     'L0_xattn_a2_li3_w': 3.081,
     'L0_ffn_w1': 3.292,
     'L0_ffn_conv_w': 3.117,
     'L1_ffn_gate_w': 8.0,
     'L1_ffn_w1': 8.0,
     'L1_ffn_w3': 8.0,
     'L1_ffn_w2': 8.0,
     'L2_xattn_bo': 45.947,
     'L2_ffn_W_r': 8.0,
     'L2_ffn_mu_r': 8.0,
     'L2_ffn_mu_k': 4.052,
     'L3_ffn_b1': 29.881,
     'L3_ffn_b2': 8.0,
     'L3_ffn_sw1': 8.0,
     'L3_ffn_sb1': 25.398,
     'L3_ffn_sw2': 8.0,
     'L3_ffn_sb2': 64.0,
     'L3_ffn_w1': 2.833}
    for name, (base, spread) in spreads.items():
        noise = np.random.default_rng([zlib.crc32(name.encode()), seed]).standard_normal(out[name].shape)
        drawn = base * np.exp(spread * noise) if base else spread * noise
        out[name] = jnp.asarray(drawn.astype(out[name].dtype))
    for name, factor in factors.items():
        out[name] = (out[name] * factor).astype(out[name].dtype)
    return out
```

```python
from contextlib import ExitStack

import concourse.bass as bass
from concourse import mybir

ALU = mybir.AluOpType
ACT = mybir.ActivationFunctionType
F32 = mybir.dt.float32
BF16 = mybir.dt.bfloat16
F32R = mybir.dt.float32r
AX = mybir.AxisListType.X

P = 128
B, S, M = 4, 512, 32
N = B * S
C = 512
NC_ = N // C
TT = C // P
H = 16
CD = 64
F = 512
NF = F // P
E = 8
NT = N // P
CAP = min(max(4, -(-2 * 5 * N // (4 * E))), N)
MAGIC = 12582912.0
LN_EPS = 1e-5
FLT_EPS = 1.1920929e-07

COLS = {}
for _name, _n in [
    ("gx", 4), ("gf", 4), ("ln1_g", 1), ("ln1_b", 1), ("ln2_g", 1), ("ln2_b", 1),
    ("a1_lnx_g", 1), ("a1_lnx_b", 1), ("a1_lny_g", 1), ("a1_lny_b", 1), ("a1_ln3_g", 1), ("a1_ln3_b", 1),
    ("a1_li1_b", 1), ("a1_li2_b", 4), ("a1_li3_b", 1),
    ("a2_lnx_g", 1), ("a2_lnx_b", 1), ("a2_lny_g", 1), ("a2_lny_b", 1), ("a2_ln3_g", 1), ("a2_ln3_b", 1),
    ("a2_li1_b", 1), ("a2_li2_b", 4), ("a2_li3_b", 1),
    ("conv_w", 12), ("conv_b", 4), ("bo2", 1), ("mu_r", 1), ("mu_k", 1),
    ("bq3", 1), ("bk3", 1), ("bv3", 1), ("bo3", 1), ("sb1", 4), ("sb2", 1),
]:
    COLS[_name] = (sum(n for _, n in COLS.values()), _n)
NCOLS = sum(n for _, n in COLS.values())

CROSS = [
    dict(nch=4, scale=32.0 ** -0.5, gate=None, bias="a2_li1_b"),
    dict(nch=1, scale=8.0 ** -0.5, gate=1, bias=None),
    dict(nch=8, scale=64.0 ** -0.5, gate=2, bias="bo2"),
    dict(nch=1, scale=8.0 ** -0.5, gate=3, bias="bo3"),
]
LN_AFF = [0, 1, 2, 1, 1, 1, 1, 0, 0, 0, 0, 0, 0, 0]
EXP_COLS = {"moe1": 12 * P, "moe3": 8 * P + 5}


def build(nc, d):
    ctx = ExitStack()
    with ctx:
        def sb(name, shape, dt=F32):
            return ctx.enter_context(nc.sbuf_tensor(name, shape, dt))

        def sem(name):
            return ctx.enter_context(nc.semaphore(name))

        bank = [ctx.enter_context(nc.psum_tensor(f"bank{i}", [P, C], F32)) for i in range(8)]

        x = sb("x", [P, N])
        a1 = sb("a1", [P, N])
        a234 = sb("a234", [P, 3 * N])
        a2, a3, a4 = (a234[:, k * N:(k + 1) * N] for k in range(3))
        arena = sb("arena", [P, 8192])
        arena_r = sb("arena_r", [P, 12288], F32R)
        cols = sb("cols", [P, NCOLS])
        tg = sb("tg", [P, 8])
        gbo = sb("gbo", [P, 4])
        ident = sb("ident", [P, P])
        identb = sb("identb", [P, P], BF16)
        mean_mat = sb("mean_mat", [P, P])
        ones_mat = sb("ones_mat", [P, P])
        mean64 = sb("mean64", [CD, CD])
        before = sb("before", [P, P])
        eps = sb("eps", [P, 1])
        credit = sb("credit", [P, 32])
        masks = {1: sb("mask8", [P, 16]), 4: sb("mask32", [P, 4]), 8: sb("mask64", [P, 2])}
        rank = sb("rank", [P, E])

        def col(name, j=0):
            return cols[:, COLS[name][0] + j:COLS[name][0] + j + 1]

        def ch(t, c):
            return t[:, c * C:(c + 1) * C]

        ln_sqr = sb("ln_sqr", [P, 2, C])
        ln_rs = sb("ln_rs", [P, NC_, TT])
        w_qkv = sb("w_qkv", [P, 4, 3, P])
        w_li1 = sb("w_li1", [P, 4, P])
        pbuf = sb("pbuf", [P, 2, 4, C])

        q_st = arena_r[:, 0:8 * C].rearrange("p (a h s) -> p a h s", a=2, h=4)
        k_st = arena_r[:, 8 * C:16 * C].rearrange("p (a h s) -> p a h s", a=2, h=4)
        parts = arena_r[:, 16 * C:20 * C].rearrange("p (k h s) -> p k h s", k=2, h=2)
        sel = arena_r[:, 20 * C:21 * C].rearrange("p (k m) -> p k m", k=4)
        ptb = arena[:, 0:8 * C].rearrange("p (a h k s) -> p a h k s", a=2, h=4, k=TT)
        qt = arena[:, 8 * C:9 * C]
        kt = arena[:, 9 * C:10 * C]
        vt = arena[:, 10 * C:11 * C]
        vs = arena[:, 11 * C:13 * C].rearrange("p (a t m) -> p a t m", a=2, t=TT)
        nmx = sb("nmx", [P, 64])
        rsum = sb("rsum", [P, 2, TT, 4])
        rcol = sb("rcol", [P, 16])
        rinv = sb("rinv", [P, TT, P])
        rbs = sb("rbs", [P, C])
        osb = sb("osb", [P, C])
        w_li2 = sb("w_li2", [P, F])
        w_li3 = sb("w_li3", [P, NF, P])
        hid = pbuf

        def hid_t(k):
            return hid[:, 0, k, :]
        ctx_t = sb("ctx_t", [CD, P])
        ctx_n = sb("ctx_n", [CD, P])
        cln = sb("cln", [CD, 3, P])
        cwq = sb("cwq", [P, 1024])
        cwk = sb("cwk", [CD, 1024])
        cwv = sb("cwv", [CD, 1024])
        cwo = sb("cwo", [P, 1024])
        qk = sb("qk", [P, B, C])
        vw = a3
        qb = arena[0:1, 4608:4608 + 4 * C].rearrange("p (b s) -> p b s", b=B)
        kbd = arena[:, 0:2048]
        vbd = arena[:, 2048:4096]
        kts = arena[:, 4096:4096 + 2 * P].rearrange("p (a t) -> p a t", a=2)
        e_ = arena[:, 0:2048].rearrange("p (a s) -> p a s", a=4)
        pn = arena[:, 2048:3072].rearrange("p (a s) -> p a s", a=2)
        ptc = pbuf
        cmx = sb("cmx", [P, 2, H])
        csum = sb("csum", [P, 2, H])
        crin = sb("crin", [P, 4, H])

        f0w1 = arena[:, 6144:6144 + F]
        f0w2 = arena[:, 6144 + F:6144 + 2 * F]
        f0tmp = arena[:, 6144 + 2 * F:6144 + 3 * F]
        w1q = sb("w1q", [P, F], BF16)
        w2q = sb("w2q", [P, F], BF16)
        cwm = sb("cwm", [P, 12])
        wmean = sb("wmean", [P, 2])
        wsc = sb("wsc", [P, 2])
        wabs = sb("wabs", [P, 2])
        sil = [t.rearrange("p (f s) -> p f s", f=NF) for t in
               (a2, a3, a4, qk[:, :, :].rearrange("p b s -> p (b s)"))]
        t32 = arena[:, 1536:2560].rearrange("p (a s) -> p a s", a=2)
        hpad = arena[:, 2560:2560 + 2 * (C + 2)].rearrange("p (a s) -> p a s", a=2)
        yc = arena[:, 3604:4628].rearrange("p (a s) -> p a s", a=2)
        ibs = arena[:, 4628:5652].rearrange("p (a s) -> p a s", a=2)
        os_ = arena[:, 5652:5908].rearrange("p (a s) -> p a s", a=2)
        lowp = pbuf[:, 1, :, :].rearrange("p k s -> p (k s)").bitcast(BF16).rearrange("p (k s) -> p k s", s=C)
        qa = sb("qa", [P, 2, 3, 4])
        wr = sb("wr", [P, 3, P])
        omu = sb("omu", [P, 2])
        mixr = arena[:, 0:1024].rearrange("p (a s) -> p a s", a=2)
        mixk = arena[:, 1024:2048].rearrange("p (a s) -> p a s", a=2)
        rg = arena[:, 2048:3072].rearrange("p (a s) -> p a s", a=2)
        kact = arena[:, 3072:4096].rearrange("p (a s) -> p a s", a=2)
        rv = arena[:, 4096:5120].rearrange("p (a s) -> p a s", a=2)
        gate_w = sb("gate_w", [P, 2, E])
        ew = arena[:, 0:3072].rearrange("p (a w) -> p a w", a=2)
        wb = a234[:, 0:2 * N].rearrange("p (a n) -> p a n", a=2)
        hring = pbuf[:, 0, :, :].rearrange("p k s -> p (k s)").rearrange("p (k s) -> p k s", k=4)
        esil = arena[:, 3072:4096].rearrange("p (k s) -> p k s", k=2)
        yt = arena[:, 7040:8064].rearrange("p (k s) -> p k s", k=2)
        gt = [arena[:, 5120 + k * P:5120 + (k + 1) * P] for k in range(14)]
        g16 = arena[:, 6912:6912 + 8 * NT].rearrange("p (k t) -> p k t", k=8)

        s = {}

        def sg(name):
            if name not in s:
                s[name] = sem(name)
            return s[name]

        for name in (
            "ld_x ld_cols ld_ctx const_ready gates_ready "
            "ln_mean ln_cent ln_sq ln_var ln_std ln_rinv ln_spread ln_norm ln_aff "
            "w_qkv_in sel_ready prep_mm_act prep_mm_dve prep_act prep_dve q_split k_split sc_ready max_ready exp_ready "
            "masked turned ev_dve ev_act av_done rcol_ready rinv_ready o_ready r1_init "
            "mlp_w_in mlp_up mlp_gelu mlp_down mlp_res mlp_out dve_link act_link pool_link "
            "cw_in cx_proj cx_kts cx_bd cx_fold cx_folded cx_ln_mm cx_ln_dve cx_ln_act cx_bias cx_bias_row "
            "ca_score ca_max ca_sub ca_exp ca_sum ca_rinv ca_prob ca_turned ca_pt ca_av ca_res "
            "small_in f0w_in f0w_mean f0w_ready f1_turned f1_am f1_q f1_qt f1_ib f1_ibs f1_xqt f1_h f1_hd f1_c0  f1_c2 "
            "f1_silu f2_turned f2_am f2_step f2_q f2_qt f2_hqt f2_o f2_os f2_ot f2_res "
            "m1_w0 m1_w1 m1_up m1_sil m1_h m1_down m1_t m1_acc m3_w0 m3_w1 m3_wsh m3_up m3_h m3_down m3_t m3_acc "
            "g_logit g_exp g_in g_pre g_cum g_row g_rowt g_stored "
            "r_mix0 r_mix r_up r_gate r_act r_val r_out x_out m1_out sh_weight stored g_capmm "
        ).split():
            sg(name)

        LN_PRE = [4 * sum(LN_AFF[:n]) for n in range(len(LN_AFF) + 1)]

        def aff_at(n, c, j):
            return LN_PRE[n] + c * LN_AFF[n] + j + 1

        def ln_pe(pe, n, src, ready):
            for c in range(NC_):
                for sm, v in ready(c):
                    pe.wait_ge(sm, v)
                if c >= 2:
                    pe.wait_ge(s["ln_cent"], 4 * n + c - 1)
                pe.matmul(bank[c % 2][:, :], mean_mat[:, :], ch(src, c), start=True, stop=True)\
                    .then_inc(s["ln_mean"], 1)

            def variance(c):
                pe.wait_ge(s["ln_sq"], 4 * n + c + 1)
                if c < 2:
                    pe.wait_ge(s["ln_cent"], 4 * n + c + 3)
                else:
                    pe.wait_ge(s["ln_std"], 4 * n + c - 1)
                for t in range(TT):
                    ins = pe.matmul(bank[c % 2][:, t:t + 1], ln_sqr[:, c % 2, t * P:(t + 1) * P], mean_mat[:, 0:1],
                                    start=True, stop=True)
                ins.then_inc(s["ln_var"], 1)

            def spread(c):
                pe.wait_ge(s["ln_rinv"], 4 * n + c + 1)
                if c >= 2:
                    pe.wait_ge(s["ln_norm"], 4 * n + c - 1)
                for t in range(TT):
                    ins = pe.matmul(bank[2 + c % 2][:, t * P:(t + 1) * P],
                                    ln_rs[:, c, t:t + 1].to_broadcast([P, P]), ident[:, :], start=True, stop=True)
                ins.then_inc(s["ln_spread"], 1)
            variance(0)
            for c in range(1, NC_):
                variance(c)
                spread(c - 1)
            spread(NC_ - 1)

        def ln_dve(dve, n, src, dst):
            for c in range(NC_):
                dve.wait_ge(s["ln_mean"], 4 * n + c + 1)
                dve.tensor_tensor(ch(dst, c), ch(src, c), bank[c % 2][:, :], ALU.subtract)\
                    .then_inc(s["ln_cent"], 1)

            def inverse(c):
                dve.wait_ge(s["ln_std"], 4 * n + c + 1)
                dve.reciprocal(ln_rs[:, c, :], ln_rs[:, c, :]).then_inc(s["ln_rinv"], 1)

            inverse(0)
            for c in range(NC_):
                if c + 1 < NC_:
                    inverse(c + 1)
                dve.wait_ge(s["ln_spread"], 4 * n + c + 1)
                dve.tensor_tensor(ch(dst, c), ch(dst, c), bank[2 + c % 2][:, :], ALU.mult)\
                    .then_inc(s["ln_norm"], 1)

        def ln_act(act, n, dst, affine=()):
            for c in range(NC_):
                act.wait_ge(s["ln_cent"], 4 * n + c + 1)
                if 4 * n + c >= 2:
                    act.wait_ge(s["ln_var"], 4 * n + c - 1)
                act.activation(ln_sqr[:, c % 2, :], ch(dst, c), ACT.Square).then_inc(s["ln_sq"], 1)

            def out(c):
                act.wait_ge(s["ln_norm"], 4 * n + c + 1)
                for o, g, b in affine:
                    act.activation(ch(o, c), ch(dst, c), ACT.Identity, bias=col(b), scale=col(g))\
                        .then_inc(s["ln_aff"], 1)
            for c in range(NC_):
                act.wait_ge(s["ln_var"], 4 * n + c + 1)
                act.activation(ln_rs[:, c, :], bank[c % 2][:, 0:TT], ACT.Sqrt, bias=eps[:, 0:1])\
                    .then_inc(s["ln_std"], 1)
                if c >= 1 and affine:
                    out(c - 1)
            if affine:
                out(NC_ - 1)

        CR = 8
        PREP = 6
        JOBS = 28

        def sa_jobs(u):
            g, i = u // 4, u % 4
            if i == 0:
                return [["q"], ["k"], ["v"], ["spread"] if g else []]
            if i == 1:
                return [["q0"], [], ["v_turn"], ["q1"]]
            if i == 2:
                return [["k0"], ["q2"], ["k1"], ["out"] if g else []]
            return [["k2"], ["q3"], ["k3"], []]

        BY_ACT = ("q", "v", "q0", "q1", "q2", "q3", "spread")

        def sa_count(u, name):
            n = 0
            for w in range(16):
                for slot in sa_jobs(w):
                    for job in slot:
                        if (w, job) == (u, name):
                            return n
                        n += (job in BY_ACT) == (name in BY_ACT)
            return n

        def sa_kind(u, act):
            return [job for slot in sa_jobs(u) for job in slot if (job in BY_ACT) == act]

        def sa_sp(sp):
            sp.dma_start(w_qkv[:, :, :, :].rearrange("p g k m -> p (g k m)"), d["w_qkv"]).then_inc(s["w_qkv_in"], 16)
            sp.dma_start(w_li1[:, :, :].rearrange("p g m -> p (g m)"), d["w_li1"]).then_inc(s["w_qkv_in"], 16)

        def sa_sel_dve(dve):
            dve.tensor_scalar(sel[:, :, :], ones_mat[:, :].unsqueeze(1).to_broadcast([P, 4, P]), 0.0, None, ALU.mult).then_inc(s["sel_ready"], 1)
            dve.wait_ge(s["sel_ready"], 1)
            for kind, blocks in enumerate(((0, 1), (2, 3), (0, 2), (1, 3))):
                for blk in blocks:
                    for h in range(4):
                        rows = slice(32 * h, 32 * h + 32)
                        dve.tensor_copy(sel[rows, kind, 32 * blk:32 * blk + 32], ident[rows, rows])\
                            .then_inc(s["sel_ready"], 1)

        PREP_ACT, PREP_DVE = ("q", "v", "q0", "q1", "q2", "q3"), ("k", "v_turn", "k0", "k1", "k2", "k3")

        def sa_pe(pe):
            def prepare(name, g, col_, before_, v_copied, group):
                act = name in BY_ACT
                out = bank[6 if act else 7]
                if type(before_) is not int or before_:
                    pe.wait_ge(s["prep_act" if act else "prep_dve"], before_)
                if name in ("q", "k", "v"):
                    src = a234[:, bass.ds(col_ + (0 if name == "q" else N), C)]
                    ins = pe.matmul(out[:, :], w_qkv[:, g, "qkv".index(name), :], src, start=True, stop=True)
                elif name == "v_turn":
                    pe.wait_ge(s["prep_act"], v_copied)
                    for t in range(TT):
                        ins = pe.transpose(out[:, t * P:(t + 1) * P], vt[:, t * P:(t + 1) * P], ident[:, :])
                else:
                    k = 0 if act else 1
                    rows = slice(32 * int(name[1]), 32 * int(name[1]) + 32)
                    pe.wait_ge(s["k_split" if k else "q_split"], group * 2 + 2)
                    for low in range(2):
                        ins = pe.matmul(out[:, :], sel[rows, 2 * k + low, :], parts[rows, k, low, :],
                                        start=(low == 0), stop=(low == 1))
                ins.then_inc(s["prep_mm_act" if act else "prep_mm_dve"], 1)

            pe.wait_ge(s["w_qkv_in"], 32)
            pe.wait_ge(s["sel_ready"], 33)
            for n in range(PREP):
                prepare(PREP_ACT[n], 0, 0, n, 2, 0)
                prepare(PREP_DVE[n], 0, 0, n, 2, 0)
            with pe.Fori(0, B) as b:
                def score(u, h):
                    g, i, t = u // 4, u % 4, 4 * u + h
                    if i == 0 and h == 0:
                        last = JOBS * b if g == 0 else PREP + JOBS * b + sa_count(u, "q")
                        pe.wait_ge(s["prep_act"], last + (PREP if g == 0 else 0))
                        last = JOBS * b if g == 0 else PREP + JOBS * b + sa_count(u, "k")
                        pe.wait_ge(s["prep_dve"], last + (PREP if g == 0 else 0))
                    pe.wait_ge(s["exp_ready"], b * 64 + (t - 2 if t > 2 else 0) + CR)
                    pe.matmul(bank[t % 3][:, :], q_st[:, g % 2, h, i * P:(i + 1) * P], k_st[:, g % 2, h, :],
                              start=True, stop=True).then_inc(s["sc_ready"], 1)

                def turn(u, h):
                    i = u % 4
                    if h == 0:
                        pe.wait_ge(s["masked"], b * 16 + u + 1)
                    pe.wait_ge(s["ev_act" if h % 2 else "ev_dve"], b * 32 + 2 * u + h // 2 + CR)
                    for k in range(i, 4):
                        ins = pe.transpose(bank[3 + h % 2][:, (k - i) * P:(k - i + 1) * P],
                                           pbuf[:, u % 2, h, k * P:(k + 1) * P], ident[:, :])
                    ins.then_inc(s["turned"], 1)

                def attend(u):
                    g, i = u // 4, u % 4
                    pe.wait_ge(s["ev_dve"], b * 32 + 2 * u + 2 + CR)
                    pe.wait_ge(s["ev_act"], b * 32 + 2 * u + 2 + CR)
                    if i == 0 and g:
                        pe.wait_ge(s["o_ready"], b * 4 + g)
                    for h in range(4):
                        for k in range(i, 4):
                            ins = pe.matmul(bank[5][32 * h:32 * h + 32, i * P:(i + 1) * P],
                                            vs[:, g % 2, k, 32 * h:32 * h + 32], ptb[:, u % 2, h, k - i, :],
                                            start=(k == i), stop=(k == 3))
                    ins.then_inc(s["av_done"], 1)

                def finish(name, u, g):
                    if name == "spread":
                        pe.wait_ge(s["prep_act"], PREP + JOBS * b + sa_count(u, name))
                        pe.wait_ge(s["rinv_ready"], b * 4 + g + 1)
                        for i in range(TT):
                            ins = pe.matmul(bank[6][:, i * P:(i + 1) * P], rinv[:, i, :], ident[:, :],
                                            start=True, stop=True)
                        ins.then_inc(s["prep_mm_act"], 1)
                    else:
                        pe.wait_ge(s["prep_dve"], PREP + JOBS * b + sa_count(u, name))
                        pe.wait_ge(s["o_ready"], b * 4 + g + 1)
                        pe.matmul(bank[7][:, :], w_li1[:, g, :], osb[:, :], start=True, stop=True)\
                            .then_inc(s["prep_mm_dve"], 1)

                def slot(u, n):
                    g = u // 4
                    for name in sa_jobs(u)[n]:
                        if name in ("spread", "out"):
                            finish(name, u, g - 1)
                        else:
                            prepare(name, (g + 1) % 4, (b * C + C) if g == 3 else b * C,
                                    PREP + JOBS * b + sa_count(u, name),
                                    PREP + JOBS * b + sa_count(4 * g, "v") + 1, 4 * b + g + 1)

                for u in range(16):
                    score(u, 0)
                    score(u, 1)
                    for n in range(4):
                        if u:
                            turn(u - 1, n)
                        slot(u, n)
                        if n < 2:
                            score(u, n + 2)
                        if n == 1 and u >= 2:
                            attend(u - 2)
                for h in range(4):
                    turn(15, h)
                attend(14)
                attend(15)
                finish("spread", 16, 3)
                finish("out", 16, 3)

        def sa_dve(dve):
            def read(name, a, before_):
                dve.wait_ge(s["prep_mm_dve"], before_ + 1)
                dst = {"k": kt, "v_turn": vs[:, a, :, :].rearrange("p t m -> p (t m)")}.get(name)
                if dst is None:
                    dst = k_st[:, a, int(name[1]), :]
                dve.tensor_copy(dst, bank[7][:, :]).then_inc(s["prep_dve"], 1)

            for n in range(PREP):
                read(PREP_DVE[n], 0, n)
            with dve.Fori(0, B) as b:
                def maximum(u, h):
                    t = 4 * u + h
                    dve.wait_ge(s["sc_ready"], b * 64 + t + 1)
                    dve.tensor_reduce(nmx[:, t:t + 1], bank[t % 3][:, :], AX, ALU.max, negate=True)\
                        .then_inc(s["max_ready"], 1)

                def copy(u, h):
                    dve.wait_ge(s["turned"], b * 64 + 4 * u + h + 1)
                    dve.tensor_copy(ptb[:, u % 2, h, 0:4 - u % 4, :],
                                    bank[3][:, 0:(4 - u % 4) * P].rearrange("p (k q) -> p k q", q=P))\
                        .then_inc(s["ev_dve"], 1)

                def inverse(g):
                    dve.wait_ge(s["exp_ready"], b * 64 + 16 * g + 16 + CR)
                    dve.reciprocal(rcol[:, :], rsum[:, g % 2, :, :].rearrange("p t h -> p (t h)"))\
                        .then_inc(s["rcol_ready"], 1)
                    dve.wait_ge(s["rcol_ready"], b * 4 + g + 1)
                    dve.tensor_copy(rinv[:, :, :].rearrange("p t (h r) -> p (t h) r", r=32),
                                    rcol[:, :].unsqueeze(2).to_broadcast([P, 16, 32])).then_inc(s["rinv_ready"], 1)

                def normalise(u, g):
                    dve.wait_ge(s["prep_act"], PREP + JOBS * b + sa_count(u, "spread") + 1)
                    dve.wait_ge(s["av_done"], b * 16 + 4 * g + 4)
                    dve.tensor_tensor(osb[:, :], bank[5][:, :], rbs[:, :], ALU.mult).then_inc(s["o_ready"], 1)

                def residual(u):
                    acc = a234[:, bass.ds(b * C + 2 * N, C)]
                    n = PREP + JOBS * b + sa_count(u, "out")
                    dve.wait_ge(s["prep_dve"], n)
                    dve.wait_ge(s["prep_mm_dve"], n + 1)
                    dve.tensor_tensor(acc, bank[7][:, :], acc, ALU.add).then_inc(s["prep_dve"], 1)

                def job(u, name):
                    if name == "out":
                        residual(u)
                    else:
                        read(name, (u // 4 + 1) % 2, PREP + JOBS * b + sa_count(u, name))

                for u in range(16):
                    g, i = u // 4, u % 4
                    jobs = sa_kind(u, False)
                    maximum(u, 0)
                    maximum(u, 1)
                    if i == 0 and g:
                        inverse(g - 1)
                    if u:
                        copy(u - 1, 0)
                    maximum(u, 2)
                    job(u, jobs[0])
                    maximum(u, 3)
                    if u:
                        copy(u - 1, 2)
                    for name in jobs[1:]:
                        job(u, name)
                    if i == 1 and g:
                        normalise(4 * g, g - 1)
                inverse(3)
                copy(15, 0)
                copy(15, 2)
                normalise(16, 3)
                residual(16)

        def sa_act(act):
            def read(name, a, before_):
                act.wait_ge(s["prep_mm_act"], before_ + 1)
                if name == "q":
                    act.activation(qt, bank[6][:, :], ACT.Copy, scale=32.0 ** -0.5).then_inc(s["prep_act"], 1)
                    return
                dst = {"v": vt, "spread": rbs[:, :]}.get(name)
                if dst is None:
                    dst = q_st[:, a, int(name[1]), :]
                act.activation(dst, bank[6][:, :], ACT.Copy).then_inc(s["prep_act"], 1)

            for n in range(PREP):
                read(PREP_ACT[n], 0, n)
            with act.Fori(0, B) as b:
                def power(u, h):
                    t = 4 * u + h
                    if u >= 2:
                        act.wait_ge(s["turned"], b * 64 + 4 * (u - 2) + h + 1)
                    act.wait_ge(s["max_ready"], b * 64 + t + 1)
                    act.activation(pbuf[:, u % 2, h, :], bank[t % 3][:, :], ACT.Exp, bias=nmx[:, t:t + 1],
                                   accum_out=rsum[:, (u // 4) % 2, u % 4, h:h + 1]).then_inc(s["exp_ready"], 1)

                def copy(u, h):
                    act.wait_ge(s["turned"], b * 64 + 4 * u + h + 1)
                    act.activation(ptb[:, u % 2, h, 0:4 - u % 4, :],
                                   bank[4][:, 0:(4 - u % 4) * P].rearrange("p (k q) -> p k q", q=P),
                                   ACT.Copy).then_inc(s["ev_act"], 1)

                def job(u, name):
                    read(name, (u // 4 + 1) % 2, PREP + JOBS * b + sa_count(u, name))

                for u in range(16):
                    jobs = sa_kind(u, True)
                    power(u, 0)
                    power(u, 1)
                    power(u, 2)
                    job(u, jobs[0])
                    if u:
                        copy(u - 1, 1)
                    power(u, 3)
                    for name in jobs[1:]:
                        job(u, name)
                    if u:
                        copy(u - 1, 3)
                copy(15, 1)
                copy(15, 3)
                job(16, "spread")

        def sa_pool(pool):
            def split(k, half, count, ready):
                src, sm = (kt, "k_split") if k else (qt, "q_split")
                if half == 0:
                    pool.wait_ge(s["prep_dve" if k else "prep_act"], ready)
                    pool.tensor_tensor(parts[:, k, 0, :], src, ones_mat[:, 0:1].to_broadcast([P, C]), ALU.mult)\
                        .then_inc(s[sm], 1)
                else:
                    pool.wait_ge(s[sm], count + 1)
                    pool.tensor_tensor(parts[:, k, 1, :], src, parts[:, k, 0, :].bitcast(F32), ALU.subtract)\
                        .then_inc(s[sm], 1)

            for k in range(2):
                for half in range(2):
                    split(k, half, 0, 1)
            with pool.Fori(0, B) as b:
                for u in range(16):
                    g, i = u // 4, u % 4
                    pool.wait_ge(s["exp_ready"], b * 64 + 4 * u + 4 + CR)
                    blk = pbuf[:, u % 2, :, i * P:(i + 1) * P]
                    pool.tensor_tensor(blk, blk, before[:, :].unsqueeze(1).to_broadcast([P, 4, P]), ALU.mult)\
                        .then_inc(s["masked"], 1)
                    if i < 2:
                        for half in range(2):
                            split(i, half, (4 * b + g + 1) * 2,
                                  PREP + JOBS * b + sa_count(4 * g, "k" if i else "q") + 1)

        def mlp_sp(sp, m):
            if m:
                sp.wait_ge(s["mlp_down"], 16)
            sp.dma_start(w_li2[:, :], d[f"a{m + 1}_li2"]).then_inc(s["mlp_w_in"], 16)
            sp.dma_start(w_li3[:, :, :].rearrange("p f m -> p (f m)"), d[f"a{m + 1}_li3"])\
                .then_inc(s["mlp_w_in"], 16)

        def mlp_pe(pe, m, n):
            b0 = 16 * m

            def up(u):
                c, f = u // NF, u % NF
                if f == 0:
                    pe.wait_ge(s["ln_aff"], aff_at(n, c, 0))
                if u >= 2:
                    pe.wait_ge(s["mlp_gelu"], b0 + u - 1)
                pe.matmul(bank[4 + u % 2][:, :], w_li2[:, f * P:(f + 1) * P], ch(a2, c), start=True, stop=True)\
                    .then_inc(s["mlp_up"], 1)

            def down(u):
                c, f = u // NF, u % NF
                pe.wait_ge(s["mlp_gelu"], b0 + u + 1)
                if f == 0 and c >= 2:
                    pe.wait_ge(s["mlp_res"], 4 * m + c - 1)
                pe.matmul(bank[6 + c % 2][:, :], w_li3[:, f, :], hid_t(u % 4), start=(f == 0), stop=(f == NF - 1))\
                    .then_inc(s["mlp_down"], 1)
            pe.wait_ge(s["mlp_w_in"], 32 * (m + 1))
            up(0)
            up(1)
            for u in range(16):
                down(u)
                if u + 2 < 16:
                    up(u + 2)

        def mlp_act(act, m):
            b0 = 16 * m
            for u in range(16):
                act.wait_ge(s["mlp_up"], b0 + u + 1)
                if u >= 4:
                    act.wait_ge(s["mlp_down"], b0 + u - 3)
                act.activation(hid_t(u % 4), bank[4 + u % 2][:, :], ACT.Gelu, bias=col(f"a{m + 1}_li2_b", u % NF))\
                    .then_inc(s["mlp_gelu"], 1)

        def mlp_dve(dve, m):
            for c in range(NC_):
                dve.wait_ge(s["mlp_down"], 16 * m + 4 * c + 4)
                dve.scalar_tensor_tensor(ch(a4, c), bank[6 + c % 2][:, :], col(f"a{m + 1}_li3_b"), ch(a4, c),
                                         ALU.add, ALU.add).then_inc(s["mlp_res"], 1)
                dve.wait_ge(s["mlp_res"], 4 * m + c + 1)
                ins = dve.tensor_tensor(ch(a1, c), ch(a1, c), ch(a4, c), ALU.add)
                ins.then_inc(s["mlp_out"], 1)
                if m:
                    dve.wait_ge(s["mlp_out"], 4 + 2 * c + 1)
                    dve.scalar_tensor_tensor(ch(x, c), ch(a1, c), tg[:, 0:1], ch(x, c), ALU.mult, ALU.add)\
                        .then_inc(s["mlp_out"], 1)

        NCH = [c["nch"] for c in CROSS]
        BD_PRE = [2 * sum(NCH[:l]) for l in range(5)]

        def cx_sp(sp, l):
            if l:
                sp.wait_ge(s["cx_fold"], 8 * l)
            k = NCH[l] * P
            for t, name in ((cwq, "q"), (cwk, "k"), (cwv, "v"), (cwo, "o")):
                sp.dma_start(t[:, 0:k], d[f"c{l}_{name}"]).then_inc(s["cw_in"], 16)

        def cx_src(l):
            return ctx_n if l == 0 else ctx_t

        def cx_pe(pe, l, free=()):
            nch = NCH[l]
            for sm, v in free:
                pe.wait_ge(sm, v)
            pe.wait_ge(s["cw_in"], 64 * (l + 1))
            for m in range(2 * nch):
                w = cwv if m >= nch else cwk
                q = BD_PRE[l] + m
                if m >= 2:
                    pe.wait_ge(s["cx_kts"], q - 1)
                pe.matmul(bank[5 + m % 2][:, 0:P], w[:, (m % nch) * P:(m % nch + 1) * P], cx_src(l)[:, :],
                          start=True, stop=True).then_inc(s["cx_proj"], 1)
            hw = H // nch * M
            for b in range(B):
                if b == 0:
                    pe.wait_ge(s["cx_bd"], BD_PRE[l] + nch)
                    pe.wait_ge(s["cx_kts"], BD_PRE[l] + 2 * nch)
                if b >= 2:
                    pe.wait_ge(s["cx_folded"], 8 * l + b - 1)
                for c in range(nch):
                    ins = pe.matmul(bank[5 + b % 2][:, c * hw:(c + 1) * hw], cwq[:, c * P:(c + 1) * P],
                                    kbd[:, (c * B + b) * hw:(c * B + b + 1) * hw], start=True, stop=True)
                ins.then_inc(s["cx_fold"], 1)
            for b in range(B):
                if b == 0:
                    pe.wait_ge(s["cx_bd"], BD_PRE[l] + 2 * nch)
                pe.wait_ge(s["cx_folded"], 8 * l + 4 + b - 1)
                for g in range(4):
                    o = bank[5 + b % 2][:, g * P:(g + 1) * P]
                    if nch == 1:
                        ins = pe.matmul(o, vbd[:, b * hw + g * P:b * hw + (g + 1) * P], cwo[:, 0:P],
                                        start=True, stop=True)
                    elif nch == 4:
                        ins = pe.matmul(o, vbd[:, (g * B + b) * hw:(g * B + b + 1) * hw], cwo[:, g * P:(g + 1) * P],
                                        start=True, stop=True)
                    else:
                        for k in range(2):
                            c = 2 * g + k
                            ins = pe.matmul(bank[5 + b % 2][64 * k:64 * k + 64, g * P:(g + 1) * P],
                                            vbd[:, (c * B + b) * hw:(c * B + b + 1) * hw],
                                            cwo[:, c * P:(c + 1) * P], start=True, stop=True)
                ins.then_inc(s["cx_fold"], 1)
            if l == 3:
                for b in range(B):
                    if b:
                        pe.wait_ge(s["cx_bias_row"], b)
                    else:
                        pe.wait_ge(s["cx_folded"], 8 * l + 8)
                    pe.matmul(bank[7][0:1, :], col("bq3"), kbd[:, b * C:(b + 1) * C], start=True, stop=True)\
                        .then_inc(s["cx_bias"], 1)

        def cx_act(act, l):
            nch = NCH[l]
            for m in range(2 * nch):
                q = BD_PRE[l] + m
                act.wait_ge(s["cx_proj"], q + 1)
                if m >= 2:
                    act.wait_ge(s["cx_bd"], q - 1)
                bias = col("bv3" if m >= nch else "bk3") if l == 3 else 0.0
                act.activation(kts[:, m % 2, :], bank[5 + m % 2][:, 0:P], ACT.Identity, bias=bias)\
                    .then_inc(s["cx_kts"], 1)
            for k in range(8):
                act.wait_ge(s["cx_fold"], 8 * l + k + 1)
                if k < 4:
                    act.activation(qk[:, k, :], bank[5 + k % 2][:, :], ACT.Copy).then_inc(s["cx_folded"], 1)
                else:
                    g = CROSS[l]["gate"]
                    scale = 1.0 if g is None else tg[:, g:g + 1]
                    act.activation(ch(vw, k - 4), bank[5 + k % 2][:, :], ACT.Identity, scale=scale)\
                        .then_inc(s["cx_folded"], 1)
            if l == 3:
                for b in range(B):
                    act.wait_ge(s["cx_bias"], b + 1)
                    act.activation(qb[:, b, :], bank[7][0:1, :], ACT.Copy).then_inc(s["cx_bias_row"], 1)

        def cx_dve(dve, l):
            nch = NCH[l]
            hc = H // nch
            hw = hc * M
            for m in range(2 * nch):
                dst = (vbd if m >= nch else kbd)[:, (m % nch) * B * hw:(m % nch + 1) * B * hw]
                dve.wait_ge(s["cx_kts"], BD_PRE[l] + m + 1)
                for b in range(B):
                    ins = dve.tensor_tensor(
                        dst[:, b * hw:(b + 1) * hw].rearrange("p (h t) -> p h t", t=M),
                        kts[:, m % 2, b * M:(b + 1) * M].unsqueeze(1).to_broadcast([P, hc, M]),
                        masks[nch][:, :].unsqueeze(2).to_broadcast([P, hc, M]), ALU.mult)
                ins.then_inc(s["cx_bd"], 1)

        def ca_guard(eng, name, count):
            if count > 0:
                eng.wait_ge(s[name], count)

        def ca_pool(pool, l):
            for v in range(16 * l, 16 * l + 16):
                pool.wait_ge(s["ca_rinv"], v + 1)
                ca_guard(pool, "ca_turned", v - 1)
                pool.tensor_tensor(pn[:, v % 2, :].rearrange("p (h t) -> p h t", t=M),
                                   e_[:, v % 4, :].rearrange("p (h t) -> p h t", t=M),
                                   crin[:, v % 4, :].unsqueeze(2).to_broadcast([P, H, M]), ALU.mult)\
                    .then_inc(s["ca_prob"], 1)

        def ca_pe(pe, l, z, ready):
            v0 = 16 * l

            def score(v):
                b = (v - v0) // TT
                if (v - v0) % TT == 0:
                    for sm, n in ready(b):
                        pe.wait_ge(sm, n)
                ca_guard(pe, "ca_sub", v - 1)
                ins = pe.matmul(bank[v % 2][:, :], z[:, (v - v0) * P:(v - v0 + 1) * P], qk[:, b, :],
                                start=True, stop=(l != 3))
                if l == 3:
                    ins = pe.matmul(bank[v % 2][:, :], ones_mat[0:1, :], qb[:, b, :], start=False, stop=True)
                ins.then_inc(s["ca_score"], 1)

            def turn(v):
                pe.wait_ge(s["ca_prob"], v + 1)
                ca_guard(pe, "ca_pt", v - 1)
                for g in range(4):
                    ins = pe.transpose(bank[2 + v % 2][:, g * P:(g + 1) * P], pn[:, v % 2, g * P:(g + 1) * P],
                                       ident[:, :])
                ins.then_inc(s["ca_turned"], 1)

            def attend(b):
                i = 4 * l + b
                pe.wait_ge(s["ca_pt"], v0 + 4 * b + 4)
                ca_guard(pe, "ca_res", i - 1)
                for g in range(4):
                    ins = pe.matmul(bank[4 + 3 * (b % 2)][:, :], vw[:, b * C + g * P:b * C + (g + 1) * P],
                                    ptc[:, b % 2, g, :], start=(g == 0), stop=(g == 3))
                ins.then_inc(s["ca_av"], 1)
            score(v0)
            score(v0 + 1)
            for v in range(v0, v0 + 16):
                if v + 2 < v0 + 16:
                    score(v + 2)
                turn(v)
                if (v - v0) % TT == 1 and v - v0 > TT:
                    attend((v - v0) // TT - 1)
            attend(B - 1)

        def ca_dve(dve, l, src, dst):
            hs = lambda ap: ap.rearrange("p (h t) -> p h t", t=M)
            v0 = 16 * l

            def centre(v):
                dve.wait_ge(s["ca_score"], v + 1)
                dve.tensor_reduce(cmx[:, v % 2, :], hs(bank[v % 2][:, :]), AX, ALU.max).then_inc(s["ca_max"], 1)
                ca_guard(dve, "ca_prob", v - 3)
                dve.wait_ge(s["ca_max"], v + 1)
                dve.tensor_tensor(hs(e_[:, v % 4, :]), hs(bank[v % 2][:, :]),
                                  cmx[:, v % 2, :].unsqueeze(2).to_broadcast([P, H, M]), ALU.subtract)\
                    .then_inc(s["ca_sub"], 1)

            def total(v):
                dve.wait_ge(s["ca_exp"], v + 1)
                dve.tensor_reduce(csum[:, v % 2, :], hs(e_[:, v % 4, :]), AX, ALU.add).then_inc(s["ca_sum"], 1)
                dve.wait_ge(s["ca_sum"], v + 1)
                dve.reciprocal(crin[:, v % 4, :], csum[:, v % 2, :]).then_inc(s["ca_rinv"], 1)

            def residual(b):
                dve.wait_ge(s["ca_av"], 4 * l + b + 1)
                bias = col("a2_li1_b") if l == 0 else gbo[:, l:l + 1]
                dve.scalar_tensor_tensor(ch(dst, b), bank[4 + 3 * (b % 2)][:, :], bias, ch(src, b),
                                         ALU.add, ALU.add).then_inc(s["ca_res"], 1)
            centre(v0)
            centre(v0 + 1)
            for v in range(v0, v0 + 16):
                total(v)
                if v + 2 < v0 + 16:
                    centre(v + 2)
                if (v - v0) % TT == 3 and v - v0 > TT:
                    residual((v - v0) // TT - 1)
            residual(B - 1)

        def ca_act(act, l):
            v0 = 16 * l

            def power(v):
                act.wait_ge(s["ca_sub"], v + 1)
                act.activation(e_[:, v % 4, :], e_[:, v % 4, :], ACT.Exp, scale=CROSS[l]["scale"])\
                    .then_inc(s["ca_exp"], 1)

            def copy(v):
                b, t = (v - v0) // TT, v % TT
                if t == 0:
                    ca_guard(act, "ca_av", 4 * l + b - 1)
                act.wait_ge(s["ca_turned"], v + 1)
                act.activation(ptc[:, b % 2, :, t * P:(t + 1) * P],
                               bank[2 + v % 2][:, :].rearrange("p (g q) -> p g q", q=P), ACT.Copy)\
                    .then_inc(s["ca_pt"], 1)
            power(v0)
            power(v0 + 1)
            for v in range(v0, v0 + 16):
                if v + 2 < v0 + 16:
                    power(v + 2)
                copy(v)

        CREDIT = [(k, CR) for k in ("exp_ready", "ev_dve", "ev_act")]

        def setup_sp(sp):
            for c in range(NC_):
                sp.dma_start(ch(x, c), d["x"][:, c * C:(c + 1) * C]).then_inc(s["ld_x"], 16)
            sp.dma_start(cols[:, :], d["cols"]).then_inc(s["ld_cols"], 16)
            sp.dma_start(ctx_t[:, :], d["ctx"]).then_inc(s["ld_ctx"], 16)
            sp.dma_start(wr[:, :, :].rearrange("p k m -> p (k m)"), d["f2_w"]).then_inc(s["small_in"], 16)
            sp.dma_start(gate_w[:, :, :].rearrange("p k m -> p (k m)"), d["gates"]).then_inc(s["small_in"], 16)

        n_const = [0]

        def setup_pool(pool):
            def put(ins):
                n_const[0] += 1
                ins.then_inc(s["const_ready"], 1)
                pool.wait_ge(s["const_ready"], n_const[0])
            for k, (name, v) in enumerate(CREDIT):
                pool.memset(credit[:, k:k + 1], 0.0).then_inc(s[name], v)
            put(pool.memset(eps[:, :], LN_EPS))
            put(pool.memset(mean_mat[:, :], 1.0 / P))
            put(pool.memset(mean64[:, :], 1.0 / CD))
            put(pool.memset(ones_mat[:, :], 1.0))
            put(pool.memset(ident[:, :], 0.0))
            put(pool.affine_select(out=ident[:, :], in_=ident[:, :], compare_op=ALU.not_equal, fill=1.0, base=0,
                                   pattern=[[-1, P]], channel_multiplier=1))
            put(pool.tensor_copy(identb[:, :], ident[:, :]))
            put(pool.affine_select(out=before[:, :], in_=ones_mat[:, :], compare_op=ALU.is_gt, fill=0.0, base=0,
                                   pattern=[[1, P]], channel_multiplier=-1))
            for nch, m in masks.items():
                hc = H // nch
                dh = P // hc
                put(pool.memset(m[:, :], 1.0))
                put(pool.affine_select(out=m[:, :], in_=m[:, :], compare_op=ALU.is_ge, fill=0.0, base=0,
                                       pattern=[[-dh, hc]], channel_multiplier=1))
                put(pool.affine_select(out=m[:, :], in_=m[:, :], compare_op=ALU.is_ge, fill=0.0, base=dh - 1,
                                       pattern=[[dh, hc]], channel_multiplier=-1))
            for e in range(E):
                put(pool.memset(rank[:, e:e + 1], float(E - e)))

        N_CONST = 8 + 3 * len(masks) + E

        def setup_act(act):
            act.wait_ge(s["ld_cols"], 16)
            act.activation(tg[:, :], cols[:, 0:8], ACT.Tanh).then_inc(s["gates_ready"], 1)

        links = {"dve": 0, "act": 0, "pool": 0}

        def link(eng, who, ins):
            links[who] += 1
            ins.then_inc(s[who + "_link"], 1)
            eng.wait_ge(s[who + "_link"], links[who])

        def setup_dve(dve):
            dve.wait_ge(s["const_ready"], N_CONST)
            dve.wait_ge(s["gates_ready"], 1)
            dve.memset(gbo[:, :], 0.0).then_inc(s["gates_ready"], 1)
            dve.wait_ge(s["gates_ready"], 2)
            for l, name in ((2, "bo2"), (3, "bo3")):
                dve.tensor_scalar(gbo[:, l:l + 1], col(name), tg[:, l:l + 1], None, ALU.mult)\
                    .then_inc(s["gates_ready"], 1)
            for k, name in enumerate(("mu_r", "mu_k")):
                dve.tensor_scalar(omu[:, k:k + 1], col(name), -1.0, 1.0, ALU.mult, ALU.add)\
                    .then_inc(s["gates_ready"], 1)

        def r1_init_pool(pool):
            for c in range(NC_):
                pool.wait_ge(s["ln_aff"], aff_at(1, c, 0))
                pool.tensor_scalar(ch(a4, c), ch(a1, c), col("a1_li1_b"), None, ALU.add).then_inc(s["r1_init"], 1)

        def cln_pe(pe):
            pe.wait_ge(s["ld_ctx"], 16)
            pe.matmul(bank[4][0:CD, 0:P], mean64[:, :], ctx_t[:, :], start=True, stop=True)\
                .then_inc(s["cx_ln_mm"], 1)
            pe.wait_ge(s["cx_ln_act"], 1)
            pe.matmul(bank[5][0:CD, 0:P], mean64[:, :], cln[:, 1, :], start=True, stop=True)\
                .then_inc(s["cx_ln_mm"], 1)

        def cln_dve(dve):
            dve.wait_ge(s["cx_ln_mm"], 1)
            dve.tensor_tensor(cln[:, 0, :], ctx_t[:, :], bank[4][0:CD, 0:P], ALU.subtract)\
                .then_inc(s["cx_ln_dve"], 1)
            dve.wait_ge(s["cx_ln_act"], 2)
            dve.reciprocal(cln[:, 2, :], cln[:, 2, :]).then_inc(s["cx_ln_dve"], 1)
            dve.wait_ge(s["cx_ln_dve"], 2)
            dve.tensor_tensor(cln[:, 0, :], cln[:, 0, :], cln[:, 2, :], ALU.mult).then_inc(s["cx_ln_dve"], 1)

        def cln_act(act):
            act.wait_ge(s["cx_ln_dve"], 1)
            act.activation(cln[:, 1, :], cln[:, 0, :], ACT.Square).then_inc(s["cx_ln_act"], 1)
            act.wait_ge(s["cx_ln_mm"], 2)
            act.activation(cln[:, 2, :], bank[5][0:CD, 0:P], ACT.Sqrt, bias=eps[0:CD, 0:1])\
                .then_inc(s["cx_ln_act"], 1)
            act.wait_ge(s["cx_ln_dve"], 3)
            act.activation(ctx_n[:, :], cln[:, 0, :], ACT.Identity, bias=col("a2_lny_b")[0:CD, :],
                           scale=col("a2_lny_g")[0:CD, :]).then_inc(s["cx_ln_act"], 1)

        def f0w_sp(sp):
            sp.wait_ge(s["av_done"], 16 * B)
            sp.dma_start(f0w1, d["f0_w1"]).then_inc(s["f0w_in"], 16)
            sp.dma_start(f0w2, d["f0_w2"]).then_inc(s["f0w_in"], 16)

        def f0w_dve(dve):
            dve.wait_ge(s["f0w_in"], 32)
            for k, w in enumerate((f0w1, f0w2)):
                ins = dve.tensor_reduce(wabs[:, k:k + 1], w, AX, ALU.add, apply_absolute_value=True)
            ins.then_inc(s["f0w_ready"], 1)
            dve.wait_ge(s["f0w_mean"], 1)
            link(dve, "dve", dve.tensor_scalar(wmean[:, :], bank[4][:, 0:2], 1.0 / F, 1e-5, ALU.mult, ALU.max))
            link(dve, "dve", dve.reciprocal(wsc[:, :], wmean[:, :]))
            for k, (w, o) in enumerate(((f0w1, w1q), (f0w2, w2q))):
                link(dve, "dve", dve.tensor_scalar(f0tmp, w, wsc[:, k:k + 1], MAGIC, ALU.mult, ALU.add))
                link(dve, "dve", dve.tensor_scalar(f0tmp, f0tmp, MAGIC, 1.0, ALU.subtract, ALU.min))
                link(dve, "dve", dve.tensor_scalar(o[:, :], f0tmp, -1.0, None, ALU.max))
            link(dve, "dve", dve.tensor_scalar(cwm[:, :], cols[:, COLS["conv_w"][0]:COLS["conv_w"][0] + 12],
                                               wmean[:, 0:1], None, ALU.mult))
            link(dve, "dve", dve.memset(hpad[:, :, 0:1], 0.0))
            dve.memset(hpad[:, :, C + 1:C + 2], 0.0).then_inc(s["f0w_ready"], 1)

        def f0w_pe(pe):
            pe.wait_ge(s["f0w_ready"], 1)
            pe.matmul(bank[4][:, 0:2], mean_mat[:, :], wabs[:, :], start=True, stop=True).then_inc(s["f0w_mean"], 1)

        def f1_pe(pe):
            for c in range(NC_):
                pe.wait_ge(s["ln_norm"], 4 * 7 + c + 1)
                if c == 0:
                    pe.wait_ge(s["f0w_ready"], 2)
                if c >= 2:
                    pe.wait_ge(s["f1_q"], c - 1)
                for t in range(TT):
                    ins = pe.transpose(bank[4 + c % 2][:, t * P:(t + 1) * P],
                                       a1[:, c * C + t * P:c * C + (t + 1) * P], ident[:, :])
                ins.then_inc(s["f1_turned"], 1)
                pe.wait_ge(s["f1_am"], c + 1)
                if c:
                    pe.wait_ge(s["f1_ibs"], c)
                for t in range(TT):
                    ins = pe.matmul(bank[7][:, t * P:(t + 1) * P], qa[:, c % 2, 2, t:t + 1].to_broadcast([P, P]),
                                    ident[:, :], start=True, stop=True)
                ins.then_inc(s["f1_ib"], 1)
                pe.wait_ge(s["f1_q"], c + 1)
                if c:
                    pe.wait_ge(s["f1_xqt"], c)
                for t in range(TT):
                    ins = pe.transpose(bank[6][:, :].bitcast(BF16)[:, t * P:(t + 1) * P],
                                       lowp[:, c % 2, t * P:(t + 1) * P], identb[:, :])
                ins.then_inc(s["f1_qt"], 1)
                pe.wait_ge(s["f1_xqt"], c + 1)
                for f in range(NF):
                    if c:
                        pe.wait_ge(s["f1_hd"], 4 * (c - 1) + f + 1)
                    pe.matmul(bank[f][:, :], w1q[:, f * P:(f + 1) * P], lowp[:, 2 + c % 2, :],
                              start=True, stop=True).then_inc(s["f1_h"], 1)

        def quantise(dve, src, a, n, width, am, q, tmp, dst):
            v = src.rearrange("p (t k) -> p t k", k=width)
            link(dve, "dve", dve.tensor_reduce(qa[:, a, 0, 0:n], v, AX, ALU.max, apply_absolute_value=True))
            link(dve, "dve", dve.tensor_scalar(qa[:, a, 0, 0:n], qa[:, a, 0, 0:n], 1e-5, None, ALU.max))
            link(dve, "dve", dve.reciprocal(qa[:, a, 1, 0:n], qa[:, a, 0, 0:n]))
            link(dve, "dve", dve.tensor_scalar(qa[:, a, 1, 0:n], qa[:, a, 1, 0:n], 127.0, None, ALU.mult))
            dve.tensor_scalar(qa[:, a, 2, 0:n], qa[:, a, 0, 0:n], 1.0 / 127.0, None, ALU.mult).then_inc(am, 1)
            for t in range(n):
                ins = dve.tensor_scalar(tmp[:, t * width:(t + 1) * width], v[:, t, :], qa[:, a, 1, t:t + 1], MAGIC,
                                        ALU.mult, ALU.add)
            link(dve, "dve", ins)
            link(dve, "dve", dve.tensor_scalar(tmp, tmp, MAGIC, 127.0, ALU.subtract, ALU.min))
            dve.tensor_scalar(dst, tmp, -128.0, None, ALU.max).then_inc(q, 1)

        def f1_dve(dve):
            for c in range(NC_):
                dve.wait_ge(s["f1_turned"], c + 1)
                quantise(dve, bank[4 + c % 2][:, :], c % 2, 4, P, s["f1_am"], s["f1_q"], t32[:, c % 2, :],
                         lowp[:, c % 2, :])
                for f in range(NF):
                    v = 4 * c + f
                    dve.wait_ge(s["f1_h"], v + 1)
                    dve.wait_ge(s["f1_ibs"], c + 1)
                    dve.tensor_tensor(hpad[:, v % 2, 1:C + 1], bank[f][:, :], ibs[:, c % 2, :], ALU.mult)\
                        .then_inc(s["f1_hd"], 1)
                    dve.wait_ge(s["f1_c0"], v + 1)
                    link(dve, "dve", dve.scalar_tensor_tensor(
                        yc[:, v % 2, :], hpad[:, v % 2, 0:C], cwm[:, 3 * f:3 * f + 1], yc[:, v % 2, :],
                        ALU.mult, ALU.add))
                    dve.scalar_tensor_tensor(yc[:, v % 2, :], hpad[:, v % 2, 2:C + 2], cwm[:, 3 * f + 2:3 * f + 3],
                                             yc[:, v % 2, :], ALU.mult, ALU.add).then_inc(s["f1_c2"], 1)

        def f1_act(act):
            act.wait_ge(s["f0w_ready"], 2)
            for c in range(NC_):
                act.wait_ge(s["f1_ib"], c + 1)
                act.activation(ibs[:, c % 2, :], bank[7][:, :], ACT.Copy).then_inc(s["f1_ibs"], 1)
                act.wait_ge(s["f1_qt"], c + 1)
                act.activation(lowp[:, 2 + c % 2, :], bank[6][:, :].bitcast(BF16)[:, 0:C], ACT.Copy)\
                    .then_inc(s["f1_xqt"], 1)

                def silu(v):
                    act.wait_ge(s["f1_c2"], v + 1)
                    act.activation(sil[v // 4][:, v % 4, :], yc[:, v % 2, :], ACT.Silu, bias=col("conv_b", v % 4))\
                        .then_inc(s["f1_silu"], 1)
                for f in range(NF):
                    v = 4 * c + f
                    act.wait_ge(s["f1_hd"], v + 1)
                    if v >= 2:
                        act.wait_ge(s["f1_silu"], v - 1)
                    act.activation(yc[:, v % 2, :], hpad[:, v % 2, 1:C + 1], ACT.Copy,
                                   scale=cwm[:, 3 * f + 1:3 * f + 2]).then_inc(s["f1_c0"], 1)
                    silu(v)

        def f2_pe(pe):
            def turn(v):
                c, t = v // 4, v % 4
                pe.wait_ge(s["f1_silu"], 4 * c + 4)
                if v >= 2:
                    pe.wait_ge(s["f2_q"], v - 1)
                for f in range(NF):
                    ins = pe.transpose(bank[4 + v % 2][:, f * P:(f + 1) * P], sil[c][:, f, t * P:(t + 1) * P],
                                       ident[:, :])
                ins.then_inc(s["f2_turned"], 1)

            def turn_q(v):
                pe.wait_ge(s["f2_q"], v + 1)
                if v >= 2:
                    pe.wait_ge(s["f2_hqt"], v - 1)
                for f in range(NF):
                    ins = pe.transpose(bank[6 + v % 2][:, :].bitcast(BF16)[:, f * P:(f + 1) * P],
                                       lowp[:, 4 + v % 2, f * P:(f + 1) * P], identb[:, :])
                ins.then_inc(s["f2_qt"], 1)

            def product(v):
                pe.wait_ge(s["f2_hqt"], v + 1)
                if v >= 2:
                    pe.wait_ge(s["f2_os"], v - 1)
                for f in range(NF):
                    ins = pe.matmul(bank[v % 2][:, 0:P], lowp[:, 6 + v % 2, f * P:(f + 1) * P],
                                    w2q[:, f * P:(f + 1) * P], start=(f == 0), stop=(f == NF - 1))
                ins.then_inc(s["f2_o"], 1)

            def back(v):
                c, t = v // 4, v % 4
                pe.wait_ge(s["f2_os"], v + 1)
                if t == 0 and c >= 2:
                    pe.wait_ge(s["f2_res"], c - 1)
                pe.transpose(bank[2 + c % 2][:, t * P:(t + 1) * P], os_[:, v % 2, :], ident[:, :])\
                    .then_inc(s["f2_ot"], 1)
            for v in range(NT + 3):
                if v < NT:
                    turn(v)
                if 1 <= v <= NT:
                    turn_q(v - 1)
                if 2 <= v <= NT + 1:
                    product(v - 2)
                if v >= 3:
                    back(v - 3)

        def f2_dve(dve):
            def residual(c):
                dve.wait_ge(s["f2_ot"], 4 * c + 4)
                dve.scalar_tensor_tensor(ch(x, c), bank[2 + c % 2][:, :], tg[:, 4:5], ch(x, c), ALU.mult, ALU.add)\
                    .then_inc(s["f2_res"], 1)
            for v in range(NT):
                dve.wait_ge(s["f2_turned"], v + 1)
                if v >= 2:
                    dve.wait_ge(s["f2_os"], v - 1)
                quantise(dve, bank[4 + v % 2][:, :], v % 2, 1, C, s["f2_am"], s["f2_q"], t32[:, v % 2, :],
                         lowp[:, 4 + v % 2, :])
                dve.wait_ge(s["f2_am"], v + 1)
                dve.tensor_scalar(qa[:, v % 2, 2, 0:1], qa[:, v % 2, 2, 0:1], wmean[:, 1:2], None, ALU.mult)\
                    .then_inc(s["f2_step"], 1)
                if v % 4 == 3 and v > 4:
                    residual(v // 4 - 1)
            residual(NC_ - 1)

        def f2_act(act):
            for v in range(NT):
                act.wait_ge(s["f2_qt"], v + 1)
                act.activation(lowp[:, 6 + v % 2, :], bank[6 + v % 2][:, :].bitcast(BF16)[:, 0:C], ACT.Copy)\
                    .then_inc(s["f2_hqt"], 1)
                act.wait_ge(s["f2_o"], v + 1)
                act.wait_ge(s["f2_step"], v + 1)
                if v >= 2:
                    act.wait_ge(s["f2_ot"], v - 1)
                act.activation(os_[:, v % 2, :], bank[v % 2][:, 0:P], ACT.Copy, scale=qa[:, v % 2, 2, 0:1])\
                    .then_inc(s["f2_os"], 1)

        def r_pool(pool):
            for c in range(NC_):
                pool.wait_ge(s["ln_norm"], 4 * 11 + c + 1)
                if c >= 2:
                    pool.wait_ge(s["r_up"], 2 * (c - 1))
                pool.tensor_scalar(mixr[:, c % 2, :], ch(a1, c), col("mu_r"), None, ALU.mult).then_inc(s["r_mix0"], 1)
                pool.tensor_scalar(mixk[:, c % 2, :], ch(a1, c), col("mu_k"), None, ALU.mult).then_inc(s["r_mix0"], 1)

        def r_dve(dve):
            def mix(c):
                for k, t in enumerate((mixr, mixk)):
                    dve.wait_ge(s["r_mix0"], 2 * c + k + 1)
                    dve.scalar_tensor_tensor(t[:, c % 2, 1:C], a1[:, c * C:(c + 1) * C - 1], omu[:, k:k + 1],
                                             t[:, c % 2, 1:C], ALU.mult, ALU.add).then_inc(s["r_mix"], 1)
            mix(0)
            for c in range(NC_):
                if c + 1 < NC_:
                    mix(c + 1)
                dve.wait_ge(s["r_up"], 2 * c + 2)
                link(dve, "dve", dve.tensor_scalar(kact[:, c % 2, :], bank[6 + c % 2][:, :], 0.0, None, ALU.max))
                dve.tensor_tensor(kact[:, c % 2, :], kact[:, c % 2, :], kact[:, c % 2, :], ALU.mult)\
                    .then_inc(s["r_act"], 1)
                dve.wait_ge(s["r_val"], c + 1)
                dve.wait_ge(s["r_gate"], c + 1)
                link(dve, "dve", dve.tensor_tensor(rv[:, c % 2, :], bank[c % 2][:, :], rg[:, c % 2, :], ALU.mult))
                dve.scalar_tensor_tensor(ch(x, c), rv[:, c % 2, :], tg[:, 6:7], ch(x, c), ALU.mult, ALU.add)\
                    .then_inc(s["r_out"], 1)

        def r_act(act):
            for c in range(NC_):
                act.wait_ge(s["r_up"], 2 * c + 1)
                if c >= 2:
                    act.wait_ge(s["r_out"], c - 1)
                act.activation(rg[:, c % 2, :], bank[4 + c % 2][:, :], ACT.Sigmoid).then_inc(s["r_gate"], 1)

        def r_pe(pe):
            pe.wait_ge(s["small_in"], 32)

            def up(c):
                pe.wait_ge(s["r_mix"], 2 * c + 2)
                if c >= 2:
                    pe.wait_ge(s["r_gate"], c - 1)
                    pe.wait_ge(s["r_act"], c - 1)
                pe.matmul(bank[4 + c % 2][:, :], wr[:, 0, :], mixr[:, c % 2, :], start=True, stop=True)\
                    .then_inc(s["r_up"], 1)
                pe.matmul(bank[6 + c % 2][:, :], wr[:, 1, :], mixk[:, c % 2, :], start=True, stop=True)\
                    .then_inc(s["r_up"], 1)
            up(0)
            for c in range(NC_):
                if c + 1 < NC_:
                    up(c + 1)
                pe.wait_ge(s["r_act"], c + 1)
                if c >= 2:
                    pe.wait_ge(s["r_out"], c - 1)
                pe.matmul(bank[c % 2][:, :], wr[:, 2, :], kact[:, c % 2, :], start=True, stop=True)\
                    .then_inc(s["r_val"], 1)

        te = lambda ap: ap.rearrange("p (t e) -> p t e", e=E)
        bc = lambda ap: ap.unsqueeze(2).to_broadcast([P, NT, E])
        LOGIT, PROB, TMP, MASK1, MASK2, PROB2, WT, POS1, POS2, SUM_A, SUM_B, TOT, WROW = range(13)

        def g_pe_logits(pe, k, n):
            pe.wait_ge(s["small_in"], 32)
            for t in range(NT):
                if t % TT == 0:
                    pe.wait_ge(s["ln_norm"], 4 * n + t // TT + 1)
                ins = pe.matmul(bank[6][:, t * E:(t + 1) * E], a1[:, t * P:(t + 1) * P], gate_w[:, k, :],
                                start=True, stop=True)
            ins.then_inc(s["g_logit"], 1)

        def g_act_exp(act, k):
            act.wait_ge(s["g_in"], k + 1)
            act.activation(gt[PROB], gt[LOGIT], ACT.Exp).then_inc(s["g_exp"], 1)

        def first_largest(dve, src, dst):
            L = lambda ins: link(dve, "dve", ins)
            L(dve.tensor_reduce(g16[:, 0, :], te(src), AX, ALU.max))
            L(dve.tensor_tensor(te(gt[TMP]), te(src), bc(g16[:, 0, :]), ALU.is_equal))
            L(dve.tensor_tensor(te(gt[TMP]), te(gt[TMP]), rank[:, :].unsqueeze(1).to_broadcast([P, NT, E]), ALU.mult))
            L(dve.tensor_reduce(g16[:, 0, :], te(gt[TMP]), AX, ALU.max))
            L(dve.tensor_tensor(te(dst), te(gt[TMP]), bc(g16[:, 0, :]), ALU.is_equal))

        def g_dve_top2(dve, k):
            L = lambda ins: link(dve, "dve", ins)
            dve.wait_ge(s["g_logit"], k + 1)
            L(dve.tensor_reduce(g16[:, 0, :], te(bank[6][:, 0:P]), AX, ALU.max))
            dve.tensor_tensor(te(gt[LOGIT]), te(bank[6][:, 0:P]), bc(g16[:, 0, :]), ALU.subtract)\
                .then_inc(s["g_in"], 1)
            dve.wait_ge(s["g_exp"], k + 1)
            L(dve.tensor_reduce(g16[:, 1, :], te(gt[PROB]), AX, ALU.add))
            L(dve.reciprocal(g16[:, 1, :], g16[:, 1, :]))
            L(dve.tensor_tensor(te(gt[PROB]), te(gt[PROB]), bc(g16[:, 1, :]), ALU.mult))
            first_largest(dve, gt[PROB], gt[MASK1])
            L(dve.tensor_tensor(gt[TMP], gt[PROB], gt[MASK1], ALU.mult))
            L(dve.tensor_tensor(gt[PROB2], gt[PROB], gt[TMP], ALU.subtract))
            first_largest(dve, gt[PROB2], gt[MASK2])

        def g_dve_weights(dve, second, floor):
            L = lambda ins: link(dve, "dve", ins)
            L(dve.tensor_tensor(gt[TMP], gt[PROB], gt[MASK1], ALU.mult))
            L(dve.tensor_tensor(gt[SUM_A], second, gt[MASK2], ALU.mult))
            L(dve.tensor_tensor(gt[TMP], gt[TMP], gt[SUM_A], ALU.add))
            L(dve.tensor_reduce(g16[:, 2, :], te(gt[TMP]), AX, ALU.add))
            if floor:
                L(dve.tensor_scalar(g16[:, 2, :], g16[:, 2, :], FLT_EPS, None, ALU.max))
            L(dve.reciprocal(g16[:, 2, :], g16[:, 2, :]))
            dve.tensor_tensor(gt[WT].rearrange("p (e t) -> p t e", e=E), te(gt[TMP]), bc(g16[:, 2, :]), ALU.mult)\
                .then_inc(s["g_row"], 1)

        def g_rows_pe(pe, k):
            pe.wait_ge(s["g_row"], k + 1)
            pe.transpose(bank[7][:, 0:P], gt[WT], ident[:, :]).then_inc(s["g_rowt"], 1)

        def g_rows_dve(dve, k):
            dve.wait_ge(s["g_rowt"], k + 1)
            dve.tensor_copy(gt[WROW], bank[7][:, 0:P]).then_inc(s["g_pre"], 1)

        def g_rows_sp(sp, k):
            sp.wait_ge(s["g_pre"], k + 1)
            sp.dma_start(d[f"wrow{k}"].rearrange("e (t p) -> (e t) p", p=P), gt[WROW]).then_inc(s["g_stored"], 16)
            sp.wait_ge(s["g_stored"], 16 * (k + 1))

        def cap_pe(pe):
            for r, mask in enumerate((MASK1, MASK2)):
                pe.wait_ge(s["g_cum"], 2 * r + 1)
                pe.matmul(bank[6][:, 0:P], before[:, :], gt[mask], start=True, stop=True)
                pe.matmul(bank[6][:, P:2 * P], ones_mat[:, :], gt[mask], start=True, stop=True)\
                    .then_inc(s["g_capmm"], 1)
            pe.wait_ge(s["g_cum"], 4)
            pe.matmul(bank[6][:, 0:P], ones_mat[:, :], gt[MASK1], start=True, stop=True).then_inc(s["g_capmm"], 1)

        def cap_dve(dve):
            L = lambda ins: link(dve, "dve", ins)

            def positions(r, pos):
                dve.wait_ge(s["g_capmm"], r + 1)
                L(dve.tensor_copy(gt[TOT], bank[6][:, P:2 * P]))
                L(dve.tensor_copy(gt[SUM_A], gt[TOT]))
                a, b = SUM_A, SUM_B
                k = 1
                while k < NT:
                    L(dve.tensor_copy(gt[b][:, 0:k * E], gt[a][:, 0:k * E]))
                    L(dve.tensor_tensor(gt[b][:, k * E:P], gt[a][:, k * E:P], gt[a][:, 0:P - k * E], ALU.add))
                    a, b = b, a
                    k *= 2
                L(dve.tensor_tensor(gt[a], gt[a], gt[TOT], ALU.subtract))
                dve.tensor_tensor(gt[pos], gt[a], bank[6][:, 0:P], ALU.add).then_inc(s["g_cum"], 1)
            L(dve.tensor_copy(gt[TMP], gt[MASK1]))
            dve.tensor_copy(gt[TOT], gt[TMP]).then_inc(s["g_cum"], 1)
            positions(0, POS1)
            dve.wait_ge(s["g_cum"], 2)
            L(dve.tensor_scalar(gt[POS1], gt[POS1], float(CAP), None, ALU.is_lt))
            dve.tensor_tensor(gt[MASK1], gt[MASK1], gt[POS1], ALU.mult).then_inc(s["g_cum"], 1)
            positions(1, POS2)
            dve.wait_ge(s["g_capmm"], 3)
            L(dve.tensor_reduce(g16[:, 3, 0:E], bank[6][:, 0:P].rearrange("p (t e) -> p e t", e=E), AX, ALU.add))
            L(dve.tensor_tensor(te(gt[POS2]), te(gt[POS2]), g16[:, 3, 0:E].unsqueeze(1).to_broadcast([P, NT, E]),
                                ALU.add))
            L(dve.tensor_scalar(gt[POS2], gt[POS2], float(CAP), None, ALU.is_lt))
            L(dve.tensor_tensor(gt[MASK2], gt[MASK2], gt[POS2], ALU.mult))

        MCR = 32

        def moe_sp(sp, k, u0):
            width = EXP_COLS["moe" + k[1]]
            row = d["wrow0" if k == "m1" else "wrow1"]
            with sp.Fori(0, E // 2) as j:
                for a in range(2):
                    sp.wait_ge(s[k + "_t"], j * 8 + (u0 + 16 * (a - 1)) // 4 + CR)
                    sp.dma_start(ew[:, a, 0:width], d["moe" + k[1]][bass.ds(j * (2 * P) + a * P, P), :])\
                        .then_inc(s[f"{k}_w{a}"], 16)
                    sp.dma_start(wb[:, a, :], row[bass.ds(j * 2 + a, 1), :].to_broadcast([P, N]))\
                        .then_inc(s[f"{k}_w{a}"], 16)

        def moe_pe(pe, k, a, base, tbase):
            def up(u):
                c, f = u // NF, u % NF
                pe.wait_ge(s[k + "_h"], base + u - 1 + MCR)
                if k == "m1":
                    for m in range(2):
                        ins = pe.matmul(bank[2 * (u % 2) + m][:, :], ew[:, a, (4 * m + f) * P:(4 * m + f + 1) * P],
                                        ch(a1, c), start=True, stop=True)
                else:
                    ins = pe.matmul(bank[u % 2][:, :], ew[:, a, f * P:(f + 1) * P], ch(a1, c), start=True, stop=True)
                ins.then_inc(s[k + "_up"], 1)

            def down(u):
                c, f = u // NF, u % NF
                pe.wait_ge(s[k + "_h"], base + u + 1 + MCR)
                if f == 0:
                    pe.wait_ge(s[k + "_t"], tbase + c - 1 + CR)
                w2 = 8 * P if k == "m1" else 4 * P
                pe.matmul(bank[4 + c % 2][:, :], ew[:, a, w2 + f * P:w2 + (f + 1) * P], hring[:, u % 4, :],
                          start=(f == 0), stop=(f == NF - 1)).then_inc(s[k + "_down"], 1)
            up(0)
            for u in range(16):
                if u + 1 < 16:
                    up(u + 1)
                down(u)

        def moe_act(act, k, a, base):
            for u in range(16):
                act.wait_ge(s[k + "_up"], base + u + 1)
                if k == "m1":
                    act.activation(esil[:, u % 2, :], bank[2 * (u % 2)][:, :], ACT.Silu).then_inc(s["m1_sil"], 1)
                else:
                    b1 = ew[:, a, 8 * P + u % 4:8 * P + u % 4 + 1]
                    act.activation(hring[:, u % 4, :], bank[u % 2][:, :], ACT.Silu, bias=b1)\
                        .then_inc(s["m3_h"], 1)

        def moe_dve(dve, k, a, base, tbase):
            def scaled(c):
                dve.wait_ge(s[k + "_down"], base + 4 * c + 4)
                dve.wait_ge(s[k + "_acc"], tbase + c - 1 + CR)
                w = wb[:, a, c * C:(c + 1) * C]
                if k == "m1":
                    ins = dve.tensor_tensor(yt[:, c % 2, :], bank[4 + c % 2][:, :], w, ALU.mult)
                else:
                    ins = dve.scalar_tensor_tensor(yt[:, c % 2, :], bank[4 + c % 2][:, :],
                                                   ew[:, a, 8 * P + 4:8 * P + 5], w, ALU.add, ALU.mult)
                ins.then_inc(s[k + "_t"], 1)
            if k == "m3":
                for c in range(NC_):
                    scaled(c)
                return
            for u in range(16):
                dve.wait_ge(s["m1_sil"], base + u + 1)
                dve.tensor_tensor(hring[:, u % 4, :], esil[:, u % 2, :], bank[2 * (u % 2) + 1][:, :], ALU.mult)\
                    .then_inc(s["m1_h"], 1)
                if u % 4 == 1 and u > 4:
                    scaled(u // 4 - 1)
            scaled(3)

        def moe_pool(pool, k, tbase):
            for c in range(NC_):
                pool.wait_ge(s[k + "_t"], tbase + c + 1 + CR)
                pool.wait_ge(s[k + "_acc"], tbase + c - 3 + CR)
                pool.tensor_tensor(ch(a4, c), ch(a4, c), yt[:, c % 2, :], ALU.add).then_inc(s[k + "_acc"], 1)

        def clear_acc(pool, k):
            for c in range(NC_):
                ins = pool.memset(ch(a4, c), 0.0)
            link(pool, "pool", ins)

        def moe_res_dve(dve, k, gate, chunks, out):
            for c in range(NC_):
                dve.wait_ge(s[k + "_acc"], chunks - 3 + c + CR)
                dve.scalar_tensor_tensor(ch(x, c), ch(a4, c), tg[:, gate:gate + 1], ch(x, c), ALU.mult, ALU.add)\
                    .then_inc(s[out], 1)

        CREDIT += [("m1_t", CR), ("m3_t", CR), ("m1_h", MCR), ("m3_h", MCR), ("m1_acc", CR), ("m3_acc", CR)]

        ld_x = lambda c: [(s["ld_x"], 64)]
        norm_of = lambda n: (lambda c: [(s["ln_norm"], 4 * n + c + 1)])
        aff_of = lambda n, j: (lambda c: [(s["ln_aff"], aff_at(n, c, j))])
        r1_of = lambda c: [(s["prep_dve"], PREP + JOBS * B)]
        res_of = lambda l: (lambda c: [(s["ca_res"], 4 * l + c + 1)])
        out1_of = lambda c: [(s["mlp_out"], c + 1)]
        out2_of = lambda c: [(s["mlp_out"], 4 + 2 * c + 2)]
        f2_of = lambda c: [(s["f2_res"], c + 1)]
        m1_of = lambda c: [(s["m1_out"], c + 1)]
        r_of = lambda c: [(s["r_out"], c + 1)]
        AFF = {1: [(a1, "ln1_g", "ln1_b")],
               2: [(a3, "a1_lny_g", "a1_lny_b"), (a2, "a1_lnx_g", "a1_lnx_b")],
               3: [(a2, "a1_ln3_g", "a1_ln3_b")],
               4: [(a1, "ln2_g", "ln2_b")],
               5: [(a2, "a2_lnx_g", "a2_lnx_b")],
               6: [(a2, "a2_ln3_g", "a2_ln3_b")]}

        block = ctx.enter_context(nc.Block())

        @block.sync
        def _(sp):
            setup_sp(sp)
            sa_sp(sp)
            mlp_sp(sp, 0)
            cx_sp(sp, 0)
            mlp_sp(sp, 1)
            f0w_sp(sp)
            cx_sp(sp, 1)
            cx_sp(sp, 2)
            g_rows_sp(sp, 0)
            moe_sp(sp, "m1", 0)
            cx_sp(sp, 3)
            sp.wait_ge(s["ca_res"], 4 * B)
            sp.dma_start(ew[:, 1, 0:EXP_COLS["moe3"]], d["shared"]).then_inc(s["m3_wsh"], 16)
            g_rows_sp(sp, 1)
            moe_sp(sp, "m3", 16)
            for c in range(NC_):
                sp.wait_ge(s["x_out"], c + 1)
                sp.dma_start(d["out"][:, c * C:(c + 1) * C], ch(x, c)).then_inc(s["stored"], 16)
            sp.wait_ge(s["stored"], 16 * NC_)

        @block.gpsimd
        def _(pool):
            setup_pool(pool)
            pool.wait_ge(s["ld_cols"], 16)
            r1_init_pool(pool)
            sa_pool(pool)
            ca_pool(pool, 0)
            ca_pool(pool, 1)
            clear_acc(pool, "m1")
            with pool.Fori(0, E * 4, 4) as t:
                moe_pool(pool, "m1", t)
            ca_pool(pool, 2)
            r_pool(pool)
            ca_pool(pool, 3)
            pool.wait_ge(s["ca_res"], 4 * B)
            pool.memset(wb[:, 1, :], 0.1).then_inc(s["sh_weight"], 1)
            clear_acc(pool, "m3")
            moe_pool(pool, "m3", 0)
            with pool.Fori(4, 4 + E * 4, 4) as t:
                moe_pool(pool, "m3", t)

        @block.scalar
        def _(act):
            setup_act(act)
            act.wait_ge(s["const_ready"], N_CONST)
            ln_act(act, 0, a1)
            ln_act(act, 1, a2, AFF[1])
            ln_act(act, 2, a2, AFF[2])
            sa_act(act)
            ln_act(act, 3, a2, AFF[3])
            mlp_act(act, 0)
            cln_act(act)
            cx_act(act, 0)
            ln_act(act, 4, a2, AFF[4])
            ln_act(act, 5, a2, AFF[5])
            ca_act(act, 0)
            ln_act(act, 6, a2, AFF[6])
            mlp_act(act, 1)
            ln_act(act, 7, a1)
            f1_act(act)
            f2_act(act)
            cx_act(act, 1)
            ln_act(act, 8, a1)
            ca_act(act, 1)
            ln_act(act, 9, a1)
            g_act_exp(act, 0)
            with act.Fori(0, E * 16, 32) as u:
                for a in range(2):
                    moe_act(act, "m1", a, u + 16 * a)
            cx_act(act, 2)
            ln_act(act, 10, a1)
            ca_act(act, 2)
            ln_act(act, 11, a1)
            r_act(act)
            cx_act(act, 3)
            ln_act(act, 12, a1)
            ca_act(act, 3)
            ln_act(act, 13, a1)
            g_act_exp(act, 1)
            moe_act(act, "m3", 1, 0)
            with act.Fori(16, 16 + E * 16, 32) as u:
                for a in range(2):
                    moe_act(act, "m3", a, u + 16 * a)

        @block.vector
        def _(dve):
            setup_dve(dve)
            sa_sel_dve(dve)
            ln_dve(dve, 0, x, a1)
            ln_dve(dve, 1, a1, a2)
            ln_dve(dve, 2, a1, a2)
            sa_dve(dve)
            ln_dve(dve, 3, a4, a2)
            mlp_dve(dve, 0)
            cln_dve(dve)
            cx_dve(dve, 0)
            ln_dve(dve, 4, a1, a2)
            ln_dve(dve, 5, a1, a2)
            ca_dve(dve, 0, a1, a4)
            ln_dve(dve, 6, a4, a2)
            mlp_dve(dve, 1)
            f0w_dve(dve)
            ln_dve(dve, 7, x, a1)
            f1_dve(dve)
            f2_dve(dve)
            cx_dve(dve, 1)
            ln_dve(dve, 8, x, a1)
            ca_dve(dve, 1, x, x)
            ln_dve(dve, 9, x, a1)
            g_dve_top2(dve, 0)
            g_dve_weights(dve, gt[PROB2], False)
            g_rows_dve(dve, 0)
            with dve.Fori(0, E // 2) as j:
                for a in range(2):
                    moe_dve(dve, "m1", a, j * 32 + 16 * a, j * 8 + 4 * a)
            moe_res_dve(dve, "m1", 5, 4 * E, "m1_out")
            cx_dve(dve, 2)
            ln_dve(dve, 10, x, a1)
            ca_dve(dve, 2, x, x)
            ln_dve(dve, 11, x, a1)
            r_dve(dve)
            cx_dve(dve, 3)
            ln_dve(dve, 12, x, a1)
            ca_dve(dve, 3, x, x)
            ln_dve(dve, 13, x, a1)
            g_dve_top2(dve, 1)
            cap_dve(dve)
            g_dve_weights(dve, gt[PROB], True)
            g_rows_dve(dve, 1)
            dve.wait_ge(s["sh_weight"], 1)
            moe_dve(dve, "m3", 1, 0, 0)
            with dve.Fori(0, E // 2) as j:
                for a in range(2):
                    moe_dve(dve, "m3", a, j * 32 + 16 + 16 * a, j * 8 + 4 + 4 * a)
            moe_res_dve(dve, "m3", 7, 4 * E + 4, "x_out")

        @block.tensor
        def _(pe):
            pe.wait_ge(s["const_ready"], N_CONST)
            ln_pe(pe, 0, x, ld_x)
            ln_pe(pe, 1, a1, norm_of(0))
            ln_pe(pe, 2, a1, aff_of(1, 0))
            pe.wait_ge(s["ln_aff"], aff_at(2, 3, 1))
            sa_pe(pe)
            ln_pe(pe, 3, a4, r1_of)
            mlp_pe(pe, 0, 3)
            cln_pe(pe)
            pe.wait_ge(s["cx_ln_act"], 3)
            cx_pe(pe, 0)
            ln_pe(pe, 4, a1, out1_of)
            ln_pe(pe, 5, a1, aff_of(4, 0))
            ca_pe(pe, 0, a2, aff_of(5, 0))
            ln_pe(pe, 6, a4, res_of(0))
            mlp_pe(pe, 1, 6)
            f0w_pe(pe)
            ln_pe(pe, 7, x, out2_of)
            f1_pe(pe)
            f2_pe(pe)
            cx_pe(pe, 1, [(s["f2_q"], NT), (s["f2_hqt"], NT)])
            ln_pe(pe, 8, x, f2_of)
            ca_pe(pe, 1, a1, norm_of(8))
            ln_pe(pe, 9, x, res_of(1))
            g_pe_logits(pe, 0, 9)
            g_rows_pe(pe, 0)
            with pe.Fori(0, E // 2) as j:
                for a in range(2):
                    pe.wait_ge(s[f"m1_w{a}"], j * 32 + 32)
                    moe_pe(pe, "m1", a, j * 32 + 16 * a, j * 8 + 4 * a)
            cx_pe(pe, 2, [(s["m1_t"], 4 * E + CR)])
            ln_pe(pe, 10, x, m1_of)
            ca_pe(pe, 2, a1, norm_of(10))
            ln_pe(pe, 11, x, res_of(2))
            r_pe(pe)
            cx_pe(pe, 3, [(s["r_out"], NC_)])
            ln_pe(pe, 12, x, r_of)
            ca_pe(pe, 3, a1, norm_of(12))
            ln_pe(pe, 13, x, res_of(3))
            g_pe_logits(pe, 1, 13)
            cap_pe(pe)
            g_rows_pe(pe, 1)
            pe.wait_ge(s["m3_wsh"], 16)
            moe_pe(pe, "m3", 1, 0, 0)
            with pe.Fori(0, E // 2) as j:
                for a in range(2):
                    pe.wait_ge(s[f"m3_w{a}"], j * 32 + 32)
                    moe_pe(pe, "m3", a, j * 32 + 16 + 16 * a, j * 8 + 4 + 4 * a)


def kernel(**inputs):
    import numpy as np
    import concourse.bacc as bacc
    from concourse.bass_utils import run_bass_kernel_spmd as run

    i = {k: np.asarray(v) for k, v in inputs.items()}

    def blocks(w):
        n = w.shape[0] // P
        return w.reshape(n, P, w.shape[1]).transpose(1, 0, 2).reshape(P, n * w.shape[1])

    def heads(w):
        return w.transpose(1, 0, 2).reshape(w.shape[1], -1)

    packed = np.zeros((P, NCOLS), np.float32)

    def put(name, v):
        at, n = COLS[name]
        v = v.reshape(n, -1).T
        packed[0:v.shape[0], at:at + n] = v
    packed[:, 0:4] = i["g_xattn"][None, :]
    packed[:, 4:8] = i["g_ffn"][None, :]
    for name in COLS:
        if name[:3] in ("ln1", "ln2", "a1_", "a2_"):
            put(name, i["L0_xattn_" + name])
    at = COLS["conv_w"][0]
    packed[:, at:at + 12] = i["L0_ffn_conv_w"].reshape(NF, P, 3).transpose(1, 0, 2).reshape(P, 12)
    put("conv_b", i["L0_ffn_conv_b"])
    put("bo2", i["L2_xattn_bo"])
    put("mu_r", i["L2_ffn_mu_r"])
    put("mu_k", i["L2_ffn_mu_k"])
    for name in ("bq", "bk", "bv", "bo"):
        put(name + "3", i["L3_xattn_" + name])
    put("sb1", i["L3_ffn_sb1"])
    put("sb2", i["L3_ffn_sb2"])

    arrays = {
        "x": i["x"].reshape(N, P).T,
        "cols": packed,
        "ctx": i["ctx_512"].reshape(B * M, CD).T,
    }
    hq, hk, hv = (heads(i["L0_xattn_a1_" + n]) for n in ("wq", "wk", "wv"))
    arrays["w_qkv"] = np.concatenate([w[:, g * P:(g + 1) * P] for g in range(4) for w in (hq, hk, hv)], 1)
    arrays["w_li1"] = blocks(i["L0_xattn_a1_li1_w"])
    for a in ("a1", "a2"):
        arrays[a + "_li2"] = i[f"L0_xattn_{a}_li2_w"]
        arrays[a + "_li3"] = blocks(i[f"L0_xattn_{a}_li3_w"])
    q = [heads(i["L0_xattn_a2_wq"]), i["L1_xattn_Wq"].T, i["L2_xattn_Wq"], i["L3_xattn_Wq"]]
    k = [heads(i["L0_xattn_a2_wk"]), i["L1_xattn_Wkv"][0:P].T, i["L2_xattn_Wk"], i["L3_xattn_Wk"]]
    v = [heads(i["L0_xattn_a2_wv"]), i["L1_xattn_Wkv"][P:2 * P].T, i["L2_xattn_Wv"], i["L3_xattn_Wv"]]
    o = [i["L0_xattn_a2_li1_w"], i["L1_xattn_Wo"].T, i["L2_xattn_Wo"], i["L3_xattn_Wo"]]
    for l in range(4):
        arrays[f"c{l}_q"] = blocks(q[l].T)
        arrays[f"c{l}_k"] = k[l]
        arrays[f"c{l}_v"] = v[l]
        arrays[f"c{l}_o"] = blocks(o[l])
    arrays["f0_w1"] = i["L0_ffn_w1"].T
    arrays["f0_w2"] = blocks(i["L0_ffn_w2"].T)
    arrays["f2_w"] = np.concatenate([i["L2_ffn_" + n].T for n in ("W_r", "W_k", "W_v")], 1)
    arrays["gates"] = np.concatenate([i["L1_ffn_gate_w"], i["L3_ffn_router_w"]], 1)
    arrays["moe1"] = np.concatenate([
        np.concatenate([i["L1_ffn_w1"][e], i["L1_ffn_w3"][e], blocks(i["L1_ffn_w2"][e])], 1) for e in range(E)], 0)
    arrays["moe3"] = np.concatenate([
        np.concatenate([i["L3_ffn_w1"][e], blocks(i["L3_ffn_w2"][e]), i["L3_ffn_b1"][e].reshape(NF, P).T,
                        i["L3_ffn_b2"][e][:, None]], 1) for e in range(E)], 0)
    arrays["shared"] = np.concatenate([i["L3_ffn_sw1"], blocks(i["L3_ffn_sw2"]), i["L3_ffn_sb1"].reshape(NF, P).T,
                                       i["L3_ffn_sb2"][:, None]], 1)
    arrays = {n: np.ascontiguousarray(a) for n, a in arrays.items()}

    nc = bacc.Bacc("TRN2", target_bir_lowering=False, num_devices=1)
    d = {n: nc.dram_tensor("in_" + n, a.shape, F32, kind="ExternalInput").ap() for n, a in arrays.items()}
    for n in ("wrow0", "wrow1"):
        d[n] = nc.dram_tensor(n, (E, N), F32, kind="Internal").ap()
    d["out"] = nc.dram_tensor("out_x", (P, N), F32, kind="ExternalOutput").ap()
    build(nc, d)
    r = run(nc, [{"in_" + n: a for n, a in arrays.items()}], core_ids=[0])
    return np.ascontiguousarray(r.results[0]["out_x"].T.reshape(B, S, P))
```

```python
from contextlib import ExitStack

import concourse.bass as bass
from concourse import mybir

ALU = mybir.AluOpType
ACT = mybir.ActivationFunctionType
F32 = mybir.dt.float32
BF16 = mybir.dt.bfloat16
F32R = mybir.dt.float32r
AX = mybir.AxisListType.X

P = 128
B, S, M = 4, 512, 32
N = B * S
C = 512
NC_ = N // C
TT = C // P
H = 16
CD = 64
F = 512
NF = F // P
E = 8
NT = N // P
CAP = min(max(4, -(-2 * 5 * N // (4 * E))), N)
MAGIC = 12582912.0
LN_EPS = 1e-5
FLT_EPS = 1.1920929e-07

COLS = {}
for _name, _n in [
    ("gx", 4), ("gf", 4), ("ln1_g", 1), ("ln1_b", 1), ("ln2_g", 1), ("ln2_b", 1),
    ("a1_lnx_g", 1), ("a1_lnx_b", 1), ("a1_lny_g", 1), ("a1_lny_b", 1), ("a1_ln3_g", 1), ("a1_ln3_b", 1),
    ("a1_li1_b", 1), ("a1_li2_b", 4), ("a1_li3_b", 1),
    ("a2_lnx_g", 1), ("a2_lnx_b", 1), ("a2_lny_g", 1), ("a2_lny_b", 1), ("a2_ln3_g", 1), ("a2_ln3_b", 1),
    ("a2_li1_b", 1), ("a2_li2_b", 4), ("a2_li3_b", 1),
    ("conv_w", 12), ("conv_b", 4), ("bo2", 1), ("mu_r", 1), ("mu_k", 1),
    ("bq3", 1), ("bk3", 1), ("bv3", 1), ("bo3", 1), ("sb1", 4), ("sb2", 1),
]:
    COLS[_name] = (sum(n for _, n in COLS.values()), _n)
NCOLS = sum(n for _, n in COLS.values())

CROSS = [
    dict(nch=4, scale=32.0 ** -0.5, gate=None, bias="a2_li1_b"),
    dict(nch=1, scale=8.0 ** -0.5, gate=1, bias=None),
    dict(nch=8, scale=64.0 ** -0.5, gate=2, bias="bo2"),
    dict(nch=1, scale=8.0 ** -0.5, gate=3, bias="bo3"),
]
LN_AFF = [0, 1, 2, 1, 1, 1, 1, 0, 0, 0, 0, 0, 0, 0]
EXP_COLS = {"moe1": 12 * P, "moe3": 8 * P + 5}


def build(nc, d):
    ctx = ExitStack()
    with ctx:
        def sb(name, shape, dt=F32):
            return ctx.enter_context(nc.sbuf_tensor(name, shape, dt))

        def sem(name):
            return ctx.enter_context(nc.semaphore(name))

        bank = [ctx.enter_context(nc.psum_tensor(f"bank{i}", [P, C], F32)) for i in range(8)]

        x = sb("x", [P, N])
        a1 = sb("a1", [P, N])
        a234 = sb("a234", [P, 3 * N])
        a2, a3, a4 = (a234[:, k * N:(k + 1) * N] for k in range(3))
        arena = sb("arena", [P, 8192])
        arena_r = sb("arena_r", [P, 13312], F32R)
        cols = sb("cols", [P, NCOLS])
        tg = sb("tg", [P, 8])
        gbo = sb("gbo", [P, 4])
        ident = sb("ident", [P, P])
        identb = sb("identb", [P, P], BF16)
        mean_mat = sb("mean_mat", [P, P])
        ones_mat = sb("ones_mat", [P, P])
        mean64 = sb("mean64", [CD, CD])
        before = sb("before", [P, P])
        eps = sb("eps", [P, 1])
        credit = sb("credit", [P, 32])
        warm = sb("warm", [P, 1])
        masks = {1: sb("mask8", [P, 16]), 4: sb("mask32", [P, 4]), 8: sb("mask64", [P, 2])}
        rank = sb("rank", [P, E])

        def col(name, j=0):
            return cols[:, COLS[name][0] + j:COLS[name][0] + j + 1]

        def ch(t, c):
            return t[:, c * C:(c + 1) * C]

        ln_sqr = sb("ln_sqr", [P, 2, C])
        ln_rs = sb("ln_rs", [P, NC_, TT])
        w_qkv = sb("w_qkv", [P, 4, 3, P])
        w_li1 = sb("w_li1", [P, 4, P])
        pbuf = sb("pbuf", [P, 2, 4, C])

        q_st = arena_r[:, 0:8 * C].rearrange("p (a h s) -> p a h s", a=2, h=4)
        k_st = arena_r[:, 8 * C:16 * C].rearrange("p (a h s) -> p a h s", a=2, h=4)
        parts = arena_r[:, 16 * C:20 * C].rearrange("p (k h s) -> p k h s", k=2, h=2)
        sel = arena_r[:, 20 * C:21 * C].rearrange("p (k m) -> p k m", k=4)
        ptb = arena[:, 0:8 * C].rearrange("p (a h k s) -> p a h k s", a=2, h=4, k=TT)
        qt = arena[:, 8 * C:9 * C]
        kt = arena[:, 9 * C:10 * C]
        vt = arena[:, 10 * C:11 * C]
        vs = arena[:, 11 * C:13 * C].rearrange("p (a t m) -> p a t m", a=2, t=TT)
        nmx = sb("nmx", [P, 64])
        rsum = sb("rsum", [P, 2, TT, 4])
        rcol = sb("rcol", [P, 16])
        rinv = arena[:, 13 * C:14 * C].rearrange("p (t m) -> p t m", t=TT)
        rbs = arena[:, 14 * C:15 * C]
        osb = arena[:, 15 * C:16 * C]
        w_li2 = sb("w_li2", [P, F])
        w_li3 = sb("w_li3", [P, NF, P])
        hid = pbuf

        def hid_t(k):
            return hid[:, 0, k, :]
        ctx_t = sb("ctx_t", [CD, P])
        ctx_n = sb("ctx_n", [CD, P])
        cln = sb("cln", [CD, 3, P])
        cwq = sb("cwq", [P, 1024])
        cwk = sb("cwk", [CD, 1024])
        cwv = sb("cwv", [CD, 1024])
        cwo = sb("cwo", [P, 1024])
        qk = sb("qk", [P, B, C])
        vw = a3
        qb = arena[0:1, 4608:4608 + 4 * C].rearrange("p (b s) -> p b s", b=B)
        kbd = arena[:, 0:2048]
        vbd = arena[:, 2048:4096]
        kts = arena[:, 4096:4096 + 2 * P].rearrange("p (a t) -> p a t", a=2)
        e_ = arena[:, 0:2048].rearrange("p (a s) -> p a s", a=4)
        pn = arena[:, 2048:3072].rearrange("p (a s) -> p a s", a=2)
        ptc = pbuf
        cmx = sb("cmx", [P, 2, H])
        csum = sb("csum", [P, 2, H])
        crin = sb("crin", [P, 4, H])

        f0w1 = arena[:, 6656:6656 + F]
        f0w2 = arena[:, 6656 + F:6656 + 2 * F]
        f0tmp = arena[:, 6656 + 2 * F:6656 + 3 * F]
        w1q = sb("w1q", [P, F], BF16)
        w2q = sb("w2q", [P, F], BF16)
        cwm = sb("cwm", [P, 12])
        wmean = sb("wmean", [P, 2])
        wsc = sb("wsc", [P, 2])
        wabs = sb("wabs", [P, 2])
        sil = [t.rearrange("p (f s) -> p f s", f=NF) for t in
               (a2, a3, a4, qk[:, :, :].rearrange("p b s -> p (b s)"))]
        t32 = arena[:, 2056:3080].rearrange("p (a s) -> p a s", a=2)
        hpad = arena[:, 0:4 * (C + 2)].rearrange("p (a s) -> p a s", a=4)
        yc = arena[:, 3080:5128].rearrange("p (a s) -> p a s", a=4)
        ibs = arena[:, 5128:6152].rearrange("p (a s) -> p a s", a=2)
        right = arena[:, 6152:6152 + 2 * C].rearrange("p (a s) -> p a s", a=2)
        f2t = right
        lowp = pbuf[:, :, :, :].rearrange("p a k s -> p (a k s)").bitcast(BF16).rearrange("p (k s) -> p k s", s=C)
        qa = sb("qa", [P, 2, 3, 4])
        wr = sb("wr", [P, 3, P])
        omu = sb("omu", [P, 2])
        mixr = arena[:, 0:1024].rearrange("p (a s) -> p a s", a=2)
        mixk = arena[:, 1024:2048].rearrange("p (a s) -> p a s", a=2)
        rg = arena[:, 2048:3072].rearrange("p (a s) -> p a s", a=2)
        kact = arena[:, 3072:4096].rearrange("p (a s) -> p a s", a=2)
        rv = arena[:, 4096:5120].rearrange("p (a s) -> p a s", a=2)
        gate_w = sb("gate_w", [P, 2, E])
        ew = arena[:, 0:3072].rearrange("p (a w) -> p a w", a=2)
        wb = a234[:, 0:2 * N].rearrange("p (a n) -> p a n", a=2)
        hring = pbuf[:, 0, :, :].rearrange("p k s -> p (k s)").rearrange("p (k s) -> p k s", k=4)
        ewr = {k: arena_r[:, 0:4 * w].rearrange("p (a k w) -> p a k w", a=2, k=2)
               for k, w in (("m1", 12 * P), ("m3", 8 * P))}
        xp = arena_r[:, 6144:10240].rearrange("p (k n) -> p k n", k=2)
        hp = [arena_r[:, at_:at_ + 2 * C].rearrange("p (k s) -> p k s", k=2) for at_ in (10240, 11264, 12288, 4096)]
        esil = arena[:, 3072:4096].rearrange("p (k s) -> p k s", k=2)
        yt = arena[:, 7040:8064].rearrange("p (k s) -> p k s", k=2)
        gt = [arena[:, 5120 + k * P:5120 + (k + 1) * P] for k in range(14)]
        g16 = arena[:, 6912:6912 + 8 * NT].rearrange("p (k t) -> p k t", k=8)

        s = {}

        def sg(name):
            if name not in s:
                s[name] = sem(name)
            return s[name]

        for name in (
            "ld_x0 ld_x1 ld_x2 ld_x3 ld_cols ld_ctx const_ready gates_ready "
            "ln_mean ln_cent ln_sq ln_var ln_std ln_rinv ln_spread ln_norm ln_aff "
            "w_qkv_in sel_ready prep_mm_act prep_mm_dve prep_act prep_dve q_split k_split sc_ready max_ready exp_ready "
            "masked turned ev_dve ev_act av_done rcol_ready rinv_ready o_ready r1_init "
            "mlp_w_in mlp_up mlp_gelu mlp_down mlp_res mlp_out dve_link act_link pool_link "
            "cw_in cx_proj cx_kts cx_bd cx_fold cx_folded cx_ln_mm cx_ln_dve cx_ln_act cx_bias cx_bias_row "
            "ca_score ca_max ca_sub ca_exp ca_sum ca_rinv ca_prob ca_turned ca_pt ca_av ca_res "
            "small_in f0w_in f0w_mean f0w_ready f1_turned f1_am f1_q f1_qt f1_ib f1_ibs f1_xqt f1_h f1_hd f1_c0 f1_right f1_c1 f1_c2 "
            "f1_silu f2_turned f2_am f2_step f2_q f2_qt f2_hqt f2_o f2_scaled f2_round f2_ibs f2_res0 f2_res "
            "xp_split m1_ws m3_ws m1_hh m3_hh m1_hl m3_hl m1_b0 m1_b1 m3_b0 m3_b1 "
            "m1_w0 m1_w1 m1_up m1_sil m1_h m1_down m1_t m1_acc m3_w0 m3_w1 m3_wsh m3_up m3_h m3_down m3_t m3_acc "
            "g_logit g_exp g_in g_pre g_cum g_row g_rowt g_stored "
            "r_mix0 r_mix r_up r_gate r_act r_val r_out x_out m1_out sh_weight stored g_capmm "
        ).split():
            sg(name)

        LN_PRE = [4 * sum(LN_AFF[:n]) for n in range(len(LN_AFF) + 1)]

        def aff_at(n, c, j):
            return LN_PRE[n] + c * LN_AFF[n] + j + 1

        def ln_pe(pe, n, src, ready):
            for c in range(NC_):
                for sm, v in ready(c):
                    pe.wait_ge(sm, v)
                if c >= 2:
                    pe.wait_ge(s["ln_cent"], 4 * n + c - 1)
                pe.matmul(bank[c % 2][:, :], mean_mat[:, :], ch(src, c), start=True, stop=True)\
                    .then_inc(s["ln_mean"], 1)

            def variance(c):
                pe.wait_ge(s["ln_sq"], 4 * n + c + 1)
                if c < 2:
                    pe.wait_ge(s["ln_cent"], 4 * n + c + 3)
                else:
                    pe.wait_ge(s["ln_std"], 4 * n + c - 1)
                for t in range(TT):
                    ins = pe.matmul(bank[c % 2][:, t:t + 1], ln_sqr[:, c % 2, t * P:(t + 1) * P], mean_mat[:, 0:1],
                                    start=True, stop=True)
                ins.then_inc(s["ln_var"], 1)

            def spread(c):
                pe.wait_ge(s["ln_rinv"], 4 * n + c + 1)
                if c >= 2:
                    pe.wait_ge(s["ln_norm"], 4 * n + c - 1)
                for t in range(TT):
                    ins = pe.matmul(bank[2 + c % 2][:, t * P:(t + 1) * P],
                                    ln_rs[:, c, t:t + 1].to_broadcast([P, P]), ident[:, :], start=True, stop=True)
                ins.then_inc(s["ln_spread"], 1)
            if n == 0:
                pe.wait_ge(s["const_ready"], N_CONST)
            variance(0)
            for c in range(1, NC_):
                variance(c)
                spread(c - 1)
            spread(NC_ - 1)

        def ln_dve(dve, n, src, dst):
            for c in range(NC_):
                dve.wait_ge(s["ln_mean"], 4 * n + c + 1)
                dve.tensor_tensor(ch(dst, c), ch(src, c), bank[c % 2][:, :], ALU.subtract)\
                    .then_inc(s["ln_cent"], 1)

            def inverse(c):
                dve.wait_ge(s["ln_std"], 4 * n + c + 1)
                dve.reciprocal(ln_rs[:, c, :], ln_rs[:, c, :]).then_inc(s["ln_rinv"], 1)

            inverse(0)
            for c in range(NC_):
                if c + 1 < NC_:
                    inverse(c + 1)
                dve.wait_ge(s["ln_spread"], 4 * n + c + 1)
                dve.tensor_tensor(ch(dst, c), ch(dst, c), bank[2 + c % 2][:, :], ALU.mult)\
                    .then_inc(s["ln_norm"], 1)

        def ln_act(act, n, dst, affine=()):
            act.activation(warm[:, 0:1], eps[:, 0:1], ACT.Sqrt)
            for c in range(NC_):
                act.wait_ge(s["ln_cent"], 4 * n + c + 1)
                if 4 * n + c >= 2:
                    act.wait_ge(s["ln_var"], 4 * n + c - 1)
                act.activation(ln_sqr[:, c % 2, :], ch(dst, c), ACT.Square).then_inc(s["ln_sq"], 1)

            def out(c):
                act.wait_ge(s["ln_norm"], 4 * n + c + 1)
                for o, g, b in affine:
                    act.activation(ch(o, c), ch(dst, c), ACT.Identity, bias=col(b), scale=col(g))\
                        .then_inc(s["ln_aff"], 1)
            for c in range(NC_):
                act.wait_ge(s["ln_var"], 4 * n + c + 1)
                act.activation(ln_rs[:, c, :], bank[c % 2][:, 0:TT], ACT.Sqrt, bias=eps[:, 0:1])\
                    .then_inc(s["ln_std"], 1)
                if c >= 1 and affine:
                    out(c - 1)
            if affine:
                out(NC_ - 1)

        CR = 8
        PREP = 6
        SB = 2
        G = 4 * SB
        U = 4 * G
        JOBS = 7 * G

        def sa_jobs(u):
            g, i = u // 4, u % 4
            if i == 0:
                return [["q"], ["k"], ["v"], ["spread"] if g else []]
            if i == 1:
                return [["q0"], [], ["v_turn"], ["q1"]]
            if i == 2:
                return [["k0"], ["q2"], ["k1"], ["out"] if g else []]
            return [["k2"], ["q3"], ["k3"], []]

        BY_ACT = ("q", "v", "q0", "q1", "q2", "q3", "spread")

        def sa_count(u, name):
            n = 0
            for w in range(U):
                for slot in sa_jobs(w):
                    for job in slot:
                        if (w, job) == (u, name):
                            return n
                        n += (job in BY_ACT) == (name in BY_ACT)
            return n

        def sa_jobs_at(u, n, act):
            w, slot = (u - 1, n + 2) if n < 2 else (u, n - 2)
            if not 0 <= w < U:
                return []
            return [(w, job) for job in sa_jobs(w)[slot] if (job in BY_ACT) == act]

        def sa_sp(sp):
            sp.dma_start(w_qkv[:, :, :, :].rearrange("p g k m -> p (g k m)"), d["w_qkv"]).then_inc(s["w_qkv_in"], 16)
            sp.dma_start(w_li1[:, :, :].rearrange("p g m -> p (g m)"), d["w_li1"]).then_inc(s["w_qkv_in"], 16)

        def sa_sel_dve(dve):
            dve.tensor_scalar(sel[:, :, :], ones_mat[:, :].unsqueeze(1).to_broadcast([P, 4, P]), 0.0, None, ALU.mult).then_inc(s["sel_ready"], 1)
            dve.wait_ge(s["sel_ready"], 1)
            for kind, blocks in enumerate(((0, 1), (2, 3), (0, 2), (1, 3))):
                for blk in blocks:
                    for h in range(4):
                        rows = slice(32 * h, 32 * h + 32)
                        dve.tensor_copy(sel[rows, kind, 32 * blk:32 * blk + 32], ident[rows, rows])\
                            .then_inc(s["sel_ready"], 1)

        PREP_ACT, PREP_DVE = ("q", "v", "q0", "q1", "q2", "q3"), ("k", "v_turn", "k0", "k1", "k2", "k3")

        def sa_pe(pe):
            def prepare(name, g, col_, before_, v_copied, group):
                act = name in BY_ACT
                out = bank[6 if act else 7]
                if type(before_) is not int or before_:
                    pe.wait_ge(s["prep_act" if act else "prep_dve"], before_)
                if name in ("q", "k", "v"):
                    src = a234[:, bass.ds(col_ + (0 if name == "q" else N), C)]
                    ins = pe.matmul(out[:, :], w_qkv[:, g, "qkv".index(name), :], src, start=True, stop=True)
                elif name == "v_turn":
                    pe.wait_ge(s["prep_act"], v_copied)
                    for t in range(TT):
                        ins = pe.transpose(out[:, t * P:(t + 1) * P], vt[:, t * P:(t + 1) * P], ident[:, :])
                else:
                    k = 0 if act else 1
                    rows = slice(32 * int(name[1]), 32 * int(name[1]) + 32)
                    pe.wait_ge(s["k_split" if k else "q_split"], group + 1)
                    for low in range(2):
                        ins = pe.matmul(out[:, :], sel[rows, 2 * k + low, :], parts[rows, k, low, :],
                                        start=(low == 0), stop=(low == 1))
                ins.then_inc(s["prep_mm_act" if act else "prep_mm_dve"], 1)

            pe.wait_ge(s["w_qkv_in"], 32)
            pe.wait_ge(s["sel_ready"], 33)
            for n in range(PREP):
                prepare(PREP_ACT[n], 0, 0, n, 2, 0)
                prepare(PREP_DVE[n], 0, 0, n, 2, 0)
            with pe.Fori(0, B // SB) as b:
                def made(name, u):
                    w = max(w for w in range(u) if any(name in slot for slot in sa_jobs(w)))
                    return PREP + JOBS * b + sa_count(w, name)

                def score(u, h):
                    g, i, t = u // 4, u % 4, 4 * u + h
                    if i == 0 and g:
                        pe.wait_ge(s["prep_act"], made(f"q{h}", u) + 1)
                        pe.wait_ge(s["prep_dve"], made(f"k{h}", u) + 1)
                    elif i == 0 and h == 0:
                        pe.wait_ge(s["prep_act"], PREP + JOBS * b)
                        pe.wait_ge(s["prep_dve"], PREP + JOBS * b)
                    pe.wait_ge(s["exp_ready"], b * (4 * U) + (t - 2 if t > 2 else 0) + CR)
                    pe.matmul(bank[t % 3][:, :], q_st[:, g % 2, h, i * P:(i + 1) * P], k_st[:, g % 2, h, :],
                              start=True, stop=True).then_inc(s["sc_ready"], 1)

                def turn(u, h):
                    i = u % 4
                    if h == 0:
                        pe.wait_ge(s["masked"], b * U + u + 1)
                    pe.wait_ge(s["ev_act" if h % 2 else "ev_dve"], b * (2 * U) + 2 * u + h // 2 + CR)
                    for k in range(i, 4):
                        ins = pe.transpose(bank[3 + h % 2][:, (k - i) * P:(k - i + 1) * P],
                                           pbuf[:, u % 2, h, k * P:(k + 1) * P], ident[:, :])
                    ins.then_inc(s["turned"], 1)

                def attend(u):
                    g, i = u // 4, u % 4
                    pe.wait_ge(s["ev_dve"], b * (2 * U) + 2 * u + 2 + CR)
                    pe.wait_ge(s["ev_act"], b * (2 * U) + 2 * u + 2 + CR)
                    if i == 0 and g:
                        pe.wait_ge(s["o_ready"], b * G + g)
                    for h in range(4):
                        for k in range(i, 4):
                            ins = pe.matmul(bank[5][32 * h:32 * h + 32, i * P:(i + 1) * P],
                                            vs[:, g % 2, k, 32 * h:32 * h + 32], ptb[:, u % 2, h, k - i, :],
                                            start=(k == i), stop=(k == 3))
                    ins.then_inc(s["av_done"], 1)

                def finish(name, u, g):
                    if name == "spread":
                        pe.wait_ge(s["prep_act"], PREP + JOBS * b + sa_count(u, name))
                        pe.wait_ge(s["rinv_ready"], b * G + g + 1)
                        for i in range(TT):
                            ins = pe.matmul(bank[6][:, i * P:(i + 1) * P], rinv[:, i, :], ident[:, :],
                                            start=True, stop=True)
                        ins.then_inc(s["prep_mm_act"], 1)
                    else:
                        pe.wait_ge(s["prep_dve"], PREP + JOBS * b + sa_count(u, name))
                        pe.wait_ge(s["o_ready"], b * G + g + 1)
                        pe.matmul(bank[7][:, :], w_li1[:, g % 4, :], osb, start=True, stop=True)\
                            .then_inc(s["prep_mm_dve"], 1)

                def slot(u, n):
                    g = u // 4
                    for name in sa_jobs(u)[n]:
                        if name in ("spread", "out"):
                            finish(name, u, g - 1)
                        else:
                            prepare(name, (g + 1) % 4, b * (SB * C) + (g + 1) // 4 * C,
                                    PREP + JOBS * b + sa_count(u, name),
                                    PREP + JOBS * b + sa_count(4 * g, "v") + 1, b * G + g + 1)

                for u in range(U + 1):
                    for n in range(4):
                        if u < U:
                            score(u, n)
                        if n == 3 and u >= 2:
                            attend(u - 2)
                        if u == U and n == 2:
                            finish("spread", U, G - 1)
                        w = u - 2 if n < 2 else u - 1
                        if w >= 0:
                            turn(w, (n + 2) % 4)
                        if n < 2 and u:
                            slot(u - 1, n + 2)
                        elif n >= 2 and u < U:
                            slot(u, n - 2)
                turn(U - 1, 2)
                turn(U - 1, 3)
                attend(U - 1)
                finish("out", U, G - 1)

        def sa_dve(dve):
            def read(name, a, before_):
                dve.wait_ge(s["prep_mm_dve"], before_ + 1)
                if name == "k":
                    dve.tensor_copy(parts[:, 1, 0, :], bank[7][:, :])
                dst = {"k": kt, "v_turn": vs[:, a, :, :].rearrange("p t m -> p (t m)")}.get(name)
                if dst is None:
                    dst = k_st[:, a, int(name[1]), :]
                dve.tensor_copy(dst, bank[7][:, :]).then_inc(s["prep_dve"], 1)

            for n in range(PREP):
                read(PREP_DVE[n], 0, n)
            with dve.Fori(0, B // SB) as b:
                def maximum(u, h):
                    t = 4 * u + h
                    dve.wait_ge(s["sc_ready"], b * (4 * U) + t + 1)
                    dve.tensor_reduce(nmx[:, t % 64:t % 64 + 1], bank[t % 3][:, :], AX, ALU.max, negate=True)\
                        .then_inc(s["max_ready"], 1)

                def copy(u, h):
                    dve.wait_ge(s["turned"], b * (4 * U) + 4 * u + h + 1)
                    dve.tensor_copy(ptb[:, u % 2, h, 0:4 - u % 4, :],
                                    bank[3][:, 0:(4 - u % 4) * P].rearrange("p (k q) -> p k q", q=P))\
                        .then_inc(s["ev_dve"], 1)

                def inverse(g):
                    dve.wait_ge(s["exp_ready"], b * (4 * U) + 16 * g + 16 + CR)
                    dve.reciprocal(rcol[:, :], rsum[:, g % 2, :, :].rearrange("p t h -> p (t h)"))\
                        .then_inc(s["rcol_ready"], 1)
                    dve.wait_ge(s["rcol_ready"], b * G + g + 1)
                    dve.tensor_copy(rinv[:, :, :].rearrange("p t (h r) -> p (t h) r", r=32),
                                    rcol[:, :].unsqueeze(2).to_broadcast([P, 16, 32])).then_inc(s["rinv_ready"], 1)

                def normalise(u, g):
                    dve.wait_ge(s["prep_act"], PREP + JOBS * b + sa_count(u, "spread") + 1)
                    dve.wait_ge(s["av_done"], b * U + 4 * g + 4)
                    dve.tensor_tensor(osb, bank[5][:, :], rbs, ALU.mult).then_inc(s["o_ready"], 1)

                def residual(u):
                    acc = a234[:, bass.ds(b * (SB * C) + ((u // 4 - 1) // 4 * C + 2 * N), C)]
                    n = PREP + JOBS * b + sa_count(u, "out")
                    dve.wait_ge(s["prep_dve"], n)
                    dve.wait_ge(s["prep_mm_dve"], n + 1)
                    dve.tensor_tensor(acc, bank[7][:, :], acc, ALU.add).then_inc(s["prep_dve"], 1)

                def job(u, name):
                    if name == "out":
                        residual(u)
                    else:
                        read(name, (u // 4 + 1) % 2, PREP + JOBS * b + sa_count(u, name))

                for u in range(U + 1):
                    for n in range(4):
                        if u < U:
                            maximum(u, n)
                        if n == 0 and u >= 2:
                            copy(u - 2, 2)
                        if n == 2:
                            if u and u % 4 == 0:
                                inverse(u // 4 - 1)
                            if u:
                                copy(u - 1, 0)
                        for w, name in sa_jobs_at(u, n, False):
                            job(w, name)
                    if u % 4 == 1 and u > 4:
                        normalise(u - 1, u // 4 - 1)
                copy(U - 1, 2)
                normalise(U, G - 1)
                residual(U)

        def sa_act(act):
            def read(name, a, before_):
                act.wait_ge(s["prep_mm_act"], before_ + 1)
                if name == "q":
                    act.activation(parts[:, 0, 0, :], bank[6][:, :], ACT.Copy, scale=32.0 ** -0.5)
                    act.activation(qt, bank[6][:, :], ACT.Copy, scale=32.0 ** -0.5).then_inc(s["prep_act"], 1)
                    return
                dst = {"v": vt, "spread": rbs}.get(name)
                if dst is None:
                    dst = q_st[:, a, int(name[1]), :]
                act.activation(dst, bank[6][:, :], ACT.Copy).then_inc(s["prep_act"], 1)

            for n in range(PREP):
                read(PREP_ACT[n], 0, n)
            with act.Fori(0, B // SB) as b:
                def power(u, h):
                    t = 4 * u + h
                    if u >= 2:
                        act.wait_ge(s["turned"], b * (4 * U) + 4 * (u - 2) + h + 1)
                    act.wait_ge(s["max_ready"], b * (4 * U) + t + 1)
                    act.activation(pbuf[:, u % 2, h, :], bank[t % 3][:, :], ACT.Exp, bias=nmx[:, t % 64:t % 64 + 1],
                                   accum_out=rsum[:, (u // 4) % 2, u % 4, h:h + 1]).then_inc(s["exp_ready"], 1)

                def copy(u, h):
                    act.wait_ge(s["turned"], b * (4 * U) + 4 * u + h + 1)
                    act.activation(ptb[:, u % 2, h, 0:4 - u % 4, :],
                                   bank[4][:, 0:(4 - u % 4) * P].rearrange("p (k q) -> p k q", q=P),
                                   ACT.Copy).then_inc(s["ev_act"], 1)

                def job(u, name):
                    read(name, (u // 4 + 1) % 2, PREP + JOBS * b + sa_count(u, name))

                for u in range(U + 1):
                    for n in range(4):
                        if u < U:
                            power(u, n)
                        if n == 1 and u >= 2:
                            copy(u - 2, 3)
                        if n == 3 and u:
                            copy(u - 1, 1)
                        for w, name in sa_jobs_at(u, n, True):
                            job(w, name)
                        if u == U and n == 2:
                            job(U, "spread")
                copy(U - 1, 3)

        def sa_pool(pool):
            def split(k, ready):
                src, sm = (kt, "k_split") if k else (qt, "q_split")
                pool.wait_ge(s["prep_dve" if k else "prep_act"], ready)
                pool.tensor_tensor(parts[:, k, 1, :], src, parts[:, k, 0, :].bitcast(F32), ALU.subtract)\
                    .then_inc(s[sm], 1)

            split(0, 1)
            split(1, 1)
            with pool.Fori(0, B // SB) as b:
                for u in range(U):
                    g, i = u // 4, u % 4
                    pool.wait_ge(s["exp_ready"], b * (4 * U) + 4 * u + 4 + CR)
                    blk = pbuf[:, u % 2, :, i * P:(i + 1) * P]
                    pool.tensor_tensor(blk, blk, before[:, :].unsqueeze(1).to_broadcast([P, 4, P]), ALU.mult)\
                        .then_inc(s["masked"], 1)
                    if i == 0:
                        for k, name in enumerate("qk"):
                            split(k, PREP + JOBS * b + sa_count(u, name) + 1)

        def mlp_sp(sp, m):
            if m:
                sp.wait_ge(s["mlp_down"], 16)
            sp.dma_start(w_li2[:, :], d[f"a{m + 1}_li2"]).then_inc(s["mlp_w_in"], 16)
            sp.dma_start(w_li3[:, :, :].rearrange("p f m -> p (f m)"), d[f"a{m + 1}_li3"])\
                .then_inc(s["mlp_w_in"], 16)

        def mlp_pe(pe, m, n):
            b0 = 16 * m

            def up(u):
                c, f = u // NF, u % NF
                if f == 0:
                    pe.wait_ge(s["ln_aff"], aff_at(n, c, 0))
                if u >= 2:
                    pe.wait_ge(s["mlp_gelu"], b0 + u - 1)
                pe.matmul(bank[4 + u % 2][:, :], w_li2[:, f * P:(f + 1) * P], ch(a2, c), start=True, stop=True)\
                    .then_inc(s["mlp_up"], 1)

            def down(u):
                c, f = u // NF, u % NF
                pe.wait_ge(s["mlp_gelu"], b0 + u + 1)
                if f == 0 and c >= 2:
                    pe.wait_ge(s["mlp_res"], 4 * m + c - 1)
                pe.matmul(bank[6 + c % 2][:, :], w_li3[:, f, :], hid_t(u % 4), start=(f == 0), stop=(f == NF - 1))\
                    .then_inc(s["mlp_down"], 1)
            pe.wait_ge(s["mlp_w_in"], 32 * (m + 1))
            up(0)
            up(1)
            for u in range(16):
                down(u)
                if u + 2 < 16:
                    up(u + 2)

        def mlp_act(act, m):
            b0 = 16 * m
            for u in range(16):
                act.wait_ge(s["mlp_up"], b0 + u + 1)
                if u >= 4:
                    act.wait_ge(s["mlp_down"], b0 + u - 3)
                act.activation(hid_t(u % 4), bank[4 + u % 2][:, :], ACT.Gelu, bias=col(f"a{m + 1}_li2_b", u % NF))\
                    .then_inc(s["mlp_gelu"], 1)

        def mlp_dve(dve, m):
            for c in range(NC_):
                dve.wait_ge(s["mlp_down"], 16 * m + 4 * c + 4)
                dve.scalar_tensor_tensor(ch(a4, c), bank[6 + c % 2][:, :], col(f"a{m + 1}_li3_b"), ch(a4, c),
                                         ALU.add, ALU.add).then_inc(s["mlp_res"], 1)
                dve.wait_ge(s["mlp_res"], 4 * m + c + 1)
                ins = dve.tensor_tensor(ch(a1, c), ch(a1, c), ch(a4, c), ALU.add)
                ins.then_inc(s["mlp_out"], 1)
                if m:
                    dve.wait_ge(s["mlp_out"], 4 + 2 * c + 1)
                    dve.scalar_tensor_tensor(ch(x, c), ch(a1, c), tg[:, 0:1], ch(x, c), ALU.mult, ALU.add)\
                        .then_inc(s["mlp_out"], 1)

        NCH = [c["nch"] for c in CROSS]
        BD_PRE = [2 * sum(NCH[:l]) for l in range(5)]

        def cx_sp(sp, l):
            if l:
                sp.wait_ge(s["cx_fold"], 8 * l)
            k = NCH[l] * P
            for t, name in ((cwq, "q"), (cwk, "k"), (cwv, "v"), (cwo, "o")):
                sp.dma_start(t[:, 0:k], d[f"c{l}_{name}"]).then_inc(s["cw_in"], 16)

        def cx_src(l):
            return ctx_n if l == 0 else ctx_t

        def cx_pe(pe, l, free=()):
            nch = NCH[l]
            for sm, v in free:
                pe.wait_ge(sm, v)
            pe.wait_ge(s["cw_in"], 64 * (l + 1))
            for m in range(2 * nch):
                w = cwv if m >= nch else cwk
                q = BD_PRE[l] + m
                if m >= 2:
                    pe.wait_ge(s["cx_kts"], q - 1)
                pe.matmul(bank[5 + m % 2][:, 0:P], w[:, (m % nch) * P:(m % nch + 1) * P], cx_src(l)[:, :],
                          start=True, stop=True).then_inc(s["cx_proj"], 1)
            hw = H // nch * M
            for b in range(B):
                if b == 0:
                    pe.wait_ge(s["cx_bd"], BD_PRE[l] + nch)
                    pe.wait_ge(s["cx_kts"], BD_PRE[l] + 2 * nch)
                if b >= 2:
                    pe.wait_ge(s["cx_folded"], 8 * l + b - 1)
                w = min(B * hw, C)
                for at_ in range(b * C, (b + 1) * C, w):
                    c = at_ // (B * hw)
                    ins = pe.matmul(bank[5 + b % 2][:, at_ % C:at_ % C + w], cwq[:, c * P:(c + 1) * P],
                                    kbd[:, at_:at_ + w], start=True, stop=True)
                ins.then_inc(s["cx_fold"], 1)
            for b in range(B):
                if b == 0:
                    pe.wait_ge(s["cx_bd"], BD_PRE[l] + 2 * nch)
                pe.wait_ge(s["cx_folded"], 8 * l + 4 + b - 1)
                for g in range(4):
                    o = bank[5 + b % 2][:, g * P:(g + 1) * P]
                    if nch == 1:
                        ins = pe.matmul(o, vbd[:, b * hw + g * P:b * hw + (g + 1) * P], cwo[:, 0:P],
                                        start=True, stop=True)
                    elif nch == 4:
                        ins = pe.matmul(o, vbd[:, (g * B + b) * hw:(g * B + b + 1) * hw], cwo[:, g * P:(g + 1) * P],
                                        start=True, stop=True)
                    else:
                        for k in range(2):
                            c = 2 * g + k
                            ins = pe.matmul(bank[5 + b % 2][64 * k:64 * k + 64, g * P:(g + 1) * P],
                                            vbd[:, (c * B + b) * hw:(c * B + b + 1) * hw],
                                            cwo[:, c * P:(c + 1) * P], start=True, stop=True)
                ins.then_inc(s["cx_fold"], 1)
            if l == 3:
                for b in range(B):
                    if b:
                        pe.wait_ge(s["cx_bias_row"], b)
                    else:
                        pe.wait_ge(s["cx_folded"], 8 * l + 8)
                    pe.matmul(bank[7][0:1, :], col("bq3"), kbd[:, b * C:(b + 1) * C], start=True, stop=True)\
                        .then_inc(s["cx_bias"], 1)

        def cx_act(act, l):
            nch = NCH[l]
            for m in range(2 * nch):
                q = BD_PRE[l] + m
                act.wait_ge(s["cx_proj"], q + 1)
                if m >= 2:
                    act.wait_ge(s["cx_bd"], q - 1)
                bias = col("bv3" if m >= nch else "bk3") if l == 3 else 0.0
                act.activation(kts[:, m % 2, :], bank[5 + m % 2][:, 0:P], ACT.Identity, bias=bias)\
                    .then_inc(s["cx_kts"], 1)
            for k in range(8):
                act.wait_ge(s["cx_fold"], 8 * l + k + 1)
                if k < 4:
                    if nch == 1:
                        dst, src = qk[:, k, :], bank[5 + k % 2][:, :]
                    else:
                        n = nch // 4
                        dst = qk[:, :, :].rearrange("p b (c w) -> p c b w", c=nch)[:, n * k:n * k + n]
                        src = bank[5 + k % 2][:, :].rearrange("p (c b w) -> p c b w", c=n, b=B)
                    act.activation(dst, src, ACT.Copy).then_inc(s["cx_folded"], 1)
                else:
                    g = CROSS[l]["gate"]
                    scale = 1.0 if g is None else tg[:, g:g + 1]
                    act.activation(ch(vw, k - 4), bank[5 + k % 2][:, :], ACT.Identity, scale=scale)\
                        .then_inc(s["cx_folded"], 1)
            if l == 3:
                for b in range(B):
                    act.wait_ge(s["cx_bias"], b + 1)
                    act.activation(qb[:, b, :], bank[7][0:1, :], ACT.Copy).then_inc(s["cx_bias_row"], 1)

        def cx_dve(dve, l):
            nch = NCH[l]
            hc = H // nch
            hw = hc * M
            for m in range(2 * nch):
                dst = (vbd if m >= nch else kbd)[:, (m % nch) * B * hw:(m % nch + 1) * B * hw]
                dve.wait_ge(s["cx_kts"], BD_PRE[l] + m + 1)
                ins = dve.tensor_tensor(
                    dst.rearrange("p (b h t) -> p b h t", b=B, h=hc),
                    kts[:, m % 2, :].rearrange("p (b t) -> p b t", b=B).unsqueeze(2).to_broadcast([P, B, hc, M]),
                    masks[nch][:, :].unsqueeze(1).unsqueeze(3).to_broadcast([P, B, hc, M]), ALU.mult)
                ins.then_inc(s["cx_bd"], 1)

        def ca_guard(eng, name, count):
            if count > 0:
                eng.wait_ge(s[name], count)

        def ca_bank(v):
            return bank[(0, 1, 5, 6)[v % 4]]

        def ca_pool(pool, l):
            for v in range(16 * l, 16 * l + 16):
                pool.wait_ge(s["ca_rinv"], v + 1)
                ca_guard(pool, "ca_turned", v - 1)
                pool.tensor_tensor(pn[:, v % 2, :].rearrange("p (h t) -> p h t", t=M),
                                   e_[:, v % 4, :].rearrange("p (h t) -> p h t", t=M),
                                   crin[:, v % 4, :].unsqueeze(2).to_broadcast([P, H, M]), ALU.mult)\
                    .then_inc(s["ca_prob"], 1)

        def ca_pe(pe, l, z, ready):
            v0 = 16 * l

            def score(v):
                b = (v - v0) // TT
                if (v - v0) % TT == 0:
                    for sm, n in ready(b):
                        pe.wait_ge(sm, n)
                ca_guard(pe, "ca_sub", v - 3)
                ins = pe.matmul(ca_bank(v)[:, :], z[:, (v - v0) * P:(v - v0 + 1) * P], qk[:, b, :],
                                start=True, stop=(l != 3))
                if l == 3:
                    ins = pe.matmul(ca_bank(v)[:, :], ones_mat[0:1, :], qb[:, b, :], start=False, stop=True)
                ins.then_inc(s["ca_score"], 1)

            def turn(v):
                pe.wait_ge(s["ca_prob"], v + 1)
                ca_guard(pe, "ca_pt", v - 1)
                for g in range(4):
                    ins = pe.transpose(bank[2 + v % 2][:, g * P:(g + 1) * P], pn[:, v % 2, g * P:(g + 1) * P],
                                       ident[:, :])
                ins.then_inc(s["ca_turned"], 1)

            def attend(b, g):
                i = 4 * l + b
                if g == 0:
                    pe.wait_ge(s["ca_pt"], v0 + 4 * b + 4)
                    ca_guard(pe, "ca_res", i - 1)
                ins = pe.matmul(bank[4 + 3 * (b % 2)][:, :], vw[:, b * C + g * P:b * C + (g + 1) * P],
                                ptc[:, b % 2, g, :], start=(g == 0), stop=(g == 3))
                if g == 3:
                    ins.then_inc(s["ca_av"], 1)
            for v in range(v0, v0 + 3):
                score(v)
            for v in range(v0, v0 + 16):
                if v + 3 < v0 + 16:
                    score(v + 3)
                turn(v)
                if v - v0 >= TT:
                    attend((v - v0) // TT - 1, v % TT)
            for g in range(4):
                attend(B - 1, g)

        def ca_dve(dve, l, src, dst):
            hs = lambda ap: ap.rearrange("p (h t) -> p h t", t=M)
            v0 = 16 * l

            def centre(v):
                dve.wait_ge(s["ca_score"], v + 1)
                dve.tensor_reduce(cmx[:, v % 2, :], hs(ca_bank(v)[:, :]), AX, ALU.max).then_inc(s["ca_max"], 1)
                ca_guard(dve, "ca_prob", v - 3)
                dve.wait_ge(s["ca_max"], v + 1)
                dve.tensor_tensor(hs(e_[:, v % 4, :]), hs(ca_bank(v)[:, :]),
                                  cmx[:, v % 2, :].unsqueeze(2).to_broadcast([P, H, M]), ALU.subtract)\
                    .then_inc(s["ca_sub"], 1)

            def total(v):
                dve.wait_ge(s["ca_exp"], v + 1)
                dve.tensor_reduce(csum[:, v % 2, :], hs(e_[:, v % 4, :]), AX, ALU.add).then_inc(s["ca_sum"], 1)
                dve.wait_ge(s["ca_sum"], v + 1)
                dve.reciprocal(crin[:, v % 4, :], csum[:, v % 2, :]).then_inc(s["ca_rinv"], 1)

            def residual(b):
                dve.wait_ge(s["ca_av"], 4 * l + b + 1)
                bias = col("a2_li1_b") if l == 0 else gbo[:, l:l + 1]
                dve.scalar_tensor_tensor(ch(dst, b), bank[4 + 3 * (b % 2)][:, :], bias, ch(src, b),
                                         ALU.add, ALU.add).then_inc(s["ca_res"], 1)
            for v in range(v0, v0 + 3):
                centre(v)
            for v in range(v0, v0 + 16):
                total(v)
                if v + 3 < v0 + 16:
                    centre(v + 3)
                if v % TT == 0 and v - v0 > TT:
                    residual((v - v0) // TT - 2)
            residual(B - 2)
            residual(B - 1)

        def ca_act(act, l):
            v0 = 16 * l

            def power(v):
                act.wait_ge(s["ca_sub"], v + 1)
                act.activation(e_[:, v % 4, :], e_[:, v % 4, :], ACT.Exp, scale=CROSS[l]["scale"])\
                    .then_inc(s["ca_exp"], 1)

            def copy(v):
                b, t = (v - v0) // TT, v % TT
                if t == 0:
                    ca_guard(act, "ca_av", 4 * l + b - 1)
                act.wait_ge(s["ca_turned"], v + 1)
                act.activation(ptc[:, b % 2, :, t * P:(t + 1) * P],
                               bank[2 + v % 2][:, :].rearrange("p (g q) -> p g q", q=P), ACT.Copy)\
                    .then_inc(s["ca_pt"], 1)
            for v in range(v0, v0 + 3):
                power(v)
            for v in range(v0, v0 + 16):
                if v + 3 < v0 + 16:
                    power(v + 3)
                copy(v)

        CREDIT = [(k, CR) for k in ("exp_ready", "ev_dve", "ev_act")]

        def setup_sp(sp):
            for c in range(NC_):
                sp.dma_start(ch(x, c), d["x"][:, c * C:(c + 1) * C]).then_inc(s[f"ld_x{c}"], 16)
            sp.dma_start(cols[:, :], d["cols"]).then_inc(s["ld_cols"], 16)
            sp.dma_start(ctx_t[:, :], d["ctx"]).then_inc(s["ld_ctx"], 16)
            sp.dma_start(wr[:, :, :].rearrange("p k m -> p (k m)"), d["f2_w"]).then_inc(s["small_in"], 16)
            sp.dma_start(gate_w[:, :, :].rearrange("p k m -> p (k m)"), d["gates"]).then_inc(s["small_in"], 16)

        n_const = [0]

        def setup_pool(pool):
            def put(ins):
                n_const[0] += 1
                ins.then_inc(s["const_ready"], 1)
                pool.wait_ge(s["const_ready"], n_const[0])
            put(pool.memset(eps[:, :], LN_EPS))
            put(pool.memset(mean_mat[:, :], 1.0 / P))
            for k, (name, v) in enumerate(CREDIT):
                pool.memset(credit[:, k:k + 1], 0.0).then_inc(s[name], v)
            put(pool.memset(mean64[:, :], 1.0 / CD))
            put(pool.memset(ones_mat[:, :], 1.0))
            put(pool.memset(ident[:, :], 0.0))
            put(pool.affine_select(out=ident[:, :], in_=ident[:, :], compare_op=ALU.not_equal, fill=1.0, base=0,
                                   pattern=[[-1, P]], channel_multiplier=1))
            put(pool.tensor_copy(identb[:, :], ident[:, :]))
            put(pool.affine_select(out=before[:, :], in_=ones_mat[:, :], compare_op=ALU.is_gt, fill=0.0, base=0,
                                   pattern=[[1, P]], channel_multiplier=-1))
            for nch, m in masks.items():
                hc = H // nch
                dh = P // hc
                put(pool.memset(m[:, :], 1.0))
                put(pool.affine_select(out=m[:, :], in_=m[:, :], compare_op=ALU.is_ge, fill=0.0, base=0,
                                       pattern=[[-dh, hc]], channel_multiplier=1))
                put(pool.affine_select(out=m[:, :], in_=m[:, :], compare_op=ALU.is_ge, fill=0.0, base=dh - 1,
                                       pattern=[[dh, hc]], channel_multiplier=-1))
            for e in range(E):
                put(pool.memset(rank[:, e:e + 1], float(E - e)))

        N_CONST = 8 + 3 * len(masks) + E

        def setup_act(act):
            act.wait_ge(s["ld_cols"], 16)
            act.activation(tg[:, :], cols[:, 0:8], ACT.Tanh).then_inc(s["gates_ready"], 1)

        links = {"dve": 0, "act": 0, "pool": 0}

        def link(eng, who, ins):
            links[who] += 1
            ins.then_inc(s[who + "_link"], 1)
            eng.wait_ge(s[who + "_link"], links[who])

        def setup_dve(dve):
            dve.wait_ge(s["const_ready"], N_CONST)
            dve.wait_ge(s["gates_ready"], 1)
            dve.memset(gbo[:, :], 0.0).then_inc(s["gates_ready"], 1)
            dve.wait_ge(s["gates_ready"], 2)
            for l, name in ((2, "bo2"), (3, "bo3")):
                dve.tensor_scalar(gbo[:, l:l + 1], col(name), tg[:, l:l + 1], None, ALU.mult)\
                    .then_inc(s["gates_ready"], 1)
            for k, name in enumerate(("mu_r", "mu_k")):
                dve.tensor_scalar(omu[:, k:k + 1], col(name), -1.0, 1.0, ALU.mult, ALU.add)\
                    .then_inc(s["gates_ready"], 1)

        def r1_init_pool(pool):
            for c in range(NC_):
                pool.wait_ge(s["ln_aff"], aff_at(1, c, 0))
                pool.tensor_scalar(ch(a4, c), ch(a1, c), col("a1_li1_b"), None, ALU.add).then_inc(s["r1_init"], 1)

        def cln_pe(pe):
            pe.wait_ge(s["ld_ctx"], 16)
            pe.matmul(bank[4][0:CD, 0:P], mean64[:, :], ctx_t[:, :], start=True, stop=True)\
                .then_inc(s["cx_ln_mm"], 1)
            pe.wait_ge(s["cx_ln_act"], 1)
            pe.matmul(bank[5][0:CD, 0:P], mean64[:, :], cln[:, 1, :], start=True, stop=True)\
                .then_inc(s["cx_ln_mm"], 1)

        def cln_dve(dve):
            dve.wait_ge(s["cx_ln_mm"], 1)
            dve.tensor_tensor(cln[:, 0, :], ctx_t[:, :], bank[4][0:CD, 0:P], ALU.subtract)\
                .then_inc(s["cx_ln_dve"], 1)
            dve.wait_ge(s["cx_ln_act"], 2)
            dve.reciprocal(cln[:, 2, :], cln[:, 2, :]).then_inc(s["cx_ln_dve"], 1)
            dve.wait_ge(s["cx_ln_dve"], 2)
            dve.tensor_tensor(cln[:, 0, :], cln[:, 0, :], cln[:, 2, :], ALU.mult).then_inc(s["cx_ln_dve"], 1)

        def cln_act(act):
            act.wait_ge(s["cx_ln_dve"], 1)
            act.activation(cln[:, 1, :], cln[:, 0, :], ACT.Square).then_inc(s["cx_ln_act"], 1)
            act.wait_ge(s["cx_ln_mm"], 2)
            act.activation(cln[:, 2, :], bank[5][0:CD, 0:P], ACT.Sqrt, bias=eps[0:CD, 0:1])\
                .then_inc(s["cx_ln_act"], 1)
            act.wait_ge(s["cx_ln_dve"], 3)
            act.activation(ctx_n[:, :], cln[:, 0, :], ACT.Identity, bias=col("a2_lny_b")[0:CD, :],
                           scale=col("a2_lny_g")[0:CD, :]).then_inc(s["cx_ln_act"], 1)

        def f0w_sp(sp):
            sp.wait_ge(s["prep_dve"], PREP + JOBS * (B // SB))
            sp.dma_start(f0w1, d["f0_w1"]).then_inc(s["f0w_in"], 16)
            sp.dma_start(f0w2, d["f0_w2"]).then_inc(s["f0w_in"], 16)

        def f0w_dve(dve):
            dve.wait_ge(s["f0w_in"], 32)
            for k, w in enumerate((f0w1, f0w2)):
                ins = dve.tensor_reduce(wabs[:, k:k + 1], w, AX, ALU.add, apply_absolute_value=True)
            ins.then_inc(s["f0w_ready"], 1)
            dve.wait_ge(s["f0w_mean"], 1)
            link(dve, "dve", dve.tensor_scalar(wmean[:, :], bank[4][:, 0:2], 1.0 / F, 1e-5, ALU.mult, ALU.max))
            link(dve, "dve", dve.reciprocal(wsc[:, :], wmean[:, :]))
            for k, (w, o) in enumerate(((f0w1, w1q), (f0w2, w2q))):
                link(dve, "dve", dve.tensor_scalar(f0tmp, w, wsc[:, k:k + 1], MAGIC, ALU.mult, ALU.add))
                link(dve, "dve", dve.tensor_scalar(f0tmp, f0tmp, MAGIC, 1.0, ALU.subtract, ALU.min))
                link(dve, "dve", dve.tensor_scalar(o[:, :], f0tmp, -1.0, None, ALU.max))
            link(dve, "dve", dve.tensor_scalar(cwm[:, :], cols[:, COLS["conv_w"][0]:COLS["conv_w"][0] + 12],
                                               wmean[:, 0:1], None, ALU.mult))
            link(dve, "dve", dve.memset(hpad[:, :, 0:1], 0.0))
            dve.memset(hpad[:, :, C + 1:C + 2], 0.0).then_inc(s["f0w_ready"], 1)

        def f0w_pe(pe):
            pe.wait_ge(s["f0w_ready"], 1)
            pe.matmul(bank[4][:, 0:2], mean_mat[:, :], wabs[:, :], start=True, stop=True).then_inc(s["f0w_mean"], 1)

        def f1_pe(pe):
            for c in range(NC_):
                pe.wait_ge(s["ln_norm"], 4 * 7 + c + 1)
                if c == 0:
                    pe.wait_ge(s["f0w_ready"], 2)
                if c >= 2:
                    pe.wait_ge(s["f1_q"], c - 1)
                for t in range(TT):
                    ins = pe.transpose(bank[4 + c % 2][:, t * P:(t + 1) * P],
                                       a1[:, c * C + t * P:c * C + (t + 1) * P], ident[:, :])
                ins.then_inc(s["f1_turned"], 1)
                pe.wait_ge(s["f1_am"], c + 1)
                if c:
                    pe.wait_ge(s["f1_ibs"], c)
                for t in range(TT):
                    ins = pe.matmul(bank[7][:, t * P:(t + 1) * P], qa[:, c % 2, 2, t:t + 1].to_broadcast([P, P]),
                                    ident[:, :], start=True, stop=True)
                ins.then_inc(s["f1_ib"], 1)
                pe.wait_ge(s["f1_q"], c + 1)
                if c:
                    pe.wait_ge(s["f1_xqt"], c)
                for t in range(TT):
                    ins = pe.transpose(bank[6][:, :].bitcast(BF16)[:, t * P:(t + 1) * P],
                                       lowp[:, c % 2, t * P:(t + 1) * P], identb[:, :])
                ins.then_inc(s["f1_qt"], 1)
                pe.wait_ge(s["f1_xqt"], c + 1)
                for f in range(NF):
                    if c:
                        pe.wait_ge(s["f1_hd"], 4 * (c - 1) + f + 1)
                    pe.matmul(bank[f][:, :], w1q[:, f * P:(f + 1) * P], lowp[:, 2 + c % 2, :],
                              start=True, stop=True).then_inc(s["f1_h"], 1)

        def quantise(dve, src, a, n, width, am, q, tmp, dst):
            v = src.rearrange("p (t k) -> p t k", k=width)
            link(dve, "dve", dve.tensor_reduce(qa[:, a, 0, 0:n], v, AX, ALU.max, apply_absolute_value=True))
            link(dve, "dve", dve.tensor_scalar(qa[:, a, 0, 0:n], qa[:, a, 0, 0:n], 1e-5, None, ALU.max))
            link(dve, "dve", dve.reciprocal(qa[:, a, 1, 0:n], qa[:, a, 0, 0:n]))
            link(dve, "dve", dve.tensor_scalar(qa[:, a, 1, 0:n], qa[:, a, 1, 0:n], 127.0, None, ALU.mult))
            dve.tensor_scalar(qa[:, a, 2, 0:n], qa[:, a, 0, 0:n], 1.0 / 127.0, None, ALU.mult).then_inc(am, 1)
            for t in range(n):
                ins = dve.tensor_scalar(tmp[:, t * width:(t + 1) * width], v[:, t, :], qa[:, a, 1, t:t + 1], MAGIC,
                                        ALU.mult, ALU.add)
            link(dve, "dve", ins)
            link(dve, "dve", dve.tensor_scalar(tmp, tmp, MAGIC, 127.0, ALU.subtract, ALU.min))
            dve.tensor_scalar(dst, tmp, -128.0, None, ALU.max).then_inc(q, 1)

        def f1_dve(dve):
            def step(c):
                dve.wait_ge(s["f1_turned"], c + 1)
                quantise(dve, bank[4 + c % 2][:, :], c % 2, 4, P, s["f1_am"], s["f1_q"], t32[:, c % 2, :],
                         lowp[:, c % 2, :])

            def left_tap(v):
                dve.wait_ge(s["f1_c0"], v + 1)
                f = v % 4
                dve.scalar_tensor_tensor(yc[:, f, :], hpad[:, f, 0:C], cwm[:, 3 * f:3 * f + 1], yc[:, f, :],
                                         ALU.mult, ALU.add).then_inc(s["f1_c1"], 1)
            step(0)
            for v in range(16):
                c, f = v // 4, v % 4
                if f == 0 and c + 1 < NC_:
                    step(c + 1)
                dve.wait_ge(s["f1_h"], v + 1)
                dve.wait_ge(s["f1_ibs"], c + 1)
                if v >= 4:
                    dve.wait_ge(s["f1_c2"], v - 3)
                dve.tensor_tensor(hpad[:, f, 1:C + 1], bank[f][:, :], ibs[:, c % 2, :], ALU.mult)\
                    .then_inc(s["f1_hd"], 1)
                if v:
                    left_tap(v - 1)
            left_tap(15)

        def f1_pool(pool):
            for v in range(16):
                pool.wait_ge(s["f1_c1"], v + 1)
                pool.wait_ge(s["f1_right"], v + 1)
                pool.tensor_tensor(yc[:, v % 4, :], yc[:, v % 4, :], right[:, v % 2, :], ALU.add)\
                    .then_inc(s["f1_c2"], 1)

        def f1_act(act):
            act.wait_ge(s["f0w_ready"], 2)

            def copies(c):
                act.wait_ge(s["f1_ib"], c + 1)
                act.activation(ibs[:, c % 2, :], bank[7][:, :], ACT.Copy).then_inc(s["f1_ibs"], 1)
                act.wait_ge(s["f1_qt"], c + 1)
                act.activation(lowp[:, 2 + c % 2, :], bank[6][:, :].bitcast(BF16)[:, 0:C], ACT.Copy)\
                    .then_inc(s["f1_xqt"], 1)

            def silu(v):
                act.wait_ge(s["f1_c2"], v + 1)
                act.activation(sil[v // 4][:, v % 4, :], yc[:, v % 4, :], ACT.Silu, bias=col("conv_b", v % 4))\
                    .then_inc(s["f1_silu"], 1)
            copies(0)
            for v in range(16):
                c, f = v // 4, v % 4
                if f == 2 and c + 1 < NC_:
                    copies(c + 1)
                act.wait_ge(s["f1_hd"], v + 1)
                if v >= 4:
                    act.wait_ge(s["f1_silu"], v - 3)
                act.activation(yc[:, f, :], hpad[:, f, 1:C + 1], ACT.Copy, scale=cwm[:, 3 * f + 1:3 * f + 2])\
                    .then_inc(s["f1_c0"], 1)
                if v >= 2:
                    silu(v - 2)
                act.activation(right[:, v % 2, :], hpad[:, f, 2:C + 2], ACT.Copy,
                               scale=cwm[:, 3 * f + 2:3 * f + 3]).then_inc(s["f1_right"], 1)
            silu(14)
            silu(15)

        def f2_pe(pe):
            def turn(v):
                c, t = v // 4, v % 4
                pe.wait_ge(s["f1_silu"], 4 * c + 4)
                if v >= 4:
                    pe.wait_ge(s["f2_scaled"], v - 3)
                for f in range(NF):
                    ins = pe.transpose(bank[4 + t][:, f * P:(f + 1) * P], sil[c][:, f, t * P:(t + 1) * P],
                                       ident[:, :])
                ins.then_inc(s["f2_turned"], 1)

            def turn_q(v):
                pe.wait_ge(s["f2_q"], v + 1)
                if v >= 2:
                    pe.wait_ge(s["f2_hqt"], v - 1)
                for f in range(NF):
                    ins = pe.transpose(bank[v % 2][:, :].bitcast(BF16)[:, f * P:(f + 1) * P],
                                       lowp[:, 4 + v % 4, f * P:(f + 1) * P], identb[:, :])
                ins.then_inc(s["f2_qt"], 1)

            def product(c):
                pe.wait_ge(s["f2_am"], c + 1)
                if c:
                    pe.wait_ge(s["f2_ibs"], c)
                for t in range(TT):
                    ins = pe.matmul(bank[3][:, t * P:(t + 1) * P], qa[:, c % 2, 2, t:t + 1].to_broadcast([P, P]),
                                    ident[:, :], start=True, stop=True)
                ins.then_inc(s["f2_step"], 1)
                pe.wait_ge(s["f2_hqt"], 4 * c + 4)
                if c:
                    pe.wait_ge(s["f2_res0"], c)
                for f in range(NF):
                    ins = pe.matmul(bank[2][:, :], w2q[:, f * P:(f + 1) * P], lowp[:, 8 + 4 * (c % 2) + f, :],
                                    start=(f == 0), stop=(f == NF - 1))
                ins.then_inc(s["f2_o"], 1)
            for t in range(TT):
                turn(t)
            for v in range(NT):
                if v + 4 < NT:
                    turn(v + 4)
                turn_q(v)
                if v % 4 == 3:
                    product(v // 4)

        def f2_dve(dve):
            L = lambda ins: link(dve, "dve", ins)

            def residual(c):
                dve.wait_ge(s["f2_o"], c + 1)
                dve.wait_ge(s["f2_ibs"], c + 1)
                if c >= 2:
                    dve.wait_ge(s["f2_res"], c - 1)
                dve.tensor_tensor(f2t[:, c % 2, :], bank[2][:, :], ibs[:, c % 2, :], ALU.mult).then_inc(s["f2_res0"], 1)
                dve.wait_ge(s["f2_res0"], c + 1)
                dve.scalar_tensor_tensor(ch(x, c), f2t[:, c % 2, :], tg[:, 4:5], ch(x, c), ALU.mult, ALU.add)\
                    .then_inc(s["f2_res"], 1)
            for c in range(NC_):
                a = c % 2
                if c >= 2:
                    dve.wait_ge(s["f2_step"], c - 1)
                for t in range(TT):
                    dve.wait_ge(s["f2_turned"], 4 * c + t + 1)
                    ins = dve.tensor_reduce(qa[:, a, 0, t:t + 1], bank[4 + t][:, :], AX, ALU.max,
                                            apply_absolute_value=True)
                L(ins)
                L(dve.tensor_scalar(qa[:, a, 0, :], qa[:, a, 0, :], 1e-5, None, ALU.max))
                L(dve.reciprocal(qa[:, a, 1, :], qa[:, a, 0, :]))
                L(dve.tensor_scalar(qa[:, a, 1, :], qa[:, a, 1, :], 127.0, None, ALU.mult))
                L(dve.tensor_scalar(qa[:, a, 2, :], qa[:, a, 0, :], 1.0 / 127.0, None, ALU.mult))
                dve.tensor_scalar(qa[:, a, 2, :], qa[:, a, 2, :], wmean[:, 1:2], None, ALU.mult)\
                    .then_inc(s["f2_am"], 1)
                for t in range(TT):
                    v = 4 * c + t
                    if v >= 2:
                        dve.wait_ge(s["f2_q"], v - 1)
                    dve.tensor_scalar(t32[:, v % 2, :], bank[4 + t][:, :], qa[:, a, 1, t:t + 1], MAGIC,
                                      ALU.mult, ALU.add).then_inc(s["f2_scaled"], 1)
                    dve.wait_ge(s["f2_scaled"], v + 1)
                    dve.tensor_scalar(t32[:, v % 2, :], t32[:, v % 2, :], MAGIC, 127.0, ALU.subtract, ALU.min)\
                        .then_inc(s["f2_round"], 1)
                if c:
                    residual(c - 1)
            residual(NC_ - 1)

        def f2_pool(pool):
            for v in range(NT):
                pool.wait_ge(s["f2_round"], v + 1)
                if v >= 4:
                    pool.wait_ge(s["f2_qt"], v - 3)
                pool.tensor_scalar(lowp[:, 4 + v % 4, :], t32[:, v % 2, :], -128.0, None, ALU.max)\
                    .then_inc(s["f2_q"], 1)

        def f2_act(act):
            for v in range(NT):
                c, t = v // 4, v % 4
                act.wait_ge(s["f2_qt"], v + 1)
                if c >= 2 and t == 0:
                    act.wait_ge(s["f2_o"], c - 1)
                act.activation(lowp[:, 8 + 4 * (c % 2):12 + 4 * (c % 2), t * P:(t + 1) * P],
                               bank[v % 2][:, :].bitcast(BF16)[:, 0:C].rearrange("p (f s) -> p f s", f=NF),
                               ACT.Copy).then_inc(s["f2_hqt"], 1)
                if t == 3:
                    act.wait_ge(s["f2_step"], c + 1)
                    act.activation(ibs[:, c % 2, :], bank[3][:, :], ACT.Copy).then_inc(s["f2_ibs"], 1)

        def r_pool(pool):
            for c in range(NC_):
                pool.wait_ge(s["ln_norm"], 4 * 11 + c + 1)
                if c >= 2:
                    pool.wait_ge(s["r_up"], 2 * (c - 1))
                pool.tensor_scalar(mixr[:, c % 2, :], ch(a1, c), col("mu_r"), None, ALU.mult).then_inc(s["r_mix0"], 1)
                pool.tensor_scalar(mixk[:, c % 2, :], ch(a1, c), col("mu_k"), None, ALU.mult).then_inc(s["r_mix0"], 1)

        def r_dve(dve):
            def mix(c):
                for k, t in enumerate((mixr, mixk)):
                    dve.wait_ge(s["r_mix0"], 2 * c + k + 1)
                    dve.scalar_tensor_tensor(t[:, c % 2, 1:C], a1[:, c * C:(c + 1) * C - 1], omu[:, k:k + 1],
                                             t[:, c % 2, 1:C], ALU.mult, ALU.add).then_inc(s["r_mix"], 1)
            mix(0)
            for c in range(NC_):
                if c + 1 < NC_:
                    mix(c + 1)
                dve.wait_ge(s["r_up"], 2 * c + 2)
                link(dve, "dve", dve.tensor_scalar(kact[:, c % 2, :], bank[6 + c % 2][:, :], 0.0, None, ALU.max))
                dve.tensor_tensor(kact[:, c % 2, :], kact[:, c % 2, :], kact[:, c % 2, :], ALU.mult)\
                    .then_inc(s["r_act"], 1)
                dve.wait_ge(s["r_val"], c + 1)
                dve.wait_ge(s["r_gate"], c + 1)
                link(dve, "dve", dve.tensor_tensor(rv[:, c % 2, :], bank[c % 2][:, :], rg[:, c % 2, :], ALU.mult))
                dve.scalar_tensor_tensor(ch(x, c), rv[:, c % 2, :], tg[:, 6:7], ch(x, c), ALU.mult, ALU.add)\
                    .then_inc(s["r_out"], 1)

        def r_act(act):
            for c in range(NC_):
                act.wait_ge(s["r_up"], 2 * c + 1)
                if c >= 2:
                    act.wait_ge(s["r_out"], c - 1)
                act.activation(rg[:, c % 2, :], bank[4 + c % 2][:, :], ACT.Sigmoid).then_inc(s["r_gate"], 1)

        def r_pe(pe):
            pe.wait_ge(s["small_in"], 32)

            def up(c):
                pe.wait_ge(s["r_mix"], 2 * c + 2)
                if c >= 2:
                    pe.wait_ge(s["r_gate"], c - 1)
                    pe.wait_ge(s["r_act"], c - 1)
                pe.matmul(bank[4 + c % 2][:, :], wr[:, 0, :], mixr[:, c % 2, :], start=True, stop=True)\
                    .then_inc(s["r_up"], 1)
                pe.matmul(bank[6 + c % 2][:, :], wr[:, 1, :], mixk[:, c % 2, :], start=True, stop=True)\
                    .then_inc(s["r_up"], 1)
            up(0)
            for c in range(NC_):
                if c + 1 < NC_:
                    up(c + 1)
                pe.wait_ge(s["r_act"], c + 1)
                if c >= 2:
                    pe.wait_ge(s["r_out"], c - 1)
                pe.matmul(bank[c % 2][:, :], wr[:, 2, :], kact[:, c % 2, :], start=True, stop=True)\
                    .then_inc(s["r_val"], 1)

        te = lambda ap: ap.rearrange("p (t e) -> p t e", e=E)
        bc = lambda ap: ap.unsqueeze(2).to_broadcast([P, NT, E])
        LOGIT, PROB, TMP, MASK1, MASK2, PROB2, WT, POS1, POS2, SUM_A, SUM_B, TOT, WROW = range(13)

        def g_pe_logits(pe, k, n):
            pe.wait_ge(s["small_in"], 32)
            for t in range(NT):
                if t % TT == 0:
                    pe.wait_ge(s["ln_norm"], 4 * n + t // TT + 1)
                ins = pe.matmul(bank[6][:, t * E:(t + 1) * E], a1[:, t * P:(t + 1) * P], gate_w[:, k, :],
                                start=True, stop=True)
            ins.then_inc(s["g_logit"], 1)

        def g_act_exp(act, k):
            act.wait_ge(s["g_in"], k + 1)
            act.activation(gt[PROB], gt[LOGIT], ACT.Exp).then_inc(s["g_exp"], 1)

        def first_largest(dve, src, dst):
            L = lambda ins: link(dve, "dve", ins)
            L(dve.tensor_reduce(g16[:, 0, :], te(src), AX, ALU.max))
            L(dve.tensor_tensor(te(gt[TMP]), te(src), bc(g16[:, 0, :]), ALU.is_equal))
            L(dve.tensor_tensor(te(gt[TMP]), te(gt[TMP]), rank[:, :].unsqueeze(1).to_broadcast([P, NT, E]), ALU.mult))
            L(dve.tensor_reduce(g16[:, 0, :], te(gt[TMP]), AX, ALU.max))
            L(dve.tensor_tensor(te(dst), te(gt[TMP]), bc(g16[:, 0, :]), ALU.is_equal))

        def g_dve_top2(dve, k):
            L = lambda ins: link(dve, "dve", ins)
            dve.wait_ge(s["g_logit"], k + 1)
            L(dve.tensor_reduce(g16[:, 0, :], te(bank[6][:, 0:P]), AX, ALU.max))
            dve.tensor_tensor(te(gt[LOGIT]), te(bank[6][:, 0:P]), bc(g16[:, 0, :]), ALU.subtract)\
                .then_inc(s["g_in"], 1)
            dve.wait_ge(s["g_exp"], k + 1)
            L(dve.tensor_reduce(g16[:, 1, :], te(gt[PROB]), AX, ALU.add))
            L(dve.reciprocal(g16[:, 1, :], g16[:, 1, :]))
            L(dve.tensor_tensor(te(gt[PROB]), te(gt[PROB]), bc(g16[:, 1, :]), ALU.mult))
            first_largest(dve, gt[PROB], gt[MASK1])
            L(dve.tensor_tensor(gt[TMP], gt[PROB], gt[MASK1], ALU.mult))
            L(dve.tensor_tensor(gt[PROB2], gt[PROB], gt[TMP], ALU.subtract))
            first_largest(dve, gt[PROB2], gt[MASK2])

        def g_dve_weights(dve, second, floor):
            L = lambda ins: link(dve, "dve", ins)
            L(dve.tensor_tensor(gt[TMP], gt[PROB], gt[MASK1], ALU.mult))
            L(dve.tensor_tensor(gt[SUM_A], second, gt[MASK2], ALU.mult))
            L(dve.tensor_tensor(gt[TMP], gt[TMP], gt[SUM_A], ALU.add))
            L(dve.tensor_reduce(g16[:, 2, :], te(gt[TMP]), AX, ALU.add))
            if floor:
                L(dve.tensor_scalar(g16[:, 2, :], g16[:, 2, :], FLT_EPS, None, ALU.max))
            L(dve.reciprocal(g16[:, 2, :], g16[:, 2, :]))
            dve.tensor_tensor(gt[WT].rearrange("p (e t) -> p t e", e=E), te(gt[TMP]), bc(g16[:, 2, :]), ALU.mult)\
                .then_inc(s["g_row"], 1)

        def g_rows_pe(pe, k):
            pe.wait_ge(s["g_row"], k + 1)
            pe.transpose(bank[7][:, 0:P], gt[WT], ident[:, :]).then_inc(s["g_rowt"], 1)

        def g_rows_dve(dve, k):
            dve.wait_ge(s["g_rowt"], k + 1)
            dve.tensor_copy(gt[WROW], bank[7][:, 0:P]).then_inc(s["g_pre"], 1)

        def g_rows_sp(sp, k):
            sp.wait_ge(s["g_pre"], k + 1)
            sp.dma_start(d[f"wrow{k}"].rearrange("e (t p) -> (e t) p", p=P), gt[WROW]).then_inc(s["g_stored"], 16)
            sp.wait_ge(s["g_stored"], 16 * (k + 1))

        def cap_pe(pe):
            for r, mask in enumerate((MASK1, MASK2)):
                pe.wait_ge(s["g_cum"], 2 * r + 1)
                pe.matmul(bank[6][:, 0:P], before[:, :], gt[mask], start=True, stop=True)
                pe.matmul(bank[6][:, P:2 * P], ones_mat[:, :], gt[mask], start=True, stop=True)\
                    .then_inc(s["g_capmm"], 1)
            pe.wait_ge(s["g_cum"], 4)
            pe.matmul(bank[6][:, 0:P], ones_mat[:, :], gt[MASK1], start=True, stop=True).then_inc(s["g_capmm"], 1)

        def cap_dve(dve):
            L = lambda ins: link(dve, "dve", ins)

            def positions(r, pos):
                dve.wait_ge(s["g_capmm"], r + 1)
                L(dve.tensor_copy(gt[TOT], bank[6][:, P:2 * P]))
                L(dve.tensor_copy(gt[SUM_A], gt[TOT]))
                a, b = SUM_A, SUM_B
                k = 1
                while k < NT:
                    L(dve.tensor_copy(gt[b][:, 0:k * E], gt[a][:, 0:k * E]))
                    L(dve.tensor_tensor(gt[b][:, k * E:P], gt[a][:, k * E:P], gt[a][:, 0:P - k * E], ALU.add))
                    a, b = b, a
                    k *= 2
                L(dve.tensor_tensor(gt[a], gt[a], gt[TOT], ALU.subtract))
                dve.tensor_tensor(gt[pos], gt[a], bank[6][:, 0:P], ALU.add).then_inc(s["g_cum"], 1)
            L(dve.tensor_copy(gt[TMP], gt[MASK1]))
            dve.tensor_copy(gt[TOT], gt[TMP]).then_inc(s["g_cum"], 1)
            positions(0, POS1)
            dve.wait_ge(s["g_cum"], 2)
            L(dve.tensor_scalar(gt[POS1], gt[POS1], float(CAP), None, ALU.is_lt))
            dve.tensor_tensor(gt[MASK1], gt[MASK1], gt[POS1], ALU.mult).then_inc(s["g_cum"], 1)
            positions(1, POS2)
            dve.wait_ge(s["g_capmm"], 3)
            L(dve.tensor_reduce(g16[:, 3, 0:E], bank[6][:, 0:P].rearrange("p (t e) -> p e t", e=E), AX, ALU.add))
            L(dve.tensor_tensor(te(gt[POS2]), te(gt[POS2]), g16[:, 3, 0:E].unsqueeze(1).to_broadcast([P, NT, E]),
                                ALU.add))
            L(dve.tensor_scalar(gt[POS2], gt[POS2], float(CAP), None, ALU.is_lt))
            L(dve.tensor_tensor(gt[MASK2], gt[MASK2], gt[POS2], ALU.mult))

        MCR = 32
        PASSES = ((0, 0), (0, 1), (1, 0))
        UPS = {"m1": 3, "m3": 6}
        AHEAD = {"m1": 3, "m3": 3}
        HPS = {"m1": 3, "m3": 4}

        def up_bank(k, t, m=0):
            return bank[2 * (t % 3) + m] if k == "m1" else bank[t % 6]

        def moe_w_sp(sp, k, j, a):
            rows = slice(a * P, a * P + P) if type(j) is int else bass.ds(j * (2 * P) + a * P, P)
            sp.dma_start(ew[:, a, 0:EXP_COLS["moe" + k[1]]], d["moe" + k[1]][rows, :]).then_inc(s[f"{k}_w{a}"], 16)

        def moe_b_sp(sp, k, j, a):
            row = slice(a, a + 1) if type(j) is int else bass.ds(j * 2 + a, 1)
            sp.dma_start(wb[:, a, :], d["wrow0" if k == "m1" else "wrow1"][row, :].to_broadcast([P, N]))\
                .then_inc(s[f"{k}_b{a}"], 16)

        def moe_sp(sp, k, u0):
            with sp.Fori(1, E // 2) as j:
                for a in range(2):
                    sp.wait_ge(s[k + "_t"], j * 8 + (u0 + 16 * (a - 1)) // 4 + CR)
                    moe_w_sp(sp, k, j, a)
                    moe_b_sp(sp, k, j, a)

        def moe_pe(pe, k, base, tbase, units, first, weights):
            def parts3(out, w, cols_, rhs, start, stop):
                for n, (wp, xp_) in enumerate(PASSES):
                    ins = pe.matmul(out, w[:, wp, cols_:cols_ + P], rhs(xp_),
                                    start=(start and n == 0), stop=(stop and n == 2))
                return ins

            def up(t):
                a, u = first + t // 16, t % 16
                c, f = u // NF, u % NF
                if u == 0:
                    pe.wait_ge(s[k + "_ws"], weights(a))
                pe.wait_ge(s[k + "_h"], base + (t - UPS[k] + 1 if t >= UPS[k] else 0) + MCR)
                for m in range(2 if k == "m1" else 1):
                    ins = parts3(up_bank(k, t, m)[:, :], ewr[k][:, a], (4 * m + f) * P,
                                 lambda p_: xp[:, p_, c * C:(c + 1) * C], True, True)
                ins.then_inc(s[k + "_up"], 1)

            def down(t):
                a, u = first + t // 16, t % 16
                c, f = t // NF, u % NF
                pe.wait_ge(s[k + "_hl"], base + t + 1)
                if f == 0:
                    pe.wait_ge(s[k + "_t"], tbase + c - 1 + CR)
                w2 = 8 * P if k == "m1" else 4 * P
                parts3(bank[6 + c % 2][:, :], ewr[k][:, a], w2 + f * P, lambda p_: hp[t % HPS[k]][:, p_, :],
                       f == 0, f == NF - 1).then_inc(s[k + "_down"], 1)
            for t in range(AHEAD[k]):
                up(t)
            for t in range(units):
                if t + AHEAD[k] < units:
                    up(t + AHEAD[k])
                down(t)

        def moe_act(act, k, base, units, first):
            def high(t):
                act.wait_ge(s[k + "_h"], base + t + 1 + MCR)
                if t >= HPS[k]:
                    act.wait_ge(s[k + "_down"], base + t - HPS[k] + 1)
                act.activation(hp[t % HPS[k]][:, 0, :], hring[:, t % 4, :], ACT.Copy).then_inc(s[k + "_hh"], 1)
            for t in range(units):
                act.wait_ge(s[k + "_up"], base + t + 1)
                b_ = up_bank(k, t)[:, :]
                if k == "m1":
                    act.activation(esil[:, t % 2, :], b_, ACT.Silu).then_inc(s["m1_sil"], 1)
                else:
                    a = first + t // 16
                    act.activation(hring[:, t % 4, :], b_, ACT.Silu, bias=ew[:, a, 8 * P + t % 4:8 * P + t % 4 + 1])\
                        .then_inc(s["m3_h"], 1)
                if k == "m3":
                    high(t)
                elif t:
                    high(t - 1)
            if k == "m1":
                high(units - 1)

        def moe_dve(dve, k, base, tbase, units, first, rows):
            def low(t):
                dve.wait_ge(s[k + "_hh"], base + t + 1)
                dve.tensor_tensor(hp[t % HPS[k]][:, 1, :], hring[:, t % 4, :], hp[t % HPS[k]][:, 0, :].bitcast(F32),
                                  ALU.subtract).then_inc(s[k + "_hl"], 1)

            def scaled(c):
                a = first + c // NC_
                if c % NC_ == 0 and rows(a) is not None:
                    dve.wait_ge(s[f"{k}_b{a}"], rows(a))
                dve.wait_ge(s[k + "_down"], base + 4 * c + 4)
                dve.wait_ge(s[k + "_acc"], tbase + c - 1 + CR)
                w = wb[:, a, c % NC_ * C:(c % NC_ + 1) * C]
                if k == "m1":
                    ins = dve.tensor_tensor(yt[:, c % 2, :], bank[6 + c % 2][:, :], w, ALU.mult)
                else:
                    ins = dve.scalar_tensor_tensor(yt[:, c % 2, :], bank[6 + c % 2][:, :],
                                                   ew[:, a, 8 * P + 4:8 * P + 5], w, ALU.add, ALU.mult)
                ins.then_inc(s[k + "_t"], 1)
            for t in range(units):
                if k == "m1":
                    dve.wait_ge(s["m1_sil"], base + t + 1)
                    dve.tensor_tensor(hring[:, t % 4, :], esil[:, t % 2, :], up_bank(k, t, 1)[:, :], ALU.mult)\
                        .then_inc(s["m1_h"], 1)
                if k == "m3":
                    low(t)
                elif t:
                    low(t - 1)
                if t % 4 == 2 and t > 4:
                    scaled(t // 4 - 1)
            if k == "m1":
                low(units - 1)
            scaled(units // 4 - 1)

        def moe_add_pool(pool, k, tbase):
            for c in range(NC_):
                pool.wait_ge(s[k + "_t"], tbase + c + 1 + CR)
                pool.wait_ge(s[k + "_acc"], tbase + c - 3 + CR)
                pool.tensor_tensor(ch(a4, c), ch(a4, c), yt[:, c % 2, :], ALU.add).then_inc(s[k + "_acc"], 1)

        def split_pool(pool, high, low, src, cols_, sm, before_):
            pool.tensor_tensor(high, src, ones_mat[:, 0:1].to_broadcast([P, cols_]), ALU.mult).then_inc(s[sm], 1)
            pool.wait_ge(s[sm], before_ + 1)
            pool.tensor_tensor(low, src, high.bitcast(F32), ALU.subtract).then_inc(s[sm], 1)

        def moe_split_pool(pool, k, a, raw, before_):
            pool.wait_ge(s[raw[0]], raw[1])
            n = (12 if k == "m1" else 8) * P
            split_pool(pool, ewr[k][:, a, 0, 0:n], ewr[k][:, a, 1, 0:n], ew[:, a, 0:n], n, k + "_ws", before_)

        def moe_pool(pool, k, u0):
            w0, t0 = u0 // 8, u0 // 4

            def pair(j, last):
                moe_split_pool(pool, k, 1, (f"{k}_w1", j * 16 + 16), j * 4 + w0 + 2)
                moe_add_pool(pool, k, j * 8 + t0)
                if not last:
                    moe_split_pool(pool, k, 0, (f"{k}_w0", j * 16 + 32), j * 4 + w0 + 4)
                moe_add_pool(pool, k, j * 8 + t0 + 4)
            with pool.Fori(0, E // 2 - 1) as j:
                pair(j, False)
            pair(E // 2 - 1, True)

        def tokens_split_pool(pool, n, k):
            for c in range(NC_):
                pool.wait_ge(s["ln_norm"], 4 * n + c + 1)
                sl = slice(c * C, (c + 1) * C)
                split_pool(pool, xp[:, 0, sl], xp[:, 1, sl], a1[:, sl], C, "xp_split", 8 * k + 2 * c)

        def clear_acc(pool):
            for c in range(NC_):
                ins = pool.memset(ch(a4, c), 0.0)
            link(pool, "pool", ins)

        def moe_res_dve(dve, k, gate, chunks, out):
            for c in range(NC_):
                dve.wait_ge(s[k + "_acc"], chunks - 3 + c + CR)
                dve.scalar_tensor_tensor(ch(x, c), ch(a4, c), tg[:, gate:gate + 1], ch(x, c), ALU.mult, ALU.add)\
                    .then_inc(s[out], 1)

        CREDIT += [("m1_t", CR), ("m3_t", CR), ("m1_h", MCR), ("m3_h", MCR), ("m1_acc", CR), ("m3_acc", CR)]

        ld_x = lambda c: [(s[f"ld_x{c}"], 16)]
        norm_of = lambda n: (lambda c: [(s["ln_norm"], 4 * n + c + 1)])
        aff_of = lambda n, j: (lambda c: [(s["ln_aff"], aff_at(n, c, j))])
        r1_of = lambda c: [(s["prep_dve"], PREP + JOBS * (B // SB))]
        res_of = lambda l: (lambda c: [(s["ca_res"], 4 * l + c + 1)])
        out1_of = lambda c: [(s["mlp_out"], c + 1)]
        out2_of = lambda c: [(s["mlp_out"], 4 + 2 * c + 2)]
        f2_of = lambda c: [(s["f2_res"], c + 1)]
        m1_of = lambda c: [(s["m1_out"], c + 1)]
        r_of = lambda c: [(s["r_out"], c + 1)]
        AFF = {1: [(a1, "ln1_g", "ln1_b")],
               2: [(a3, "a1_lny_g", "a1_lny_b"), (a2, "a1_lnx_g", "a1_lnx_b")],
               3: [(a2, "a1_ln3_g", "a1_ln3_b")],
               4: [(a1, "ln2_g", "ln2_b")],
               5: [(a2, "a2_lnx_g", "a2_lnx_b")],
               6: [(a2, "a2_ln3_g", "a2_ln3_b")]}

        block = ctx.enter_context(nc.Block())

        @block.sync
        def _(sp):
            setup_sp(sp)
            sa_sp(sp)
            mlp_sp(sp, 0)
            cx_sp(sp, 0)
            mlp_sp(sp, 1)
            f0w_sp(sp)
            cx_sp(sp, 1)
            cx_sp(sp, 2)
            sp.wait_ge(s["ca_res"], 2 * B)
            for a in range(2):
                moe_w_sp(sp, "m1", 0, a)
            g_rows_sp(sp, 0)
            for a in range(2):
                moe_b_sp(sp, "m1", 0, a)
            moe_sp(sp, "m1", 0)
            cx_sp(sp, 3)
            sp.wait_ge(s["ca_res"], 4 * B)
            sp.dma_start(ew[:, 1, 0:EXP_COLS["moe3"]], d["shared"]).then_inc(s["m3_wsh"], 16)
            moe_w_sp(sp, "m3", 0, 0)
            g_rows_sp(sp, 1)
            moe_b_sp(sp, "m3", 0, 0)
            sp.wait_ge(s["m3_t"], 4 + CR)
            moe_w_sp(sp, "m3", 0, 1)
            moe_b_sp(sp, "m3", 0, 1)
            moe_sp(sp, "m3", 16)
            for c in range(NC_):
                sp.wait_ge(s["x_out"], c + 1)
                sp.dma_start(d["out"][:, c * C:(c + 1) * C], ch(x, c)).then_inc(s["stored"], 16)
            sp.wait_ge(s["stored"], 16 * NC_)

        @block.gpsimd
        def _(pool):
            setup_pool(pool)
            pool.wait_ge(s["ld_cols"], 16)
            r1_init_pool(pool)
            sa_pool(pool)
            ca_pool(pool, 0)
            f1_pool(pool)
            f2_pool(pool)
            ca_pool(pool, 1)
            tokens_split_pool(pool, 9, 0)
            moe_split_pool(pool, "m1", 0, ("m1_w0", 16), 0)
            clear_acc(pool)
            moe_pool(pool, "m1", 0)
            ca_pool(pool, 2)
            r_pool(pool)
            ca_pool(pool, 3)
            pool.wait_ge(s["ca_res"], 4 * B)
            pool.memset(wb[:, 1, :], 0.1).then_inc(s["sh_weight"], 1)
            tokens_split_pool(pool, 13, 1)
            moe_split_pool(pool, "m3", 1, ("m3_wsh", 16), 0)
            clear_acc(pool)
            moe_split_pool(pool, "m3", 0, ("m3_w0", 16), 2)
            moe_add_pool(pool, "m3", 0)
            moe_pool(pool, "m3", 16)

        @block.scalar
        def _(act):
            setup_act(act)
            act.wait_ge(s["const_ready"], 1)
            ln_act(act, 0, a1)
            ln_act(act, 1, a2, AFF[1])
            ln_act(act, 2, a2, AFF[2])
            sa_act(act)
            ln_act(act, 3, a2, AFF[3])
            mlp_act(act, 0)
            cln_act(act)
            cx_act(act, 0)
            ln_act(act, 4, a2, AFF[4])
            ln_act(act, 5, a2, AFF[5])
            ca_act(act, 0)
            ln_act(act, 6, a2, AFF[6])
            mlp_act(act, 1)
            ln_act(act, 7, a1)
            f1_act(act)
            f2_act(act)
            cx_act(act, 1)
            ln_act(act, 8, a1)
            ca_act(act, 1)
            ln_act(act, 9, a1)
            g_act_exp(act, 0)
            with act.Fori(0, E * 16, 32) as u:
                moe_act(act, "m1", u, 32, 0)
            cx_act(act, 2)
            ln_act(act, 10, a1)
            ca_act(act, 2)
            ln_act(act, 11, a1)
            r_act(act)
            cx_act(act, 3)
            ln_act(act, 12, a1)
            ca_act(act, 3)
            ln_act(act, 13, a1)
            g_act_exp(act, 1)
            moe_act(act, "m3", 0, 16, 1)
            with act.Fori(16, 16 + E * 16, 32) as u:
                moe_act(act, "m3", u, 32, 0)

        @block.vector
        def _(dve):
            ln_dve(dve, 0, x, a1)
            setup_dve(dve)
            ln_dve(dve, 1, a1, a2)
            sa_sel_dve(dve)
            ln_dve(dve, 2, a1, a2)
            sa_dve(dve)
            ln_dve(dve, 3, a4, a2)
            mlp_dve(dve, 0)
            cln_dve(dve)
            cx_dve(dve, 0)
            ln_dve(dve, 4, a1, a2)
            ln_dve(dve, 5, a1, a2)
            ca_dve(dve, 0, a1, a4)
            ln_dve(dve, 6, a4, a2)
            mlp_dve(dve, 1)
            f0w_dve(dve)
            ln_dve(dve, 7, x, a1)
            f1_dve(dve)
            f2_dve(dve)
            cx_dve(dve, 1)
            ln_dve(dve, 8, x, a1)
            ca_dve(dve, 1, x, x)
            ln_dve(dve, 9, x, a1)
            g_dve_top2(dve, 0)
            g_dve_weights(dve, gt[PROB2], False)
            g_rows_dve(dve, 0)
            with dve.Fori(0, E // 2) as j:
                moe_dve(dve, "m1", j * 32, j * 8, 32, 0, lambda a: j * 16 + 16)
            moe_res_dve(dve, "m1", 5, 4 * E, "m1_out")
            cx_dve(dve, 2)
            ln_dve(dve, 10, x, a1)
            ca_dve(dve, 2, x, x)
            ln_dve(dve, 11, x, a1)
            r_dve(dve)
            cx_dve(dve, 3)
            ln_dve(dve, 12, x, a1)
            ca_dve(dve, 3, x, x)
            ln_dve(dve, 13, x, a1)
            g_dve_top2(dve, 1)
            cap_dve(dve)
            g_dve_weights(dve, gt[PROB], True)
            g_rows_dve(dve, 1)
            dve.wait_ge(s["sh_weight"], 1)
            moe_dve(dve, "m3", 0, 0, 16, 1, lambda a: None)
            with dve.Fori(0, E // 2) as j:
                moe_dve(dve, "m3", j * 32 + 16, j * 8 + 4, 32, 0, lambda a: j * 16 + 16)
            moe_res_dve(dve, "m3", 7, 4 * E + 4, "x_out")

        @block.tensor
        def _(pe):
            pe.wait_ge(s["const_ready"], 2)
            ln_pe(pe, 0, x, ld_x)
            ln_pe(pe, 1, a1, norm_of(0))
            ln_pe(pe, 2, a1, aff_of(1, 0))
            pe.wait_ge(s["ln_aff"], aff_at(2, 3, 1))
            sa_pe(pe)
            ln_pe(pe, 3, a4, r1_of)
            mlp_pe(pe, 0, 3)
            cln_pe(pe)
            pe.wait_ge(s["cx_ln_act"], 3)
            cx_pe(pe, 0)
            ln_pe(pe, 4, a1, out1_of)
            ln_pe(pe, 5, a1, aff_of(4, 0))
            ca_pe(pe, 0, a2, aff_of(5, 0))
            ln_pe(pe, 6, a4, res_of(0))
            mlp_pe(pe, 1, 6)
            f0w_pe(pe)
            ln_pe(pe, 7, x, out2_of)
            f1_pe(pe)
            f2_pe(pe)
            cx_pe(pe, 1, [(s["f2_scaled"], NT)])
            ln_pe(pe, 8, x, f2_of)
            ca_pe(pe, 1, a1, norm_of(8))
            ln_pe(pe, 9, x, res_of(1))
            g_pe_logits(pe, 0, 9)
            g_rows_pe(pe, 0)
            pe.wait_ge(s["xp_split"], 8)
            with pe.Fori(0, E // 2) as j:
                moe_pe(pe, "m1", j * 32, j * 8, 32, 0, lambda a: j * 4 + 2 * a + 2)
            cx_pe(pe, 2, [(s["m1_t"], 4 * E + CR)])
            ln_pe(pe, 10, x, m1_of)
            ca_pe(pe, 2, a1, norm_of(10))
            ln_pe(pe, 11, x, res_of(2))
            r_pe(pe)
            cx_pe(pe, 3, [(s["r_out"], NC_)])
            ln_pe(pe, 12, x, r_of)
            ca_pe(pe, 3, a1, norm_of(12))
            ln_pe(pe, 13, x, res_of(3))
            g_pe_logits(pe, 1, 13)
            cap_pe(pe)
            g_rows_pe(pe, 1)
            pe.wait_ge(s["xp_split"], 16)
            moe_pe(pe, "m3", 0, 0, 16, 1, lambda a: 2)
            with pe.Fori(0, E // 2) as j:
                moe_pe(pe, "m3", j * 32 + 16, j * 8 + 4, 32, 0, lambda a: j * 4 + 2 * a + 4)


def kernel(**inputs):
    import numpy as np
    import concourse.bacc as bacc
    from concourse.bass_utils import run_bass_kernel_spmd as run

    i = {k: np.asarray(v) for k, v in inputs.items()}

    def blocks(w):
        n = w.shape[0] // P
        return w.reshape(n, P, w.shape[1]).transpose(1, 0, 2).reshape(P, n * w.shape[1])

    def heads(w):
        return w.transpose(1, 0, 2).reshape(w.shape[1], -1)

    packed = np.zeros((P, NCOLS), np.float32)

    def put(name, v):
        at, n = COLS[name]
        v = v.reshape(n, -1).T
        packed[0:v.shape[0], at:at + n] = v
    packed[:, 0:4] = i["g_xattn"][None, :]
    packed[:, 4:8] = i["g_ffn"][None, :]
    for name in COLS:
        if name[:3] in ("ln1", "ln2", "a1_", "a2_"):
            put(name, i["L0_xattn_" + name])
    at = COLS["conv_w"][0]
    packed[:, at:at + 12] = i["L0_ffn_conv_w"].reshape(NF, P, 3).transpose(1, 0, 2).reshape(P, 12)
    put("conv_b", i["L0_ffn_conv_b"])
    put("bo2", i["L2_xattn_bo"])
    put("mu_r", i["L2_ffn_mu_r"])
    put("mu_k", i["L2_ffn_mu_k"])
    for name in ("bq", "bk", "bv", "bo"):
        put(name + "3", i["L3_xattn_" + name])
    put("sb1", i["L3_ffn_sb1"])
    put("sb2", i["L3_ffn_sb2"])

    arrays = {
        "x": i["x"].reshape(N, P).T,
        "cols": packed,
        "ctx": i["ctx_512"].reshape(B * M, CD).T,
    }
    hq, hk, hv = (heads(i["L0_xattn_a1_" + n]) for n in ("wq", "wk", "wv"))
    arrays["w_qkv"] = np.concatenate([w[:, g * P:(g + 1) * P] for g in range(4) for w in (hq, hk, hv)], 1)
    arrays["w_li1"] = blocks(i["L0_xattn_a1_li1_w"])
    for a in ("a1", "a2"):
        arrays[a + "_li2"] = i[f"L0_xattn_{a}_li2_w"]
        arrays[a + "_li3"] = blocks(i[f"L0_xattn_{a}_li3_w"])
    q = [heads(i["L0_xattn_a2_wq"]), i["L1_xattn_Wq"].T, i["L2_xattn_Wq"], i["L3_xattn_Wq"]]
    k = [heads(i["L0_xattn_a2_wk"]), i["L1_xattn_Wkv"][0:P].T, i["L2_xattn_Wk"], i["L3_xattn_Wk"]]
    v = [heads(i["L0_xattn_a2_wv"]), i["L1_xattn_Wkv"][P:2 * P].T, i["L2_xattn_Wv"], i["L3_xattn_Wv"]]
    o = [i["L0_xattn_a2_li1_w"], i["L1_xattn_Wo"].T, i["L2_xattn_Wo"], i["L3_xattn_Wo"]]
    for l in range(4):
        arrays[f"c{l}_q"] = blocks(q[l].T)
        arrays[f"c{l}_k"] = k[l]
        arrays[f"c{l}_v"] = v[l]
        arrays[f"c{l}_o"] = blocks(o[l])
    arrays["f0_w1"] = i["L0_ffn_w1"].T
    arrays["f0_w2"] = blocks(i["L0_ffn_w2"].T)
    arrays["f2_w"] = np.concatenate([i["L2_ffn_" + n].T for n in ("W_r", "W_k", "W_v")], 1)
    arrays["gates"] = np.concatenate([i["L1_ffn_gate_w"], i["L3_ffn_router_w"]], 1)
    arrays["moe1"] = np.concatenate([
        np.concatenate([i["L1_ffn_w1"][e], i["L1_ffn_w3"][e], blocks(i["L1_ffn_w2"][e])], 1) for e in range(E)], 0)
    arrays["moe3"] = np.concatenate([
        np.concatenate([i["L3_ffn_w1"][e], blocks(i["L3_ffn_w2"][e]), i["L3_ffn_b1"][e].reshape(NF, P).T,
                        i["L3_ffn_b2"][e][:, None]], 1) for e in range(E)], 0)
    arrays["shared"] = np.concatenate([i["L3_ffn_sw1"], blocks(i["L3_ffn_sw2"]), i["L3_ffn_sb1"].reshape(NF, P).T,
                                       i["L3_ffn_sb2"][:, None]], 1)
    arrays = {n: np.ascontiguousarray(a) for n, a in arrays.items()}

    nc = bacc.Bacc("TRN2", target_bir_lowering=False, num_devices=1)
    d = {n: nc.dram_tensor("in_" + n, a.shape, F32, kind="ExternalInput").ap() for n, a in arrays.items()}
    for n in ("wrow0", "wrow1"):
        d[n] = nc.dram_tensor(n, (E, N), F32, kind="Internal").ap()
    d["out"] = nc.dram_tensor("out_x", (P, N), F32, kind="ExternalOutput").ap()
    build(nc, d)
    r = run(nc, [{"in_" + n: a for n, a in arrays.items()}], core_ids=[0])
    return np.ascontiguousarray(r.results[0]["out_x"].T.reshape(B, S, P))
```
